# Optimizing a Trainium2 kernel written in Bass

```python
import numpy as np
import jax
import jax.numpy as jnp

def _softmax(x, axis=-1):
    return jax.nn.softmax(x, axis=axis)

def _gelu(x):
    return jax.nn.gelu(x, approximate=True)

def _silu(x):
    return jax.nn.silu(x)

def _sigmoid(x):
    return jax.nn.sigmoid(x)

def _layernorm(x, axis=-1, eps=1e-05):
    m = jnp.mean(x, axis=axis, keepdims=True)
    v = jnp.var(x, axis=axis, keepdims=True)
    return (x - m) / jnp.sqrt(v + eps)

def _scatter_add(tgt, idx, src, axis=0):
    return tgt.at[idx].add(src)

def _segment_sum(src, seg, n):
    return jax.ops.segment_sum(src, seg, n)
kernel_name = 'mk_prb_d1_jaxref_r8_c86ae5'

def setup_inputs(seed: int=0):
    np.random.seed(seed)
    _w = jnp.asarray

    def _L0_attn_setup():
        import jax, jax.numpy as jnp
        import numpy as np
        OFFSETS = tuple(sorted(set(range(0, 33)) | {48, 64, 96, 128, 192, 32, 48, 64, 96, 128, 192}))
        B, N, D, H, FF = (1, 256, 128, 16, 512)
        HD = D // H

        def _ln(x, g, b):
            mu = x.mean(-1, keepdims=True)
            var = ((x - mu) ** 2).mean(-1, keepdims=True)
            return (x - mu) * jax.lax.rsqrt(var + 1e-05) * g + b

        def _shift(a, delta, n):
            if delta == 0:
                return a
            if delta >= n:
                return jnp.zeros_like(a)
            pad = jnp.zeros(a.shape[:2] + (delta,) + a.shape[3:], a.dtype)
            return jnp.concatenate([pad, a[:, :, :n - delta]], axis=2)

        def _block(x, ln1_g, ln1_b, qkv_w, qkv_b, gate_w, gate_b, out_w, out_b, pos_bias, ln2_g, ln2_b, fc1_w, fc1_b, fc2_w, fc2_b):
            b, n, d = x.shape
            h = pos_bias.shape[1]
            hd = d // h
            xn = _ln(x, ln1_g, ln1_b)
            qkv = xn @ qkv_w + qkv_b
            q, k, v = jnp.split(qkv, 3, axis=-1)
            q = q.reshape(b, n, h, hd).transpose(0, 2, 1, 3)
            k = k.reshape(b, n, h, hd).transpose(0, 2, 1, 3)
            v = v.reshape(b, n, h, hd).transpose(0, 2, 1, 3)
            scale = hd ** (-0.5)
            scores = jnp.stack([jnp.einsum('bhnd,bhnd->bhn', q, _shift(k, delta, n)) for delta in OFFSETS], axis=-1) * scale
            scores = scores + pos_bias.T[None, :, None, :]
            offs = jnp.asarray(OFFSETS)
            mask = jnp.arange(n)[:, None] < offs[None, :]
            scores = jnp.where(mask[None, None], -jnp.inf, scores)
            alpha = jax.nn.softmax(scores, axis=-1)
            out = jnp.zeros_like(q)
            for i, delta in enumerate(OFFSETS):
                out = out + alpha[..., i, None] * _shift(v, delta, n)
            flat = out.transpose(0, 2, 1, 3).reshape(b, n, d)
            gate = jax.nn.sigmoid(xn @ gate_w + gate_b)
            attn_out = flat * gate @ out_w + out_b
            x = x + attn_out
            xn2 = _ln(x, ln2_g, ln2_b)
            ffn = jax.nn.gelu(xn2 @ fc1_w + fc1_b, approximate=False) @ fc2_w + fc2_b
            return x + ffn
        key = jax.random.key(seed)
        ks = jax.random.split(key, 6)
        w = lambda k, sh: jax.random.normal(k, sh, jnp.float32) * 0.02
        x = jax.random.normal(ks[0], (B, N, D), jnp.float32)
        deltas = jnp.log1p(jnp.asarray(OFFSETS, dtype=jnp.float32))
        alphas = jnp.linspace(0.2, 2.0, H).astype(jnp.float32)
        pos_bias = -deltas[:, None] * alphas[None, :]
        return {'x': x, 'ln1_g': jnp.ones((D,), jnp.float32), 'ln1_b': jnp.zeros((D,), jnp.float32), 'qkv_w': w(ks[1], (D, 3 * D)), 'qkv_b': jnp.zeros((3 * D,), jnp.float32), 'gate_w': w(ks[2], (D, D)), 'gate_b': jnp.full((D,), 2.0, jnp.float32), 'out_w': w(ks[3], (D, D)), 'out_b': jnp.zeros((D,), jnp.float32), 'pos_bias': pos_bias, 'ln2_g': jnp.ones((D,), jnp.float32), 'ln2_b': jnp.zeros((D,), jnp.float32), 'fc1_w': w(ks[4], (D, FF)), 'fc1_b': jnp.zeros((FF,), jnp.float32), 'fc2_w': w(ks[5], (FF, D)), 'fc2_b': jnp.zeros((D,), jnp.float32)}
    _L0_attn_in = _L0_attn_setup()

    def _L0_ffn_setup():
        import jax, jax.numpy as jnp
        import numpy as np
        ALPHA = 1.702
        LIMIT = 7.0
        K = 2
        key = jax.random.key(seed)
        ks = jax.random.split(key, 4)
        B, S, H, E, I = (1, 128, 128, 8, 128)
        return {'hidden_states': jax.random.normal(ks[0], (B, S, H), jnp.float32), 'router_weight': jax.random.normal(ks[1], (E, H), jnp.float32), 'router_bias': jnp.zeros((E,), jnp.float32), 'gate_up_proj': jax.random.normal(ks[2], (E, H, 2 * I), jnp.float32) * 0.02, 'gate_up_bias': jnp.zeros((E, 2 * I), jnp.float32), 'down_proj': jax.random.normal(ks[3], (E, I, H), jnp.float32) * 0.02, 'down_bias': jnp.zeros((E, H), jnp.float32)}
    _L0_ffn_in = _L0_ffn_setup()
    _d = {'L0_attn_x': _L0_attn_in['x'], 'L0_attn_ln1_g': _L0_attn_in['ln1_g'], 'L0_attn_ln1_b': _L0_attn_in['ln1_b'], 'L0_attn_qkv_w': _L0_attn_in['qkv_w'], 'L0_attn_qkv_b': _L0_attn_in['qkv_b'], 'L0_attn_gate_w': _L0_attn_in['gate_w'], 'L0_attn_gate_b': _L0_attn_in['gate_b'], 'L0_attn_out_w': _L0_attn_in['out_w'], 'L0_attn_out_b': _L0_attn_in['out_b'], 'L0_attn_pos_bias': _L0_attn_in['pos_bias'], 'L0_attn_ln2_g': _L0_attn_in['ln2_g'], 'L0_attn_ln2_b': _L0_attn_in['ln2_b'], 'L0_attn_fc1_w': _L0_attn_in['fc1_w'], 'L0_attn_fc1_b': _L0_attn_in['fc1_b'], 'L0_attn_fc2_w': _L0_attn_in['fc2_w'], 'L0_attn_fc2_b': _L0_attn_in['fc2_b'], 'L0_ffn_router_weight': _L0_ffn_in['router_weight'], 'L0_ffn_router_bias': _L0_ffn_in['router_bias'], 'L0_ffn_gate_up_proj': _L0_ffn_in['gate_up_proj'], 'L0_ffn_gate_up_bias': _L0_ffn_in['gate_up_bias'], 'L0_ffn_down_proj': _L0_ffn_in['down_proj'], 'L0_ffn_down_bias': _L0_ffn_in['down_bias']}
    _x0 = _d['L0_attn_x']
    _d['L0_attn_x'] = jax.random.normal(jax.random.fold_in(jax.random.key(seed), 1), (1, 2048, 128), dtype=_x0.dtype)
    del _x0
    return _d

def reference(L0_attn_x, L0_attn_ln1_g, L0_attn_ln1_b, L0_attn_qkv_w, L0_attn_qkv_b, L0_attn_gate_w, L0_attn_gate_b, L0_attn_out_w, L0_attn_out_b, L0_attn_pos_bias, L0_attn_ln2_g, L0_attn_ln2_b, L0_attn_fc1_w, L0_attn_fc1_b, L0_attn_fc2_w, L0_attn_fc2_b, L0_ffn_router_weight, L0_ffn_router_bias, L0_ffn_gate_up_proj, L0_ffn_gate_up_bias, L0_ffn_down_proj, L0_ffn_down_bias):

    def _L0_attn_ref(x, ln1_g, ln1_b, qkv_w, qkv_b, gate_w, gate_b, out_w, out_b, pos_bias, ln2_g, ln2_b, fc1_w, fc1_b, fc2_w, fc2_b):
        import jax, jax.numpy as jnp
        import numpy as np
        OFFSETS = tuple(sorted(set(range(0, 33)) | {48, 64, 96, 128, 192, 32, 48, 64, 96, 128, 192}))
        B, N, D, H, FF = (1, 256, 128, 16, 512)
        HD = D // H

        def _ln(x, g, b):
            mu = x.mean(-1, keepdims=True)
            var = ((x - mu) ** 2).mean(-1, keepdims=True)
            return (x - mu) * jax.lax.rsqrt(var + 1e-05) * g + b

        def _shift(a, delta, n):
            if delta == 0:
                return a
            if delta >= n:
                return jnp.zeros_like(a)
            pad = jnp.zeros(a.shape[:2] + (delta,) + a.shape[3:], a.dtype)
            return jnp.concatenate([pad, a[:, :, :n - delta]], axis=2)

        def _block(x, ln1_g, ln1_b, qkv_w, qkv_b, gate_w, gate_b, out_w, out_b, pos_bias, ln2_g, ln2_b, fc1_w, fc1_b, fc2_w, fc2_b):
            b, n, d = x.shape
            h = pos_bias.shape[1]
            hd = d // h
            xn = _ln(x, ln1_g, ln1_b)
            qkv = xn @ qkv_w + qkv_b
            q, k, v = jnp.split(qkv, 3, axis=-1)
            q = q.reshape(b, n, h, hd).transpose(0, 2, 1, 3)
            k = k.reshape(b, n, h, hd).transpose(0, 2, 1, 3)
            v = v.reshape(b, n, h, hd).transpose(0, 2, 1, 3)
            scale = hd ** (-0.5)
            scores = jnp.stack([jnp.einsum('bhnd,bhnd->bhn', q, _shift(k, delta, n)) for delta in OFFSETS], axis=-1) * scale
            scores = scores + pos_bias.T[None, :, None, :]
            offs = jnp.asarray(OFFSETS)
            mask = jnp.arange(n)[:, None] < offs[None, :]
            scores = jnp.where(mask[None, None], -jnp.inf, scores)
            alpha = jax.nn.softmax(scores, axis=-1)
            out = jnp.zeros_like(q)
            for i, delta in enumerate(OFFSETS):
                out = out + alpha[..., i, None] * _shift(v, delta, n)
            flat = out.transpose(0, 2, 1, 3).reshape(b, n, d)
            gate = jax.nn.sigmoid(xn @ gate_w + gate_b)
            attn_out = flat * gate @ out_w + out_b
            x = x + attn_out
            xn2 = _ln(x, ln2_g, ln2_b)
            ffn = jax.nn.gelu(xn2 @ fc1_w + fc1_b, approximate=False) @ fc2_w + fc2_b
            return x + ffn
        return _block(x, ln1_g, ln1_b, qkv_w, qkv_b, gate_w, gate_b, out_w, out_b, pos_bias, ln2_g, ln2_b, fc1_w, fc1_b, fc2_w, fc2_b)

    def _L0_ffn_ref(hidden_states, router_weight, router_bias, gate_up_proj, gate_up_bias, down_proj, down_bias):
        import jax, jax.numpy as jnp
        import numpy as np
        ALPHA = 1.702
        LIMIT = 7.0
        K = 2
        B, S, H = hidden_states.shape
        E = router_weight.shape[0]
        I = down_proj.shape[1]
        T = B * S
        flat = hidden_states.reshape(T, H)
        logits = flat @ router_weight.T + router_bias
        scores = jax.nn.softmax(logits, axis=-1)
        topk_vals, topk_idx = jax.lax.top_k(scores, K)
        w = jnp.zeros((T, E), scores.dtype).at[jnp.arange(T)[:, None], topk_idx].set(topk_vals)
        gu = jnp.einsum('th,ehf->tef', flat, gate_up_proj) + gate_up_bias
        gate = jnp.minimum(gu[..., :I], LIMIT)
        up = jnp.clip(gu[..., I:], -LIMIT, LIMIT)
        glu = gate * jax.nn.sigmoid(gate * ALPHA)
        act = (up + 1.0) * glu
        down = jnp.einsum('tei,eih->teh', act, down_proj) + down_bias
        out = jnp.einsum('teh,te->th', down, w)
        return out.reshape(B, S, H)
    x = L0_attn_x
    xn = _layernorm(x, axis=-1)
    x = x + _L0_attn_ref(xn, L0_attn_ln1_g, L0_attn_ln1_b, L0_attn_qkv_w, L0_attn_qkv_b, L0_attn_gate_w, L0_attn_gate_b, L0_attn_out_w, L0_attn_out_b, L0_attn_pos_bias, L0_attn_ln2_g, L0_attn_ln2_b, L0_attn_fc1_w, L0_attn_fc1_b, L0_attn_fc2_w, L0_attn_fc2_b) + _L0_ffn_ref(xn, L0_ffn_router_weight, L0_ffn_router_bias, L0_ffn_gate_up_proj, L0_ffn_gate_up_bias, L0_ffn_down_proj, L0_ffn_down_bias)
    return x

_drawn_inputs = setup_inputs


def setup_inputs(seed=0):
    import zlib

    import numpy as np

    out = dict(_drawn_inputs(seed))
    spreads = {'L0_attn_ln1_g': (1.0, 0.6),
     'L0_attn_ln1_b': (0.0, 0.8),
     'L0_attn_qkv_b': (0.0, 0.716),
     'L0_attn_gate_b': (2.0, 0.6),
     'L0_attn_out_b': (0.0, 0.1),
     'L0_attn_ln2_g': (1.0, 0.6),
     'L0_attn_ln2_b': (0.0, 2.0),
     'L0_attn_fc1_b': (0.0, 0.763),
     'L0_attn_fc2_b': (0.0, 0.1),
     'L0_ffn_router_bias': (0.0, 0.8),
     'L0_ffn_gate_up_bias': (0.0, 0.8),
     'L0_ffn_down_bias': (0.0, 0.1)}
    factors = {'L0_attn_qkv_w': 5.936,
     'L0_attn_gate_w': 8.0,
     'L0_attn_out_w': 3.919,
     'L0_attn_pos_bias': 6.54,
     'L0_ffn_gate_up_proj': 4.364,
     'L0_ffn_down_proj': 4.036}
    for name, (base, spread) in spreads.items():
        noise = np.random.default_rng([zlib.crc32(name.encode()), seed]).standard_normal(out[name].shape)
        drawn = base * np.exp(spread * noise) if base else spread * noise
        out[name] = jnp.asarray(drawn.astype(out[name].dtype))
    for name, factor in factors.items():
        out[name] = (out[name] * factor).astype(out[name].dtype)
    return out
```

```python
import concourse.bass as bass
from concourse import mybir
from contextlib import ExitStack

TOKENS, D = 2048, 128
TILES = TOKENS // 128
QUARTERS, QT = 4, 4
HEADS, HD = 16, 8
HG = HEADS // 4
WINDOW = 64
FF, EXPERTS, INNER = 512, 8, 128
FC = FF // 128
EPS = 1e-5
CLOSED = -1e30
FAR = (48, 64, 96, 128, 192)
NFAR = len(FAR)
LIMIT, ALPHA = 7.0, 1.702
STEPS = 32
C_G1, C_B1, C_G2, C_B2, C_BQ, C_BK, C_GU, C_F1 = 0, 1, 2, 3, 4, 5, 6, 22
N_COLS = C_F1 + FC
R_QKV, R_GATE, R_ROUTER, R_OUT, R_FC2 = 0, 384, 512, 520, 648
N_ROW = 776


def shifted_pieces(n, first_tile):
    a, back = n % 4, n // 4
    out = []
    if a < 4:
        out.append((a, 4, 0, back))
    if a:
        out.append((0, a, 4 - a, back + 1))
    return [(g0, g1, s0, b, max(0, b - first_tile)) for g0, g1, s0, b in out]


def build(nc, x, ident, anti, headmask, before, onehot, cols, row, far_bias, band, w_tok, w_qk_router,
          gate_up, down, down_bias, fc1, fc2, out_w, out):
    fp32, fp32r = mybir.dt.float32, mybir.dt.float32r
    ALU, ACT, AX = mybir.AluOpType, mybir.ActivationFunctionType, mybir.AxisListType

    qkv_dram = nc.dram_tensor("qkv_scratch", (128, 4, 3, TILES, 32), fp32, kind="Internal").ap()
    far_dram = nc.dram_tensor("far_scratch", (QUARTERS, 4, 4, 32, QT * 36), fp32, kind="Internal").ap()

    with ExitStack() as ctx:
        def sb(name, shape, dt=fp32):
            return ctx.enter_context(nc.sbuf_tensor(name, shape, dt))

        def sem(name):
            return ctx.enter_context(nc.semaphore(name))

        x_sb = sb("x_sb", [128, TILES, D])
        xn0 = sb("xn0", [128, TILES, D])
        gate = sb("gate", [128, TILES, D])
        xt_hi = sb("xt_hi", [128, TOKENS], fp32r)
        xt_lo = sb("xt_lo", [128, TOKENS], fp32r)
        xf = sb("xf", [128, 2, 512])
        xn_parts = sb("xn_parts", [128, 4, 512], fp32r)
        xn_hi, xn_lo = xn_parts[:, 0:2, :], xn_parts[:, 2:4, :]
        stats = sb("stats", [128, TILES, 6])
        mv = sb("mv", [128, TILES, 2])
        sd = sb("sd", [128, 2, TILES])
        rs = sb("rs", [128, 4, TILES])
        ident_sb = sb("ident_sb", [128, 128])
        anti_sb = sb("anti_sb", [128, 128], fp32r)
        headmask_sb = sb("headmask_sb", [128, 4])
        before_sb = sb("before_sb", [128, EXPERTS * EXPERTS])
        onehot_raw = sb("onehot_raw", [40, EXPERTS])
        onehot_sb = sb("onehot_sb", [40, EXPERTS, 128], fp32r)
        cols_sb = sb("cols_sb", [128, N_COLS])
        up_bias1 = sb("up_bias1", [128, EXPERTS])
        row_sb = sb("row_sb", [128, N_ROW])
        far_bias_sb = sb("far_bias_sb", [128, NFAR, HG])
        band_hi = sb("band_hi", [128, HG, WINDOW], fp32r)
        band_lo = sb("band_lo", [128, HG, WINDOW], fp32r)
        band0_hi = sb("band0_hi", [128, HG, WINDOW], fp32r)
        stage = sb("stage", [128, 2, 512])
        wtok_hi = sb("wtok_hi", [128, 512], fp32r)
        wtok_lo = sb("wtok_lo", [128, 512], fp32r)
        wqk_hi = sb("wqk_hi", [128, 264], fp32r)
        wqk_lo = sb("wqk_lo", [128, 264], fp32r)
        gu_hi = sb("gu_hi", [128, EXPERTS, 2 * INNER], fp32r)
        gu_lo = sb("gu_lo", [128, EXPERTS, 2 * INNER], fp32r)
        fc1_hi, fc1_lo = wtok_hi, wtok_lo
        fc2_sb = sb("fc2_sb", [128, FC, D])
        outw_sb = sb("outw_sb", [128, D])
        down_sb = sb("down_sb", [128, EXPERTS, D])
        db_raw = sb("db_raw", [EXPERTS, D])
        db3 = sb("db3", [72, D], fp32r)
        w3 = xn_parts[0:72, :, :].rearrange("p b n -> p (b n)")
        logit = sb("logit", [128, TILES, EXPERTS])
        logit_m = sb("logit_m", [128, 4, TILES])
        tok = sb("tok", [128, 4, 3, QT, 32])
        hg_q = sb("hg_q", [128, 2, 4 * QT, 32])
        hg_kv = sb("hg_kv", [128, 2, 4, TILES, 32])
        kv48 = sb("kv48", [128, 2, 2, 4 * QT, 32])
        qt = sb("qt", [128, TOKENS])
        kt = sb("kt", [128, 32 + TOKENS])
        qm = sb("qm", [128, 2, 4, 256])
        vbd = sb("vbd", [128, 2, 4 * QT, 32, 4])
        prob = sb("prob", [128, 2, 8, WINDOW])
        prob_t = sb("prob_t", [128, 2, 8, WINDOW])
        mnear = sb("mnear", [128, 2, 8])
        mall = sb("mall", [128, 2, 4, QT, HG])
        lsum = sb("lsum", [128, 2, 4, QT, HG])
        sfar = sb("sfar", [128, 2, NFAR, 4 * QT * HG])
        mfar = sb("mfar", [128, 2, 4, QT, HG])
        lfar = sb("lfar", [128, 2, 4 * QT * HG])
        prod = sb("prod", [128, 4 * QT * 32])
        tree = sb("tree", [128, 4 * QT * 16])
        ofar = sb("ofar", [128, 2, 4 * QT, 36])
        ofar_tok = sb("ofar_tok", [128, 4, QT, 36])
        tok_flat = tok[:].rearrange("p j w t x -> p (j w t x)")
        onear = tok_flat[:, 0:1024].rearrange("p (b n) -> p b n", b=2)
        mix = tok_flat[:, 1024:1536].rearrange("p (t x j) -> p t x j", t=QT, j=4)
        mix_t = xf[:, 0, :]
        g_act = sb("g_act", [128, 2, 512])
        u_act = sb("u_act", [128, 2, 512])
        th_act = sb("th_act", [128, 2, 512])
        rank_a = th_act[:].rearrange("p b n -> p (b n)")
        rank_b = u_act[:].rearrange("p b n -> p (b n)")
        anti_raw = u_act[:, 0, 0:128]
        band_raw = u_act[:, 1, 0:HG * WINDOW].rearrange("p (h w) -> p h w", h=HG)
        hid = vbd[:, :, :, :, :].rearrange("p b s x j -> p b (s x j)").rearrange("p b (f n) -> p b f n", f=FC)

        bank = [ctx.enter_context(nc.psum_tensor(f"bank{i}", [128, 512], fp32)) for i in range(8)]

        x_in = [sem(f"x_in{q}") for q in range(QUARTERS)]
        small_in, mat_in = sem("small_in"), sem("mat_in")
        stage_in = [sem("stage_in0"), sem("stage_in1")]
        qkv_out = [sem(f"qkv_out{q}") for q in range(QUARTERS)]
        hg_in = [sem(f"hg_in{q}") for q in range(QUARTERS)]
        k48_in = [sem(f"k48_in{q}") for q in range(QUARTERS)]
        far_out = [sem(f"far_out{q}") for q in range(QUARTERS)]
        far_in = [sem(f"far_in{q}") for q in range(QUARTERS)]
        stored = sem("stored")
        names = ("stats_done aggr_done sd_done dve_chain normed x_tr h_tr x_hi x_lo xf_done h_hi h_lo logits_ps "
                 "qk_ps qt_done kt_done tok_ps tok_done gate_pre gate_tanh gate_done split_done consts_done "
                 "zeroed pool_chain logit_sh logit_exp weights_done w_tr w_hi w_lo "
                 "w_hi2 db_done db_hi vbd_done qm_done sfar_done far_sh far_exp mfar_done score_ps near_max "
                 "shifted near_exp sum_done probt_done gate_ps up_ps wrep_ps g_raw u_raw g_half u_clip g_tanh "
                 "glu_done gu_done act_done acc_ps acc_done o_ps o_done lfar_done inv_done ofar_done o_tr mix1 "
                 "mix2 mix_done mix_tr mixt_done attn_ps x1_done bias_added base_done fc1_ps hid_done fc2_ps "
                 "y_done h2_tr h2_aff h2_hi h2_lo stats2 mall_done normed2 w3_zeroed down_ps o_pv").split()
        S = {n: sem(n) for n in names}

        SPLITS = ([(wtok_hi, wtok_lo, 0, 512), (wqk_hi, wqk_lo, 0, 264)]
                  + [(gu_hi, gu_lo, 512 * i, 512) for i in range(4)] + [(fc1_hi, fc1_lo, 0, 512)])
        SPLIT_SRC = [w_tok, w_qk_router] + [gate_up[:, 512 * i:512 * i + 512] for i in range(4)] + [fc1]
        N_GU = 3

        def flat2(t):
            ap = t[:]
            return ap.rearrange("p e n -> p (e n)") if len(t.shape) == 3 else ap

        FAR_SHIFT = (0, 2, 3, 4, 6)
        N_SMALL = 16 * 14
        N_MAT = 16 * 4

        with nc.Block() as block:

            @block.sync
            def _(sp):
                xv = x.rearrange("(t p) c -> p t c", p=128)
                by_g = qkv_dram.rearrange("(g r) j w t x -> g r j w t x", g=4)
                for q in range(QUARTERS):
                    sp.dma_start(x_sb[:, QT * q:QT * q + QT, :], xv[:, QT * q:QT * q + QT, :]).then_inc(x_in[q], 16)
                sp.dma_start(ident_sb[:], ident).then_inc(small_in, 16)
                sp.dma_start(cols_sb[:], cols).then_inc(small_in, 16)
                sp.dma_start(row_sb[:], row.to_broadcast([128, N_ROW])).then_inc(small_in, 16)
                for s in range(2):
                    n = SPLITS[s][3]
                    sp.dma_start(stage[:, s, 0:n], SPLIT_SRC[s]).then_inc(stage_in[s], 16)
                sp.dma_start(headmask_sb[:], headmask).then_inc(small_in, 16)
                sp.dma_start(anti_raw, anti).then_inc(small_in, 16)
                sp.dma_start(before_sb[:], before.to_broadcast([128, EXPERTS * EXPERTS])).then_inc(small_in, 16)
                sp.dma_start(onehot_raw[:], onehot).then_inc(small_in, 16)
                for j in range(4):
                    src = bass.AP(tensor=band.tensor, offset=96 * j, ap=[[1, 32], [4 * 96, HG], [1, WINDOW]])
                    sp.dma_start(band_raw[32 * j:32 * j + 32, :, :], src).then_inc(small_in, 16)
                sp.dma_start(db_raw[:], down_bias).then_inc(small_in, 16)
                sp.dma_start(far_bias_sb[:, :, :].rearrange("p f h -> p (f h)"), far_bias).then_inc(small_in, 16)
                sp.dma_start(down_sb[:], down.rearrange("e i h -> i e h")).then_inc(small_in, 16)
                sp.dma_start(outw_sb[:], out_w).then_inc(mat_in, 16)
                sp.dma_start(fc2_sb[:], fc2.rearrange("(f p) n -> p f n", p=128)).then_inc(mat_in, 16)
                for s in range(2, 4):
                    sp.wait_ge(S["split_done"], s - 1)
                    sp.dma_start(stage[:, s % 2, :], SPLIT_SRC[s]).then_inc(stage_in[s % 2], 16)

                def keys48(q):
                    for j in range(4):
                        for half in range(2):
                            n, r0, rs0 = (1, 16, 0) if half else (2, 0, 16)
                            for g0, g1, s0, back, skip in shifted_pieces(n, QT * q):
                                for w in (1, 2):
                                    dst = kv48[32 * j + r0:32 * j + r0 + 16, q % 2, w - 1, :, :].rearrange(
                                        "p (g t) x -> p g t x", g=4)[:, g0:g1, skip:QT, :]
                                    src = by_g[s0:s0 + g1 - g0, rs0:rs0 + 16, j, w,
                                               QT * q - back + skip:QT * q - back + QT, :]
                                    sp.dma_start(dst, src.rearrange("g r t x -> r g t x")).then_inc(k48_in[q], 16)

                for q in range(QUARTERS):
                    sp.wait_ge(S["tok_done"], QT * q + QT)
                    sp.dma_start(qkv_dram[:, :, :, QT * q:QT * q + QT, :].rearrange("p j w t x -> p (j w) (t x)"),
                                 tok[:].rearrange("p j w t x -> p (j w) (t x)")).then_inc(qkv_out[q], 16)
                    sp.wait_ge(qkv_out[q], 16)
                    if q >= 2:
                        sp.wait_ge(S["sfar_done"], q - 1)
                    for j in range(4):
                        for w in range(3):
                            dst = (hg_kv[32 * j:32 * j + 32, w - 1, :, QT * q:QT * q + QT, :] if w else
                                   hg_q[32 * j:32 * j + 32, q % 2, :, :].rearrange("p (g t) x -> p g t x", g=4))
                            sp.dma_start(dst,
                                         by_g[:, :, j, w, QT * q:QT * q + QT, :].rearrange("g r t x -> r g t x")
                                         ).then_inc(hg_in[q], 16)
                    if q == 0:
                        sp.wait_ge(S["zeroed"], 1)
                    if q < 2:
                        keys48(q)
                    if q == 0:
                        for s in range(4, len(SPLITS)):
                            sp.wait_ge(S["split_done"], s - 1)
                            sp.dma_start(stage[:, s % 2, :], SPLIT_SRC[s]).then_inc(stage_in[s % 2], 16)

                for q in range(QUARTERS):
                    sp.wait_ge(S["ofar_done"], q + 1)
                    if q + 2 < QUARTERS:
                        keys48(q + 2)
                    sp.wait_ge(S["inv_done"], q + 1)
                    for j in range(4):
                        sp.dma_start(far_dram[q, j].rearrange("g r n -> r g n"),
                                     ofar[32 * j:32 * j + 32, q % 2, :, :].rearrange("p (g t) x -> p g (t x)", g=4)
                                     ).then_inc(far_out[q], 16)
                    sp.wait_ge(far_out[q], 64)
                    if q >= 1:
                        sp.wait_ge(S["mix2"], q)
                    sp.dma_start(ofar_tok[:].rearrange("p j t x -> p j (t x)"),
                                 far_dram[q].rearrange("j g r n -> (g r) j n")).then_inc(far_in[q], 16)

                ov = out.rearrange("(t p) c -> p t c", p=128)
                for q in range(QUARTERS):
                    sp.wait_ge(S["y_done"], q + 1)
                    sp.dma_start(ov[:, QT * q:QT * q + QT, :], x_sb[:, QT * q:QT * q + QT, :]).then_inc(stored, 16)
                sp.wait_ge(stored, 16 * QUARTERS)

            def k48_total(q):
                return 16 * sum(4 * 2 * len(shifted_pieces(n, QT * q)) for n in (1, 2))

            @block.gpsimd
            def _(pool):
                P = nc.gpsimd
                chain = [0]

                def link(ins):
                    chain[0] += 1
                    ins.then_inc(S["pool_chain"], 1)
                    pool.wait_ge(S["pool_chain"], chain[0])

                link(P.memset(kv48[:, 0, :, :, :], 0.0))
                P.memset(kt[:, 0:32], 0.0)
                P.memset(db3[:].bitcast(fp32), 0.0)
                P.memset(prod[:], 0.0)
                P.memset(ofar[:, 0, :, :], 0.0)
                P.memset(vbd[:], 0.0).then_inc(S["zeroed"], 1)

                def split(s):
                    hi, lo, at, n = SPLITS[s]
                    raw = stage[:, s % 2, 0:n]
                    pool.wait_ge(stage_in[s % 2], 16 * (s // 2 + 1))
                    if s == 0:
                        qcols = raw[:, 0:384].rearrange("p (j w x) -> p j w x", j=4, w=3)[:, :, 0, :]
                        link(P.tensor_scalar(qcols, qcols, HD ** -0.5, None, ALU.mult))
                    if s == 1:
                        link(P.tensor_scalar(raw[:, 0:128], raw[:, 0:128], HD ** -0.5, None, ALU.mult))
                    link(P.tensor_copy(flat2(hi)[:, at:at + n], raw))
                    P.tensor_tensor(flat2(lo)[:, at:at + n], raw, flat2(hi)[:, at:at + n].bitcast(fp32),
                                    ALU.subtract).then_inc(S["split_done"], 1)

                split(0)
                split(1)
                pool.wait_ge(small_in, N_SMALL)
                P.tensor_scalar(cols_sb[:, C_BQ:C_BQ + 1], cols_sb[:, C_BQ:C_BQ + 1], HD ** -0.5, None, ALU.mult)
                qrow = row_sb[:, 0:384].rearrange("p (j w x) -> p j w x", j=4, w=3)[:, :, 0, :]
                P.tensor_scalar(qrow, qrow, HD ** -0.5, None, ALU.mult)
                P.tensor_scalar(up_bias1[:], cols_sb[:, C_GU:C_GU + 16].rearrange("p (e h) -> p e h", h=2)[:, :, 1],
                                1.0, None, ALU.add)
                P.tensor_copy(anti_sb[:], anti_raw)
                P.tensor_copy(onehot_sb[:], onehot_raw[:].unsqueeze(2).to_broadcast([40, EXPERTS, 128]))
                link(P.tensor_copy(band_hi[:], band_raw))
                P.tensor_tensor(band_lo[:], band_raw, band_hi[:].bitcast(fp32), ALU.subtract)
                link(P.tensor_copy(band0_hi[:, :, 32:], band_raw[:, :, 32:]))
                P.memset(band0_hi[:, :, 0:32].bitcast(fp32), CLOSED).then_inc(S["consts_done"], 1)
                for s in range(2, len(SPLITS) - 1):
                    split(s)

                pool.wait_ge(S["tok_ps"], TILES)
                P.memset(w3.bitcast(fp32), 0.0).then_inc(S["w3_zeroed"], 1)
                def far_scores(q):
                    pool.wait_ge(hg_in[q], 16 * 12)
                    pool.wait_ge(k48_in[q], k48_total(q))
                    if q >= 2:
                        pool.wait_ge(S["inv_done"], q - 1)
                    pv = prod[:].rearrange("p (g t x) -> p g t x", g=4, t=QT)
                    qv = hg_q[:, q % 2, :, :].rearrange("p (g t) x -> p g t x", g=4)
                    for f, n in enumerate(FAR_SHIFT):
                        if f == 0:
                            last = P.tensor_tensor(pv, qv,
                                                   kv48[:, q % 2, 0, :, :].rearrange("p (g t) x -> p g t x", g=4),
                                                   ALU.mult)
                        else:
                            for g0, g1, s0, back, skip in shifted_pieces(n, QT * q):
                                t0 = QT * q - back
                                if skip >= QT:
                                    continue
                                last = P.tensor_tensor(pv[:, g0:g1, skip:QT, :],
                                                       qv[:, g0:g1, skip:QT, :],
                                                       hg_kv[:, 0, s0:s0 + g1 - g0, t0 + skip:t0 + QT, :], ALU.mult)
                        link(last)
                        p8 = prod[:].rearrange("p (n d) -> p n d", d=HD)
                        t4 = tree[:].rearrange("p (n d) -> p n d", d=4)
                        link(P.tensor_tensor(t4, p8[:, :, 0:4], p8[:, :, 4:8], ALU.add))
                        link(P.tensor_tensor(t4[:, :, 0:2], t4[:, :, 0:2], t4[:, :, 2:4], ALU.add))
                        link(P.tensor_tensor(sfar[:, q % 2, f, :], t4[:, :, 0], t4[:, :, 1], ALU.add))
                        s3 = sfar[:, q % 2, f, :].rearrange("p (s h) -> p s h", h=HG)
                        last = P.tensor_tensor(s3, s3, far_bias_sb[:, f, :].unsqueeze(1).to_broadcast(
                            [128, 4 * QT, HG]), ALU.add)
                        if q == 0:
                            link(last)
                            s4 = sfar[:, 0, f, :].rearrange("p (g t h) -> p g t h", g=4, t=QT)
                            if f == 0:
                                link(P.memset(s4[:, 0, 0, :], CLOSED))
                                for j in range(4):
                                    last = P.memset(s4[32 * j:32 * j + 16, 1, 0, :], CLOSED)
                                    link(last)
                            else:
                                full, part = n // 4, n % 4
                                if full:
                                    last = P.memset(s4[:, :, 0:full, :], CLOSED)
                                if part:
                                    last = P.memset(s4[:, 0:part, full, :], CLOSED)
                    last.then_inc(S["sfar_done"], 1)

                def far_output(q):
                    pool.wait_ge(S["mall_done"], 8 * q + 8)
                    P.tensor_tensor(sfar[:, q % 2, :, :], sfar[:, q % 2, :, :],
                                    mall[:, q % 2].rearrange("p g t h -> p (g t h)").unsqueeze(1).to_broadcast(
                                        [128, NFAR, 4 * QT * HG]), ALU.subtract).then_inc(S["far_sh"], 1)
                    pool.wait_ge(S["far_exp"], q + 1)
                    if q >= 2:
                        pool.wait_ge(far_out[q - 2], 64)
                    ov = ofar[:, q % 2, :, 0:32].rearrange("p (g t) x -> p g t x", g=4)
                    pv = prod[:].rearrange("p (g t x) -> p g t x", g=4, t=QT)
                    for f, n in enumerate(FAR_SHIFT):
                        pf = sfar[:, q % 2, f, :].rearrange("p (g n) -> p g n", g=4)
                        if f == 0:
                            a = pf.unsqueeze(3).to_broadcast([128, 4, QT * HG, HD])
                            b = kv48[:, q % 2, 1, :, :].rearrange("p (g t) (h d) -> p g (t h) d", g=4, d=HD)
                            o = ofar[:, q % 2, :, 0:32].rearrange("p s (h d) -> p s h d", d=HD)
                            link(P.tensor_tensor(
                                o, sfar[:, q % 2, 0, :].rearrange("p (s h) -> p s h", h=HG).unsqueeze(3).to_broadcast(
                                    [128, 4 * QT, HG, HD]),
                                kv48[:, q % 2, 1, :, :].rearrange("p s (h d) -> p s h d", d=HD), ALU.mult))
                            continue
                        pieces = [p for p in shifted_pieces(n, QT * q) if p[4] < QT]
                        for g0, g1, s0, back, skip in pieces:
                            t0 = QT * q - back
                            last = P.tensor_tensor(
                                pv[:, g0:g1, skip:QT, :].rearrange("p g t (h d) -> p g (t h) d", d=HD),
                                pf[:, g0:g1, skip * HG:].unsqueeze(3).to_broadcast(
                                    [128, g1 - g0, (QT - skip) * HG, HD]),
                                hg_kv[:, 1, s0:s0 + g1 - g0, t0 + skip:t0 + QT, :].rearrange(
                                    "p g t (h d) -> p g (t h) d", d=HD), ALU.mult)
                        link(last)
                        for g0, g1, s0, back, skip in pieces:
                            last = P.tensor_tensor(ov[:, g0:g1, skip:QT, :], ov[:, g0:g1, skip:QT, :],
                                                   pv[:, g0:g1, skip:QT, :], ALU.add)
                        if f < NFAR - 1:
                            link(last)
                        else:
                            last.then_inc(S["ofar_done"], 1)

                far_scores(0)
                pool.wait_ge(S["gate_tanh"], QUARTERS)
                link(P.tensor_tensor(xn0[:], xn0[:], row_sb[:, R_OUT:R_OUT + D].unsqueeze(1).to_broadcast(
                    [128, TILES, D]), ALU.add))
                P.tensor_tensor(x_sb[:], x_sb[:], row_sb[:, R_FC2:R_FC2 + D].unsqueeze(1).to_broadcast(
                    [128, TILES, D]), ALU.add).then_inc(S["bias_added"], 1)
                P.tensor_scalar(gate[:], gate[:], 0.5, 0.5, ALU.mult, ALU.add).then_inc(S["gate_done"], 1)
                far_scores(1)
                split(len(SPLITS) - 1)
                far_output(0)
                far_scores(2)
                far_output(1)
                far_scores(3)
                far_output(2)
                far_output(3)
                for q in range(QUARTERS):
                    pool.wait_ge(S["x1_done"], q + 1)
                    pool.wait_ge(S["acc_done"], q + 1)
                    t = slice(QT * q, QT * q + QT)
                    P.tensor_tensor(x_sb[:, t, :], x_sb[:, t, :], xn0[:, t, :], ALU.add).then_inc(S["base_done"], 1)

            @block.scalar
            def _(act):
                A = nc.scalar

                def col(c):
                    return cols_sb[:, c:c + 1]

                act.wait_ge(S["aggr_done"], 1)
                A.activation(sd[:, 0, :], mv[:, :, 1], ACT.Sqrt, bias=EPS).then_inc(S["sd_done"], 1)
                act.wait_ge(S["dve_chain"], 3)
                A.activation(sd[:, 1, :], rs[:, 1, :], ACT.Sqrt, bias=EPS).then_inc(S["sd_done"], 1)

                for q in range(QUARTERS):
                    ts = slice(512 * q, 512 * q + 512)
                    act.wait_ge(S["x_tr"], q + 1)
                    A.copy(xt_hi[:, ts], bank[0][:]).then_inc(S["x_hi"], 1)
                    act.wait_ge(S["xf_done"], q + 1)
                    if q >= 2:
                        act.wait_ge(S["tok_ps"], QT * (q - 1))
                    A.copy(xn_hi[:, q % 2, :], xf[:, q % 2, :]).then_inc(S["h_hi"], 1)
                    if q == 0:
                        act.wait_ge(S["consts_done"], 1)
                    act.wait_ge(S["qk_ps"], 2 * q + 1)
                    A.activation(qt[:, ts], bank[2][:], ACT.Identity, bias=col(C_BQ)).then_inc(S["qt_done"], 1)
                    act.wait_ge(S["qk_ps"], 2 * q + 2)
                    A.activation(kt[:, 32 + 512 * q:32 + 512 * q + 512], bank[3][:], ACT.Identity,
                                 bias=col(C_BK)).then_inc(S["kt_done"], 1)
                act.wait_ge(S["logit_sh"], 1)
                A.activation(logit[:], logit[:], ACT.Exp).then_inc(S["logit_exp"], 1)
                for q in range(QUARTERS):
                    act.wait_ge(S["gate_pre"], QT * q + QT)
                    t = slice(QT * q, QT * q + QT)
                    A.activation(gate[:, t, :], gate[:, t, :], ACT.Tanh, scale=0.5).then_inc(S["gate_tanh"], 1)
                act.wait_ge(small_in, N_SMALL)
                act.wait_ge(S["zeroed"], 1)
                A.copy(db3[0:8, :], db_raw[:])
                A.copy(db3[32:40, :], db_raw[:]).then_inc(S["db_hi"], 1)
                act.wait_ge(S["w3_zeroed"], 1)
                for q in range(QUARTERS):
                    ts = slice(512 * q, 512 * q + 512)
                    act.wait_ge(S["w_tr"], q + 1)
                    A.copy(w3[0:8, ts], bank[7][0:8, :])
                    A.copy(w3[64:72, ts], bank[7][0:8, :]).then_inc(S["w_hi"], 1)

                def v_blocks(q):
                    act.wait_ge(hg_in[q], 16 * 12)
                    if q >= 2:
                        act.wait_ge(S["o_pv"], 8 * (q - 1) + 4)
                    for j in range(4):
                        last = A.copy(vbd[32 * j:32 * j + 32, q % 2, :, :, j].rearrange("p (g t) x -> p g (t x)", g=4),
                                      hg_kv[32 * j:32 * j + 32, 1, :, QT * q:QT * q + QT, :].rearrange(
                                          "p g t x -> p g (t x)"))
                    last.then_inc(S["vbd_done"], 1)

                def near_out(c):
                    act.wait_ge(S["o_pv"], 4 * c + 4)
                    if c == 0:
                        act.wait_ge(qkv_out[QUARTERS - 1], 16)
                    if c >= 4 and c % 2 == 0:
                        act.wait_ge(S["o_tr"], c // 2 - 1)
                    A.copy(onear[:, (c // 2) % 2, 256 * (c % 2):256 * (c % 2) + 256], bank[2][:, 0:256]
                           ).then_inc(S["o_done"], 1)

                def far_weights(q):
                    act.wait_ge(S["far_sh"], q + 1)
                    A.activation(sfar[:, q % 2, :, :], sfar[:, q % 2, :, :], ACT.Exp).then_inc(S["far_exp"], 1)

                def mix_evac(q):
                    act.wait_ge(S["mix_tr"], q + 1)
                    A.copy(mix_t, bank[7][:]).then_inc(S["mixt_done"], 1)

                v_blocks(0)
                for i in range(STEPS + 1):
                    if i < STEPS:
                        act.wait_ge(S["shifted"], i + 1)
                        A.activation(prob[:, i % 2, :, :], prob[:, i % 2, :, :], ACT.Exp).then_inc(S["near_exp"], 1)
                    if i >= 1:
                        act.wait_ge(S["g_half"], i)
                        A.activation(th_act[:, (i - 1) % 2, :], g_act[:, (i - 1) % 2, :], ACT.Tanh, scale=ALPHA
                                     ).then_inc(S["g_tanh"], 1)
                    if i < STEPS:
                        e = i % EXPERTS
                        act.wait_ge(S["gate_ps"], i + 1)
                        if i >= 2:
                            act.wait_ge(S["glu_done"], i - 1)
                        A.activation(g_act[:, i % 2, :], bank[3][:], ACT.Identity,
                                     bias=col(C_GU + 2 * e)).then_inc(S["g_raw"], 1)
                        act.wait_ge(S["up_ps"], i + 1)
                        if i >= 2:
                            act.wait_ge(S["down_ps"], i - 1)
                        A.activation(u_act[:, i % 2, :], bank[4][:], ACT.Identity,
                                     bias=up_bias1[:, e:e + 1]).then_inc(S["u_raw"], 1)
                    if i % 4 == 1 and i > 4:
                        near_out(i // 4 - 1)
                    if i % 8 == 1 and i > 8:
                        far_weights(i // 8 - 1)
                    if i % 8 == 5 and i // 8 < QUARTERS - 1:
                        v_blocks(i // 8 + 1)
                    if i % 8 == 7 and i > 8:
                        mix_evac(i // 8 - 1)
                near_out(7)
                far_weights(3)
                mix_evac(3)
                act.wait_ge(S["stats2"], 1)
                A.activation(sd[:, 0, :], mv[:, :, 1], ACT.Sqrt, bias=EPS).then_inc(S["sd_done"], 1)
                for q in range(QUARTERS):
                    act.wait_ge(S["h2_aff"], q + 1)
                    A.copy(xt_hi[:, 512 * q:512 * q + 512], xf[:, q % 2, :]).then_inc(S["h2_hi"], 1)
                    for f in range(FC):
                        act.wait_ge(S["fc1_ps"], FC * q + f + 1)
                        if q >= 2 and f == 0:
                            act.wait_ge(S["fc2_ps"], q - 1)
                        A.activation(hid[:, q % 2, f, :], bank[2 + f][:], ACT.Gelu,
                                     bias=col(C_F1 + f)).then_inc(S["hid_done"], 1)

            @block.vector
            def _(dve):
                V = nc.vector
                chain = [0]

                def link(ins):
                    chain[0] += 1
                    ins.then_inc(S["dve_chain"], 1)
                    dve.wait_ge(S["dve_chain"], chain[0])

                def col(c):
                    return cols_sb[:, c:c + 1]

                for t in range(TILES):
                    if t % QT == 0:
                        dve.wait_ge(x_in[t // QT], 16)
                    last = V.bn_stats(stats[:, t, :], x_sb[:, t, :])
                last.then_inc(S["stats_done"], 1)
                dve.wait_ge(S["stats_done"], 1)
                for t in range(TILES):
                    last = V.bn_aggr(mv[:, t, :], stats[:, t, :])
                last.then_inc(S["aggr_done"], 1)
                dve.wait_ge(S["sd_done"], 1)
                link(V.reciprocal(rs[:, 0, :], sd[:, 0, :]))
                link(V.tensor_tensor(rs[:, 1, :], mv[:, :, 1], rs[:, 0, :], ALU.mult))
                link(V.tensor_tensor(rs[:, 1, :], rs[:, 1, :], rs[:, 0, :], ALU.mult))
                for t in range(TILES):
                    last = V.tensor_scalar(xn0[:, t, :], x_sb[:, t, :], mv[:, t, 0:1], rs[:, 0, t:t + 1],
                                           ALU.subtract, ALU.mult)
                dve.wait_ge(S["sd_done"], 2)
                link(V.reciprocal(rs[:, 2, :], sd[:, 1, :]))
                link(V.tensor_tensor(rs[:, 3, :], rs[:, 2, :], rs[:, 0, :], ALU.mult))
                for t in range(TILES):
                    last = V.tensor_scalar(gate[:, t, :], x_sb[:, t, :], mv[:, t, 0:1], rs[:, 3, t:t + 1],
                                           ALU.subtract, ALU.mult)
                    if t % QT == QT - 1:
                        last.then_inc(S["normed"], 1)

                dve.wait_ge(small_in, N_SMALL)

                def operands(q):
                    ts = slice(512 * q, 512 * q + 512)
                    dve.wait_ge(S["h_tr"], q + 1)
                    if q >= 2:
                        dve.wait_ge(S["h_lo"], q - 1)
                    V.tensor_scalar(xf[:, q % 2, :], bank[1][:], col(C_G1), col(C_B1), ALU.mult, ALU.add
                                    ).then_inc(S["xf_done"], 1)
                    dve.wait_ge(S["x_hi"], q + 1)
                    V.tensor_tensor(xt_lo[:, ts], bank[0][:], xt_hi[:, ts].bitcast(fp32), ALU.subtract
                                    ).then_inc(S["x_lo"], 1)
                    dve.wait_ge(S["h_hi"], q + 1)
                    if q >= 2:
                        dve.wait_ge(S["tok_ps"], QT * (q - 1))
                    V.tensor_tensor(xn_lo[:, q % 2, :], xf[:, q % 2, :], xn_hi[:, q % 2, :].bitcast(fp32),
                                    ALU.subtract).then_inc(S["h_lo"], 1)

                def tokens(q):
                    if q == 0:
                        dve.wait_ge(S["consts_done"], 1)
                    else:
                        dve.wait_ge(qkv_out[q - 1], 16)
                    for tt in range(QT):
                        t = QT * q + tt
                        dve.wait_ge(S["tok_ps"], t + 1)
                        V.tensor_tensor(tok[:, :, :, tt, :].rearrange("p j w x -> p (j w) x"),
                                        bank[4 + t % 2][:, 0:384].rearrange("p (a x) -> p a x", x=32),
                                        row_sb[:, 0:384].rearrange("p (a x) -> p a x", x=32), ALU.add
                                        ).then_inc(S["tok_done"], 1)
                        V.tensor_tensor(gate[:, t, :], bank[4 + t % 2][:, 384:512], row_sb[:, R_GATE:R_GATE + D],
                                        ALU.add).then_inc(S["gate_pre"], 1)

                operands(0)
                for q in range(1, QUARTERS):
                    operands(q)
                    tokens(q - 1)
                tokens(3)

                dve.wait_ge(S["logits_ps"], 1)
                link(V.tensor_tensor(logit[:], bank[6][:, 0:TILES * EXPERTS].rearrange("p (t e) -> p t e", e=EXPERTS),
                                     row_sb[:, R_ROUTER:R_ROUTER + EXPERTS].unsqueeze(1).to_broadcast(
                                         [128, TILES, EXPERTS]), ALU.add))
                link(V.tensor_reduce(logit_m[:, 0, :], logit[:], AX.X, ALU.max))
                V.tensor_tensor(logit[:], logit[:], logit_m[:, 0, :].unsqueeze(2).to_broadcast(
                    [128, TILES, EXPERTS]), ALU.subtract).then_inc(S["logit_sh"], 1)
                dve.wait_ge(S["logit_exp"], 1)
                dve.wait_ge(S["consts_done"], 1)
                e4 = logit[:].unsqueeze(3).to_broadcast([128, TILES, EXPERTS, EXPERTS])
                e4t = logit[:].unsqueeze(2).to_broadcast([128, TILES, EXPERTS, EXPERTS])
                equal = rank_a.rearrange("p (t a b) -> p t a b", t=TILES, a=EXPERTS)
                greater = rank_b.rearrange("p (t a b) -> p t a b", t=TILES, a=EXPERTS)
                link(V.tensor_tensor(equal, e4t, e4, ALU.is_equal))
                link(V.tensor_tensor(equal, equal, before_sb[:].rearrange("p (a b) -> p a b", a=EXPERTS).unsqueeze(1)
                                     .to_broadcast([128, TILES, EXPERTS, EXPERTS]), ALU.mult))
                link(V.tensor_tensor(greater, e4t, e4, ALU.is_gt))
                link(V.tensor_tensor(equal, equal, greater, ALU.add))
                link(V.tensor_reduce(logit_m[:, 1, :], logit[:], AX.X, ALU.add))
                link(V.reciprocal(logit_m[:, 2, :], logit_m[:, 1, :]))
                rank = rank_b[:, 0:TILES * EXPERTS]
                link(V.tensor_reduce(rank.rearrange("p (t e) -> p t e", e=EXPERTS),
                                     rank_a.rearrange("p (t a b) -> p t a b", t=TILES, a=EXPERTS), AX.X, ALU.add))
                link(V.tensor_scalar(rank, rank, 2.0, None, ALU.is_lt))
                link(V.tensor_tensor(rank, rank, logit[:].rearrange("p t e -> p (t e)"), ALU.mult))
                V.tensor_tensor(rank_a[:, 0:TILES * EXPERTS].rearrange("p (t e) -> p t e", e=EXPERTS),
                                rank.rearrange("p (t e) -> p t e", e=EXPERTS),
                                logit_m[:, 2, :].unsqueeze(2).to_broadcast([128, TILES, EXPERTS]), ALU.mult
                                ).then_inc(S["normed2"], 1)
                dve.wait_ge(S["db_hi"], 1)
                V.tensor_tensor(db3[64:72, :], db_raw[:], db3[0:8, :].bitcast(fp32), ALU.subtract
                                ).then_inc(S["db_done"], 1)
                for q in range(QUARTERS):
                    ts = slice(512 * q, 512 * q + 512)
                    dve.wait_ge(S["w_hi"], q + 1)
                    V.tensor_tensor(w3[32:40, ts], bank[7][0:8, :], w3[0:8, ts].bitcast(fp32), ALU.subtract
                                    ).then_inc(S["w_lo"], 1)

                def masked_q(c):
                    dve.wait_ge(S["qt_done"], c // 2 + 1)
                    if c >= 2:
                        dve.wait_ge(S["score_ps"], 4 * (c - 1))
                    for j in range(4):
                        last = V.tensor_scalar(qm[:, c % 2, j, :], qt[:, 256 * c:256 * c + 256],
                                               headmask_sb[:, j:j + 1], None, ALU.mult)
                    last.then_inc(S["qm_done"], 1)

                def far_max(q):
                    dve.wait_ge(S["sfar_done"], q + 1)
                    V.tensor_reduce(mfar[:, q % 2].rearrange("p g t h -> p (g t h)"),
                                    sfar[:, q % 2, :, :].rearrange("p f n -> p n f"), AX.X, ALU.max
                                    ).then_inc(S["mfar_done"], 1)

                def sums_and_transpose(i):
                    c, h = i // 4, i % 4
                    q, tl = c // 2, 2 * (c % 2)
                    dve.wait_ge(S["near_exp"], i + 1)
                    if i >= 2:
                        dve.wait_ge(S["o_pv"], i - 1)
                    V.tensor_reduce(lsum[:, q % 2, :, tl:tl + 2, h].rearrange("p g t -> p t g"),
                                    prob[:, i % 2].rearrange("p (t g) w -> p t g w", t=2), AX.X, ALU.add
                                    ).then_inc(S["sum_done"], 1)
                    V.transpose(prob_t[:, i % 2].rearrange("p s w -> p (s w)"),
                                prob[:, i % 2].rearrange("p s w -> p (s w)")).then_inc(S["probt_done"], 1)

                def expert_out(i):
                    dve.wait_ge(S["g_tanh"], i + 1)
                    V.scalar_tensor_tensor(out=th_act[:, i % 2, :], in0=th_act[:, i % 2, :], scalar=1.0,
                                           in1=g_act[:, i % 2, :], op0=ALU.add, op1=ALU.mult).then_inc(S["glu_done"], 1)
                    dve.wait_ge(S["glu_done"], i + 1)
                    V.tensor_tensor(u_act[:, i % 2, :], th_act[:, i % 2, :], u_act[:, i % 2, :], ALU.mult
                                    ).then_inc(S["gu_done"], 1)
                    dve.wait_ge(S["gu_done"], i + 1)
                    dve.wait_ge(S["wrep_ps"], i + 1)
                    V.tensor_tensor(u_act[:, i % 2, :], u_act[:, i % 2, :], bank[5][:], ALU.mult
                                    ).then_inc(S["act_done"], 1)

                def acc_out(q):
                    dve.wait_ge(S["down_ps"], EXPERTS * (q + 1))
                    t = slice(QT * q, QT * q + QT)
                    if q == 0:
                        dve.wait_ge(S["bias_added"], 1)
                    V.tensor_tensor(x_sb[:, t, :], x_sb[:, t, :], bank[6][:].rearrange("p (t c) -> p t c", c=D),
                                    ALU.add).then_inc(S["acc_done"], 1)

                def far_sum(q):
                    dve.wait_ge(S["far_exp"], q + 1)
                    if q >= 2:
                        dve.wait_ge(far_out[q - 2], 64)
                    dve.wait_ge(S["sum_done"], 8 * q + 8)
                    link(V.tensor_reduce(lfar[:, q % 2, :], sfar[:, q % 2, :, :].rearrange("p f n -> p n f"),
                                         AX.X, ALU.add))
                    link(V.tensor_tensor(lfar[:, q % 2, :], lfar[:, q % 2, :],
                                         lsum[:, q % 2].rearrange("p g t h -> p (g t h)"), ALU.add))
                    if q == 0:
                        dve.wait_ge(S["zeroed"], 1)
                    V.reciprocal(ofar[:, q % 2, :, 32:36], lfar[:, q % 2, :].rearrange("p (s h) -> p s h", h=HG)
                                 ).then_inc(S["inv_done"], 1)

                def mix_heads(q):
                    t = slice(QT * q, QT * q + QT)
                    dve.wait_ge(far_in[q], 16)
                    dve.wait_ge(S["o_tr"], q + 1)
                    if q >= 1:
                        dve.wait_ge(S["mix_tr"], q)
                    if q == 0:
                        dve.wait_ge(S["gate_done"], 1)
                    V.tensor_tensor(mix, bank[7][:].rearrange("p (t x j) -> p t x j", t=QT, j=4),
                                    ofar_tok[:, :, :, 0:32].rearrange("p j t x -> p t x j"), ALU.add
                                    ).then_inc(S["mix1"], 1)
                    dve.wait_ge(S["mix1"], q + 1)
                    for tt in range(QT):
                        last = V.tensor_tensor(
                            mix[:, tt].rearrange("p (h d) j -> p h d j", d=HD),
                            mix[:, tt].rearrange("p (h d) j -> p h d j", d=HD),
                            ofar_tok[:, :, tt, 32:36].rearrange("p j h -> p h j").unsqueeze(2).to_broadcast(
                                [128, HG, HD, 4]), ALU.mult)
                    last.then_inc(S["mix2"], 1)
                    dve.wait_ge(S["mix2"], q + 1)
                    V.tensor_tensor(mix.rearrange("p t x j -> p t (x j)"), mix.rearrange("p t x j -> p t (x j)"),
                                    gate[:, t, :], ALU.mult).then_inc(S["mix_done"], 1)

                def residual(q):
                    t = slice(QT * q, QT * q + QT)
                    dve.wait_ge(S["attn_ps"], q + 1)
                    V.tensor_tensor(xn0[:, t, :], xn0[:, t, :], bank[7][:].rearrange("p (t c) -> p t c", c=D),
                                    ALU.add).then_inc(S["x1_done"], 1)
                    dve.wait_ge(S["x1_done"], q + 1)
                    for tt in range(QT * q, QT * q + QT):
                        last = V.bn_stats(stats[:, tt, :], xn0[:, tt, :])
                    last.then_inc(S["stats_done"], 1)

                def clips(i):
                    dve.wait_ge(S["g_raw"], i + 1)
                    V.tensor_scalar(g_act[:, i % 2, :], g_act[:, i % 2, :], LIMIT, 0.5, ALU.min, ALU.mult
                                    ).then_inc(S["g_half"], 1)
                    dve.wait_ge(S["u_raw"], i + 1)
                    V.tensor_scalar(u_act[:, i % 2, :], u_act[:, i % 2, :], 1.0 - LIMIT, 1.0 + LIMIT, ALU.max, ALU.min
                                    ).then_inc(S["u_clip"], 1)

                masked_q(0)
                far_max(0)
                for i in range(STEPS):
                    c, h = i // 4, i % 4
                    q, tl = c // 2, 2 * (c % 2)
                    dve.wait_ge(S["score_ps"], i + 1)
                    V.tensor_reduce(mnear[:, i % 2, :], bank[i % 2][:].rearrange("p (s w) -> p s w", w=WINDOW),
                                    AX.X, ALU.max).then_inc(S["near_max"], 1)
                    dve.wait_ge(S["near_max"], i + 1)
                    if i % 8 == 0:
                        dve.wait_ge(S["mfar_done"], q + 1)
                        if q >= 2:
                            dve.wait_ge(S["far_sh"], q - 1)
                    mv_ = mall[:, q % 2, :, tl:tl + 2, h].rearrange("p g t -> p t g")
                    V.tensor_tensor(mv_, mnear[:, i % 2, :].rearrange("p (t g) -> p t g", t=2),
                                    mfar[:, q % 2, :, tl:tl + 2, h].rearrange("p g t -> p t g"), ALU.max
                                    ).then_inc(S["mall_done"], 1)
                    dve.wait_ge(S["mall_done"], i + 1)
                    if i >= 2:
                        dve.wait_ge(S["probt_done"], i - 1)
                    V.tensor_tensor(prob[:, i % 2].rearrange("p (t g) w -> p t g w", t=2),
                                    bank[i % 2][:].rearrange("p (t g w) -> p t g w", t=2, w=WINDOW),
                                    mv_.unsqueeze(3).to_broadcast([128, 2, 4, WINDOW]), ALU.subtract
                                    ).then_inc(S["shifted"], 1)
                    if i >= 1:
                        clips(i - 1)
                        sums_and_transpose(i - 1)
                        expert_out(i - 1)
                    if h == 1 and c + 1 < 8:
                        masked_q(c + 1)
                    if i % 8 == 1 and i > 8:
                        acc_out(q - 1)
                    if i % 8 == 2 and i > 8:
                        far_sum(q - 1)
                    if i % 8 == 5 and q + 1 < QUARTERS:
                        far_max(q + 1)
                    if i % 8 == 6 and q >= 1:
                        mix_heads(q - 1)
                    if i % 8 == 1 and q >= 2:
                        residual(q - 2)
                clips(STEPS - 1)
                sums_and_transpose(STEPS - 1)
                expert_out(STEPS - 1)
                acc_out(3)
                residual(2)
                far_sum(3)
                mix_heads(3)
                residual(3)

                dve.wait_ge(S["stats_done"], 1 + QUARTERS)
                for t in range(TILES):
                    last = V.bn_aggr(mv[:, t, :], stats[:, t, :])
                last.then_inc(S["stats2"], 1)
                dve.wait_ge(S["sd_done"], 3)
                link(V.reciprocal(rs[:, 0, :], sd[:, 0, :]))
                for q in range(QUARTERS):
                    for t in range(QT * q, QT * q + QT):
                        last = V.tensor_scalar(gate[:, t, :], xn0[:, t, :], mv[:, t, 0:1], rs[:, 0, t:t + 1],
                                               ALU.subtract, ALU.mult)
                    last.then_inc(S["normed"], 1)

                def ffn_operands(q):
                    ts = slice(512 * q, 512 * q + 512)
                    dve.wait_ge(S["h2_tr"], q + 1)
                    if q >= 2:
                        dve.wait_ge(S["h2_lo"], q - 1)
                    V.tensor_scalar(xf[:, q % 2, :], bank[q % 2][:], col(C_G2), col(C_B2), ALU.mult, ALU.add
                                    ).then_inc(S["h2_aff"], 1)
                    dve.wait_ge(S["h2_hi"], q + 1)
                    V.tensor_tensor(xt_lo[:, ts], xf[:, q % 2, :], xt_hi[:, ts].bitcast(fp32), ALU.subtract
                                    ).then_inc(S["h2_lo"], 1)

                def ffn_out(q):
                    t = slice(QT * q, QT * q + QT)
                    dve.wait_ge(S["fc2_ps"], q + 1)
                    dve.wait_ge(S["base_done"], q + 1)
                    V.tensor_tensor(x_sb[:, t, :], x_sb[:, t, :], bank[6 + q % 2][:].rearrange("p (t c) -> p t c", c=D),
                                    ALU.add).then_inc(S["y_done"], 1)

                ffn_operands(0)
                for q in range(1, QUARTERS):
                    ffn_operands(q)
                    ffn_out(q - 1)
                ffn_out(3)

            @block.tensor
            def _(pe):
                E = nc.tensor

                def three(out_ap, w_hi, w_lo, m_hi, m_lo, start=True):
                    E.matmul(out_ap, w_hi, m_hi, start=start, stop=False)
                    E.matmul(out_ap, w_lo, m_hi, start=False, stop=False)
                    return E.matmul(out_ap, w_hi, m_lo, start=False, stop=True)

                def transposes(q):
                    pe.wait_ge(S["normed"], q + 1)
                    if q >= 1:
                        pe.wait_ge(S["x_lo"], q)
                        pe.wait_ge(S["xf_done"], q)
                    for tt in range(QT):
                        last = E.transpose(bank[0][:, 128 * tt:128 * tt + 128], xn0[:, QT * q + tt, :], ident_sb[:])
                    last.then_inc(S["x_tr"], 1)
                    for tt in range(QT):
                        last = E.transpose(bank[1][:, 128 * tt:128 * tt + 128], gate[:, QT * q + tt, :], ident_sb[:])
                    last.then_inc(S["h_tr"], 1)

                def projections(q):
                    b = q % 2
                    pe.wait_ge(S["x_lo"], q + 1)
                    if q == 0:
                        pe.wait_ge(S["split_done"], 2)
                    for tt in range(QT):
                        t = QT * q + tt
                        ts = slice(128 * t, 128 * t + 128)
                        last = three(bank[6][:, EXPERTS * t:EXPERTS * t + EXPERTS], xt_hi[:, ts], xt_lo[:, ts],
                                     wqk_hi[:, 256:264], wqk_lo[:, 256:264])
                    if q == QUARTERS - 1:
                        last.then_inc(S["logits_ps"], 1)
                    pe.wait_ge(S["h_lo"], q + 1)
                    for k in range(2):
                        if q >= 1:
                            pe.wait_ge(S["kt_done"] if k else S["qt_done"], q)
                        three(bank[2 + k][:], wqk_hi[:, 128 * k:128 * k + 128], wqk_lo[:, 128 * k:128 * k + 128],
                              xn_hi[:, b, :], xn_lo[:, b, :]).then_inc(S["qk_ps"], 1)
                    for tt in range(QT):
                        t = QT * q + tt
                        ts = slice(128 * tt, 128 * tt + 128)
                        if t >= 2:
                            pe.wait_ge(S["gate_pre"], t - 1)
                        three(bank[4 + t % 2][:], xn_hi[:, b, ts], xn_lo[:, b, ts], wtok_hi[:], wtok_lo[:]
                              ).then_inc(S["tok_ps"], 1)

                pe.wait_ge(small_in, N_SMALL)
                transposes(0)
                for q in range(QUARTERS):
                    if q + 1 < QUARTERS:
                        transposes(q + 1)
                    projections(q)

                pe.wait_ge(S["normed2"], 1)
                for q in range(QUARTERS):
                    if q >= 1:
                        pe.wait_ge(S["w_lo"], q)
                    for tt in range(QT):
                        t = QT * q + tt
                        last = E.transpose(bank[7][0:8, 128 * tt:128 * tt + 128],
                                           rank_a[:, EXPERTS * t:EXPERTS * t + EXPERTS], ident_sb[:])
                    last.then_inc(S["w_tr"], 1)

                def scores(i):
                    c, h = i // 4, i % 4
                    b = bank[i % 2]
                    if h == 0:
                        pe.wait_ge(S["qm_done"], c + 1)
                        pe.wait_ge(S["kt_done"], c // 2 + 1)
                    if i == 0:
                        pe.wait_ge(S["consts_done"], 1)
                        pe.wait_ge(S["x_lo"], QUARTERS)
                        pe.wait_ge(S["xf_done"], QUARTERS)
                        pe.wait_ge(S["zeroed"], 1)
                    if i >= 2:
                        pe.wait_ge(S["shifted"], i - 1)
                    n0 = 0
                    if c == 0:
                        E.matmul(b[:, 0:WINDOW], anti_sb[:], band0_hi[:, h, :], start=True, stop=False,
                                 skip_group_check=True)
                        E.matmul(b[:, 32:WINDOW], anti_sb[:], band_lo[:, h, 32:], start=False, stop=False,
                                 skip_group_check=True)
                        n0 = 1
                    n = 8 - n0
                    for k, part in enumerate((band_hi, band_lo)):
                        E.matmul(b[:, WINDOW * n0:512].rearrange("p (s w) -> p s w", w=WINDOW), anti_sb[:],
                                 part[:, h, :].unsqueeze(1).to_broadcast([128, n, WINDOW]),
                                 start=(k == 0 and n0 == 0), stop=False, skip_group_check=True)
                    for s in range(8):
                        for j in range(4):
                            last = E.matmul(b[32 * j:32 * j + 32, WINDOW * s:WINDOW * s + WINDOW],
                                            qm[32 * h:32 * h + 32, c % 2, j, 32 * s:32 * s + 32],
                                            kt[32 * h:32 * h + 32, 256 * c + 32 * s:256 * c + 32 * s + WINDOW],
                                            start=False, stop=True, skip_group_check=True,
                                            tile_position=(32 * h, 32 * j))
                    last.then_inc(S["score_ps"], 1)

                def weighted_v(i):
                    c, h = i // 4, i % 4
                    if h == 0:
                        pe.wait_ge(S["vbd_done"], c // 2 + 1)
                        if c >= 1:
                            pe.wait_ge(S["o_done"], c)
                    pe.wait_ge(S["probt_done"], i + 1)
                    if i == 0:
                        pe.wait_ge(S["qt_done"], QUARTERS)
                    for s in range(8):
                        st = 8 * c + s
                        for half in range(2):
                            kst = st - 1 + half
                            if kst < 0:
                                continue
                            slot, tile, g = (kst // 16) % 2, (kst // 4) % QT, kst % 4
                            last = E.matmul(bank[2][32 * h:32 * h + 32, 32 * s:32 * s + 32],
                                            vbd[:, slot, QT * g + tile, 8 * h:8 * h + 8, :].rearrange("p x j -> p (x j)"),
                                            prob_t[:, i % 2, s, 32 * half:32 * half + 32],
                                            start=(half == 0 or st == 0), stop=(half == 1), skip_group_check=True,
                                            tile_position=(0, 32 * h))
                    last.then_inc(S["o_pv"], 1)

                def experts_in(i):
                    q, e = i // EXPERTS, i % EXPERTS
                    ts = slice(512 * q, 512 * q + 512)
                    if i == 0:
                        pe.wait_ge(S["kt_done"], QUARTERS)
                        pe.wait_ge(S["gate_pre"], TILES)
                    if q == 0 and e % 2 == 0:
                        pe.wait_ge(S["split_done"], N_GU + e // 2)
                    for half, done, b, free in ((0, "gate_ps", 3, "g_raw"), (1, "up_ps", 4, "u_raw")):
                        if i >= 1:
                            pe.wait_ge(S[free], i)
                        ws = slice(INNER * half, INNER * half + INNER)
                        three(bank[b][:], gu_hi[:, e, ws], gu_lo[:, e, ws], xt_hi[:, ts], xt_lo[:, ts]
                              ).then_inc(S[done], 1)

                def weight_rows(i):
                    q, e = i // EXPERTS, i % EXPERTS
                    if e == 0:
                        pe.wait_ge(S["w_lo"], q + 1)
                    if i >= 1:
                        pe.wait_ge(S["act_done"], i)
                    E.matmul(bank[5][:], onehot_sb[:, e, :], w3[0:40, 512 * q:512 * q + 512], start=True, stop=True
                             ).then_inc(S["wrep_ps"], 1)

                def experts_out(i):
                    q, e = i // EXPERTS, i % EXPERTS
                    if e == 0:
                        if q == 0:
                            pe.wait_ge(S["db_done"], 1)
                            pe.wait_ge(S["logit_sh"], 1)
                        else:
                            pe.wait_ge(S["acc_done"], q)
                        for tt in range(QT):
                            t = QT * q + tt
                            E.matmul(bank[6][:, 128 * tt:128 * tt + 128], w3[:, 128 * t:128 * t + 128], db3[:],
                                     start=(tt == 0), stop=False, skip_group_check=True)
                    pe.wait_ge(S["act_done"], i + 1)
                    for tt in range(QT):
                        last = E.matmul(bank[6][:, 128 * tt:128 * tt + 128], u_act[:, i % 2, 128 * tt:128 * tt + 128],
                                        down_sb[:, e, :], start=False, stop=(e == EXPERTS - 1), skip_group_check=True)
                    last.then_inc(S["down_ps"], 1)

                def heads_to_tokens(q):
                    pe.wait_ge(S["o_done"], 2 * q + 2)
                    if q == 0:
                        pe.wait_ge(S["w_lo"], QUARTERS)
                    else:
                        pe.wait_ge(S["x1_done"], q)
                    for tt in range(QT):
                        last = E.transpose(bank[7][:, 128 * tt:128 * tt + 128],
                                           onear[:, q % 2, 128 * tt:128 * tt + 128], ident_sb[:])
                    last.then_inc(S["o_tr"], 1)

                def mix_to_channels(q):
                    pe.wait_ge(S["mix_done"], q + 1)
                    for tt in range(QT):
                        last = E.transpose(bank[7][:, 128 * tt:128 * tt + 128],
                                           mix[:, tt].rearrange("p x j -> p (x j)"), ident_sb[:])
                    last.then_inc(S["mix_tr"], 1)

                def attention_out(q):
                    if q == 0:
                        pe.wait_ge(mat_in, 32)
                    pe.wait_ge(S["mixt_done"], q + 1)
                    for tt in range(QT):
                        last = E.matmul(bank[7][:, 128 * tt:128 * tt + 128], mix_t[:, 128 * tt:128 * tt + 128],
                                        outw_sb[:], start=True, stop=True)
                    last.then_inc(S["attn_ps"], 1)

                for i in range(STEPS + 2):
                    if i < STEPS:
                        scores(i)
                    if i >= 2:
                        weighted_v(i - 2)
                        experts_out(i - 2)
                    if 1 <= i <= STEPS:
                        weight_rows(i - 1)
                    if i < STEPS:
                        experts_in(i)
                    if i % 8 == 5 and i > 8:
                        heads_to_tokens(i // 8 - 1)
                    if i % 8 == 7 and i > 8:
                        mix_to_channels(i // 8 - 1)
                    if i % 8 == 0 and i > 8:
                        attention_out(i // 8 - 2)
                heads_to_tokens(3)
                mix_to_channels(3)
                attention_out(3)

                def ffn_transposes(q):
                    pe.wait_ge(S["normed"], QUARTERS + q + 1)
                    if q >= 2:
                        pe.wait_ge(S["h2_aff"], q - 1)
                    for tt in range(QT):
                        last = E.transpose(bank[q % 2][:, 128 * tt:128 * tt + 128], gate[:, QT * q + tt, :], ident_sb[:])
                    last.then_inc(S["h2_tr"], 1)

                def ffn_up(q):
                    ts = slice(512 * q, 512 * q + 512)
                    pe.wait_ge(S["h2_lo"], q + 1)
                    for f in range(FC):
                        if q >= 1:
                            pe.wait_ge(S["hid_done"], FC * (q - 1) + f + 1)
                        ws = slice(128 * f, 128 * f + 128)
                        three(bank[2 + f][:], fc1_hi[:, ws], fc1_lo[:, ws], xt_hi[:, ts], xt_lo[:, ts]
                              ).then_inc(S["fc1_ps"], 1)

                def ffn_down(q):
                    pe.wait_ge(S["hid_done"], FC * q + FC)
                    if q == 0:
                        pe.wait_ge(S["acc_done"], QUARTERS)
                    if q >= 2:
                        pe.wait_ge(S["y_done"], q - 1)
                    for tt in range(QT):
                        for f in range(FC):
                            last = E.matmul(bank[6 + q % 2][:, 128 * tt:128 * tt + 128],
                                            hid[:, q % 2, f, 128 * tt:128 * tt + 128], fc2_sb[:, f, :],
                                            start=(f == 0), stop=(f == FC - 1))
                    last.then_inc(S["fc2_ps"], 1)

                pe.wait_ge(S["split_done"], len(SPLITS))
                ffn_transposes(0)
                ffn_up(0)
                for q in range(1, QUARTERS):
                    ffn_transposes(q)
                    ffn_up(q)
                    ffn_down(q - 1)
                ffn_down(3)


def kernel(**inputs):
    import numpy as np
    import concourse.bacc as bacc
    from concourse.bass_utils import run_bass_kernel_spmd

    a = {k: np.asarray(v) for k, v in inputs.items()}
    qkv_w, qkv_b = a["L0_attn_qkv_w"], a["L0_attn_qkv_b"]
    pos = a["L0_attn_pos_bias"]
    f32 = np.float32

    def by_group(w):
        return w.reshape(w.shape[:-1] + (4, 4, 8)).swapaxes(-1, -2).reshape(w.shape)

    w_tok = np.concatenate([qkv_w.reshape(128, 3, 4, 4, 8).transpose(0, 3, 1, 2, 4).reshape(128, 384),
                            by_group(a["L0_attn_gate_w"])], axis=1)
    row = np.concatenate([qkv_b.reshape(3, 4, 4, 8).transpose(2, 0, 1, 3).reshape(384), by_group(a["L0_attn_gate_b"]),
                          a["L0_ffn_router_bias"], a["L0_attn_out_b"], a["L0_attn_fc2_b"]])[None, :]
    gub = a["L0_ffn_gate_up_bias"].reshape(8, 2, 128).transpose(2, 0, 1).reshape(128, 16)
    cols = np.stack([a["L0_attn_ln1_g"], a["L0_attn_ln1_b"], a["L0_attn_ln2_g"], a["L0_attn_ln2_b"],
                     qkv_b[0:128], qkv_b[128:256]], axis=1)
    cols = np.concatenate([cols, gub, a["L0_attn_fc1_b"].reshape(4, 128).T], axis=1)
    band = np.full((HEADS, 96), CLOSED, f32)
    band[:, 31:64] = pos[32::-1, :].T
    far = np.broadcast_to(pos[33:38].reshape(NFAR, 4, 4).transpose(2, 0, 1).reshape(4, 1, NFAR * 4),
                          (4, 32, NFAR * 4)).reshape(128, NFAR * 4)
    p = np.arange(128)
    anti = (p[:, None] // 32 * 32 + 31 - p[:, None] % 32 == p[None, :]).astype(f32)
    headmask = (p[:, None] % 32 // 8 == np.arange(4)[None, :]).astype(f32)
    before = (np.arange(8)[None, :] < np.arange(8)[:, None]).astype(f32).reshape(1, 64)
    onehot = (np.arange(40)[:, None] % 32 == np.arange(8)[None, :]).astype(f32)
    arrays = {
        "x": a["L0_attn_x"].reshape(TOKENS, D), "ident": np.eye(128, dtype=f32), "anti": anti, "headmask": headmask,
        "before": before, "onehot": onehot, "cols": cols, "row": row, "far_bias": far, "band": band, "w_tok": w_tok,
        "w_qk_router": np.concatenate([qkv_w[:, 0:256], a["L0_ffn_router_weight"].T], axis=1),
        "gate_up": a["L0_ffn_gate_up_proj"].transpose(1, 0, 2).reshape(128, 2048), "down": a["L0_ffn_down_proj"],
        "down_bias": a["L0_ffn_down_bias"], "fc1": a["L0_attn_fc1_w"], "fc2": a["L0_attn_fc2_w"],
        "out_w": by_group(a["L0_attn_out_w"].T).T,
    }
    arrays = {"in_" + k: np.ascontiguousarray(v) for k, v in arrays.items()}

    nc = bacc.Bacc("TRN2", target_bir_lowering=False, num_devices=1)
    aps = [nc.dram_tensor(k, v.shape, mybir.dt.from_np(v.dtype), kind="ExternalInput").ap() for k, v in arrays.items()]
    y = nc.dram_tensor("y", (TOKENS, D), mybir.dt.float32, kind="ExternalOutput").ap()
    build(nc, *aps, y)
    r = run_bass_kernel_spmd(nc, [arrays], core_ids=[0])
    return r.results[0]["y"].reshape(1, TOKENS, D)
```

```python
import concourse.bass as bass
from concourse import mybir
from contextlib import ExitStack

TOKENS, D = 2048, 128
TILES = TOKENS // 128
QUARTERS, QT = 4, 4
HEADS, HD = 16, 8
HG = HEADS // 4
WINDOW = 64
FF, EXPERTS, INNER = 512, 8, 128
FC = FF // 128
EPS = 1e-5
CLOSED = -1e30
FAR = (48, 64, 96, 128, 192)
NFAR = len(FAR)
LIMIT, ALPHA = 7.0, 1.702
STEPS = 32
C_G1, C_B1, C_G2, C_B2, C_BQ, C_BK, C_GU, C_F1 = 0, 1, 2, 3, 4, 5, 6, 22
N_COLS = C_F1 + FC
R_TOK, R_ROUTER, R_OUT, R_FC2 = 0, 512, 520, 648
N_ROW = 776


def shifted_pieces(n, first_tile):
    a, back = n % 4, n // 4
    out = []
    if a < 4:
        out.append((a, 4, 0, back))
    if a:
        out.append((0, a, 4 - a, back + 1))
    return [(g0, g1, s0, b, max(0, b - first_tile)) for g0, g1, s0, b in out]


def build(nc, x, ident, anti, headmask, before, onehot, cols, row, far_bias, band, w_tok, w_qk_router,
          gate_up, down, down_bias, fc1, fc2, out_w, out):
    fp32, fp32r = mybir.dt.float32, mybir.dt.float32r
    ALU, ACT, AX = mybir.AluOpType, mybir.ActivationFunctionType, mybir.AxisListType

    qkv_dram = nc.dram_tensor("qkv_scratch", (3, 4, 32, 4, TILES, 32), fp32, kind="Internal").ap()
    far_dram = nc.dram_tensor("far_scratch", (QUARTERS, 4, 4, 32, QT * 36), fp32, kind="Internal").ap()

    with ExitStack() as ctx:
        def sb(name, shape, dt=fp32):
            return ctx.enter_context(nc.sbuf_tensor(name, shape, dt))

        def sem(name):
            return ctx.enter_context(nc.semaphore(name))

        x_sb = sb("x_sb", [128, TILES, D])
        xn0 = sb("xn0", [128, TILES, D])
        gate = sb("gate", [128, TILES, D])
        xt_hi = sb("xt_hi", [128, TOKENS], fp32r)
        xt_lo = sb("xt_lo", [128, TOKENS], fp32r)
        xf = sb("xf", [128, 2, 512])
        xn_parts = sb("xn_parts", [128, 4, 512], fp32r)
        xn_hi, xn_lo = xn_parts[:, 0:2, :], xn_parts[:, 2:4, :]
        stats = sb("stats", [128, TILES, 6])
        mv = sb("mv", [128, TILES, 2])
        sd = sb("sd", [128, 2, TILES])
        rs = sb("rs", [128, 4, TILES])
        ident_sb = sb("ident_sb", [128, 128])
        anti_sb = sb("anti_sb", [128, 128], fp32r)
        headmask_sb = sb("headmask_sb", [128, 4])
        before_sb = sb("before_sb", [128, EXPERTS * EXPERTS])
        onehot_raw = sb("onehot_raw", [40, EXPERTS])
        onehot_sb = sb("onehot_sb", [40, EXPERTS, 128], fp32r)
        cols_sb = sb("cols_sb", [128, N_COLS])
        up_bias1 = sb("up_bias1", [128, EXPERTS])
        bias_row = sb("bias_row", [40, N_ROW], fp32r)
        ones = sb("ones", [40, 128], fp32r)
        far_bias_sb = sb("far_bias_sb", [128, NFAR, HG])
        band_hi = sb("band_hi", [128, HG, WINDOW], fp32r)
        band_lo = sb("band_lo", [128, HG, WINDOW], fp32r)
        band0_hi = sb("band0_hi", [128, HG, WINDOW], fp32r)
        stage = sb("stage", [128, 2, 512])
        wtok_hi = sb("wtok_hi", [128, 512], fp32r)
        wtok_lo = sb("wtok_lo", [128, 512], fp32r)
        wqk_hi = sb("wqk_hi", [128, 264], fp32r)
        wqk_lo = sb("wqk_lo", [128, 264], fp32r)
        gu_hi = sb("gu_hi", [128, EXPERTS, 2 * INNER], fp32r)
        gu_lo = sb("gu_lo", [128, EXPERTS, 2 * INNER], fp32r)
        fc1_hi, fc1_lo = wtok_hi, wtok_lo
        fc2_sb = sb("fc2_sb", [128, FC, D])
        outw_sb = sb("outw_sb", [128, D])
        down_sb = sb("down_sb", [128, EXPERTS, D])
        db_raw = sb("db_raw", [EXPERTS, D])
        db3 = sb("db3", [72, D], fp32r)
        w3 = xn_parts[0:72, :, :].rearrange("p b n -> p (b n)")
        logit = sb("logit", [128, TILES, EXPERTS])
        logit_m = sb("logit_m", [128, 4, TILES])
        tok = sb("tok", [128, 3, 4, QT, 32])
        hg_q = sb("hg_q", [128, 2, 4 * QT, 32])
        hg_kv = sb("hg_kv", [128, 2, 4, TILES, 32])
        kv48 = sb("kv48", [128, 2, 2, 4 * QT, 32])
        qt = sb("qt", [128, TOKENS])
        kt = sb("kt", [128, 32 + TOKENS])
        qm = sb("qm", [128, 2, 8, 4, 32])
        vbd = sb("vbd", [128, 2, 4 * QT, 32, 4])
        prob = sb("prob", [128, 2, 8, WINDOW])
        prob_t = sb("prob_t", [128, 2, 8, WINDOW])
        mnear = sb("mnear", [128, 2, 8])
        mall = sb("mall", [128, 2, 4, QT, HG])
        lsum = sb("lsum", [128, 2, 4, QT, HG])
        sfar = sb("sfar", [128, 2, NFAR, 4 * QT * HG])
        mfar = sb("mfar", [128, 2, 4, QT, HG])
        lfar = sb("lfar", [128, 2, 4 * QT * HG])
        prod = sb("prod", [128, 4 * QT * 32])
        tree = sb("tree", [128, 4 * QT * 16])
        ofar = sb("ofar", [128, 2, 4 * QT, 36])
        ofar_tok = sb("ofar_tok", [128, 4, QT, 36])
        tok_flat = tok[:].rearrange("p w j t x -> p (w j t x)")
        onear = tok_flat[:, 0:1024].rearrange("p (b n) -> p b n", b=2)
        mix = tok_flat[:, 1024:1536].rearrange("p (t x j) -> p t x j", t=QT, j=4)
        mix_t = xf[:, 0, :]
        g_act = sb("g_act", [128, 2, 512])
        u_act = sb("u_act", [128, 2, 512])
        th_act = sb("th_act", [128, 2, 512])
        rank_a = th_act[:].rearrange("p b n -> p (b n)")
        rank_b = u_act[:].rearrange("p b n -> p (b n)")
        row_raw = g_act[:].rearrange("p b n -> p (b n)")[0:1, 0:N_ROW]
        raw_w = [stage[:, 0, :], stage[:, 1, :]] + [
            t[:, b].rearrange("p s w -> p (s w)") for t in (prob, prob_t) for b in range(2)] + [stage[:, 0, :]]
        anti_raw = u_act[:, 0, 0:128]
        band_raw = u_act[:, 1, 0:HG * WINDOW].rearrange("p (h w) -> p h w", h=HG)
        hid = vbd[:, :, :, :, :].rearrange("p b s x j -> p b (s x j)").rearrange("p b (f n) -> p b f n", f=FC)

        bank = [ctx.enter_context(nc.psum_tensor(f"bank{i}", [128, 512], fp32)) for i in range(8)]

        x_in = [sem(f"x_in{q}") for q in range(QUARTERS)]
        small_in, mat_in = sem("small_in"), sem("mat_in")
        first_in = sem("first_in")
        w_in = [sem(f"w_in{s}") for s in range(7)]
        qkv_out = [sem(f"qkv_out{q}") for q in range(QUARTERS)]
        hg_in = [sem(f"hg_in{q}") for q in range(QUARTERS)]
        k48_in = [sem(f"k48_in{q}") for q in range(QUARTERS)]
        v48_in = [sem(f"v48_in{q}") for q in range(QUARTERS)]
        far_out = [sem(f"far_out{q}") for q in range(QUARTERS)]
        far_in = [sem(f"far_in{q}") for q in range(QUARTERS)]
        stored = sem("stored")
        names = ("stats_done aggr_done sd_done dve_chain normed x_tr h_tr x_hi x_lo xf_done h_hi h_lo logits_ps "
                 "qk_ps qt_done kt_done tok_ps tok_done gate_pre gate_tanh gate_done split_done consts_done "
                 "zeroed pool_chain logit_sh logit_exp weights_done w_tr w_hi w_lo "
                 "w_hi2 db_done db_hi vbd_done qm_done sfar_done far_sh far_exp mfar_done score_ps near_max "
                 "near_exp sum_done probt_done gate_ps up_ps wrep_ps g_raw u_raw g_half u_clip g_tanh "
                 "glu_done gu_done act_done acc_ps acc_done o_ps o_done lfar_done inv_done ofar_done o_tr mix1 "
                 "bias_done var1_done mix2 mix_done mix_tr mixt_done attn_ps x1_done base_done fc1_ps hid_done fc2_ps "
                 "y_done h2_tr h2_aff h2_hi h2_lo stats2 mall_done normed2 w3_zeroed down_ps o_pv").split()
        S = {n: sem(n) for n in names}

        SPLITS = ([(wtok_hi, wtok_lo, 0, 512), (wqk_hi, wqk_lo, 0, 264)]
                  + [(gu_hi, gu_lo, 512 * i, 512) for i in range(4)] + [(fc1_hi, fc1_lo, 0, 512)])
        SPLIT_SRC = [w_tok, w_qk_router] + [gate_up[:, 512 * i:512 * i + 512] for i in range(4)] + [fc1]
        N_GU = 3

        def flat2(t):
            ap = t[:]
            return ap.rearrange("p e n -> p (e n)") if len(t.shape) == 3 else ap

        FAR_SHIFT = (0, 2, 3, 4, 6)
        W_BANK = (7, 5, 0, 1)
        N_SMALL = 16 * 10
        N_MAT = 16 * 3

        with nc.Block() as block:

            @block.sync
            def _(sp):
                xv = x.rearrange("(t p) c -> p t c", p=128)

                def load_x(q):
                    sp.dma_start(x_sb[:, QT * q:QT * q + QT, :], xv[:, QT * q:QT * q + QT, :]).then_inc(x_in[q], 16)

                def load_weights(s):
                    sp.dma_start(raw_w[s][:, 0:SPLITS[s][3]], SPLIT_SRC[s]).then_inc(w_in[s], 16)

                load_x(0)
                sp.dma_start(ident_sb[:], ident).then_inc(first_in, 16)
                sp.dma_start(cols_sb[:], cols).then_inc(first_in, 16)
                load_weights(0)
                sp.dma_start(row_raw, row).then_inc(first_in, 16)
                load_weights(1)
                for q in range(1, QUARTERS):
                    load_x(q)
                load_weights(2)
                load_weights(3)
                sp.dma_start(anti_raw, anti).then_inc(small_in, 16)
                for j in range(4):
                    src = bass.AP(tensor=band.tensor, offset=96 * j, ap=[[1, 32], [4 * 96, HG], [1, WINDOW]])
                    sp.dma_start(band_raw[32 * j:32 * j + 32, :, :], src).then_inc(small_in, 16)
                sp.dma_start(onehot_raw[:], onehot).then_inc(small_in, 16)
                sp.dma_start(far_bias_sb[:, :, :].rearrange("p f h -> p (f h)"), far_bias).then_inc(small_in, 16)
                sp.dma_start(headmask_sb[:], headmask).then_inc(small_in, 16)
                sp.dma_start(before_sb[:], before.to_broadcast([128, EXPERTS * EXPERTS])).then_inc(small_in, 16)
                sp.dma_start(db_raw[:], down_bias).then_inc(small_in, 16)
                load_weights(4)
                load_weights(5)

                def before48(q, w):
                    for j in range(4):
                        for half in range(2):
                            n, r0, rs0 = (1, 16, 0) if half else (2, 0, 16)
                            for g0, g1, s0, back, skip in shifted_pieces(n, QT * q):
                                dst = kv48[32 * j + r0:32 * j + r0 + 16, q % 2, w - 1, :, :].rearrange(
                                    "p (g t) x -> p g t x", g=4)[:, g0:g1, skip:QT, :]
                                src = qkv_dram[w, j, rs0:rs0 + 16, s0:s0 + g1 - g0,
                                               QT * q - back + skip:QT * q - back + QT, :]
                                sp.dma_start(dst, src).then_inc(k48_in[q] if w == 1 else v48_in[q], 16)

                def qkv_to_dram(q):
                    sp.wait_ge(S["tok_done"], QT * q + QT)
                    for g in range(4):
                        sp.dma_start(qkv_dram[:, :, :, g, QT * q:QT * q + QT, :].rearrange("w j r t x -> r (w j) (t x)"),
                                     tok[32 * g:32 * g + 32].rearrange("p w j t x -> p (w j) (t x)")
                                     ).then_inc(qkv_out[q], 16)

                def head_groups(q):
                    sp.wait_ge(qkv_out[q], 64)
                    if q >= 2:
                        sp.wait_ge(S["sfar_done"], q - 1)
                    tiles = slice(QT * q, QT * q + QT)
                    for w in range(3):
                        dst = (hg_kv[:, w - 1, :, tiles, :] if w else
                               hg_q[:, q % 2, :, :].rearrange("p (g t) x -> p g t x", g=4))
                        sp.dma_start(dst.rearrange("p g t x -> p g (t x)"),
                                     qkv_dram[w, :, :, :, tiles, :].rearrange("j r g t x -> (j r) g (t x)")
                                     ).then_inc(hg_in[q], 16)

                qkv_to_dram(0)
                head_groups(0)
                sp.wait_ge(S["zeroed"], 1)
                before48(0, 1)
                qkv_to_dram(1)
                head_groups(1)
                sp.dma_start(down_sb[:], down.rearrange("e i h -> i e h")).then_inc(mat_in, 16)
                sp.dma_start(outw_sb[:], out_w).then_inc(mat_in, 16)
                sp.dma_start(fc2_sb[:], fc2.rearrange("(f p) n -> p f n", p=128)).then_inc(mat_in, 16)
                qkv_to_dram(2)
                sp.wait_ge(S["split_done"], 1)
                load_weights(6)
                before48(1, 1)
                qkv_to_dram(3)
                before48(0, 2)
                head_groups(2)
                before48(2, 1)
                before48(1, 2)
                head_groups(3)
                before48(3, 1)

                for q in range(QUARTERS):
                    sp.wait_ge(S["ofar_done"], q + 1)
                    sp.wait_ge(S["inv_done"], q + 1)
                    for j in range(4):
                        sp.dma_start(far_dram[q, j].rearrange("g r n -> r g n"),
                                     ofar[32 * j:32 * j + 32, q % 2, :, :].rearrange("p (g t) x -> p g (t x)", g=4)
                                     ).then_inc(far_out[q], 16)
                    sp.wait_ge(far_out[q], 64)
                    if q >= 1:
                        sp.wait_ge(S["mix2"], q)
                    sp.dma_start(ofar_tok[:].rearrange("p j t x -> p j (t x)"),
                                 far_dram[q].rearrange("j g r n -> (g r) j n")).then_inc(far_in[q], 16)
                    if q + 2 < QUARTERS:
                        before48(q + 2, 2)

                ov = out.rearrange("(t p) c -> p t c", p=128)
                for q in range(QUARTERS):
                    sp.wait_ge(S["y_done"], q + 1)
                    sp.dma_start(ov[:, QT * q:QT * q + QT, :], x_sb[:, QT * q:QT * q + QT, :]).then_inc(stored, 16)
                sp.wait_ge(stored, 16 * QUARTERS)

            def total48(q):
                return 16 * sum(4 * len(shifted_pieces(n, QT * q)) for n in (1, 2))

            @block.gpsimd
            def _(pool):
                P = nc.gpsimd
                chain = [0]

                def link(ins):
                    chain[0] += 1
                    ins.then_inc(S["pool_chain"], 1)
                    pool.wait_ge(S["pool_chain"], chain[0])

                link(P.memset(kv48[:, 0, :, :, :], 0.0))
                P.memset(bias_row[:].bitcast(fp32), 0.0)
                P.memset(ones[:].bitcast(fp32), 1.0)
                link(P.memset(kt[:, 0:32], 0.0))
                P.memset(db3[:].bitcast(fp32), 0.0)
                P.memset(prod[:], 0.0)
                P.memset(ofar[:, 0, :, :], 0.0)
                P.memset(vbd[:], 0.0).then_inc(S["zeroed"], 1)

                def split(s):
                    hi, lo, at, n = SPLITS[s]
                    raw = raw_w[s][:, 0:n]
                    pool.wait_ge(w_in[s], 16)
                    if s <= 1:
                        link(P.tensor_scalar(raw[:, 0:128], raw[:, 0:128], HD ** -0.5, None, ALU.mult))
                    link(P.tensor_copy(flat2(hi)[:, at:at + n], raw))
                    P.tensor_tensor(flat2(lo)[:, at:at + n], raw, flat2(hi)[:, at:at + n].bitcast(fp32),
                                    ALU.subtract).then_inc(S["split_done"], 1)

                pool.wait_ge(first_in, 48)
                P.tensor_scalar(cols_sb[:, C_BQ:C_BQ + 1], cols_sb[:, C_BQ:C_BQ + 1], HD ** -0.5, None, ALU.mult)
                link(P.tensor_scalar(row_raw[:, 0:128], row_raw[:, 0:128], HD ** -0.5, None, ALU.mult))
                link(P.tensor_copy(bias_row[0:1, :], row_raw))
                P.tensor_tensor(bias_row[32:33, :], row_raw, bias_row[0:1, :].bitcast(fp32), ALU.subtract
                                ).then_inc(S["bias_done"], 1)
                pool.wait_ge(S["bias_done"], 1)
                split(0)
                split(1)
                pool.wait_ge(small_in, N_SMALL)
                P.tensor_scalar(up_bias1[:], cols_sb[:, C_GU:C_GU + 16].rearrange("p (e h) -> p e h", h=2)[:, :, 1],
                                1.0, None, ALU.add)
                P.tensor_copy(anti_sb[:], anti_raw)
                P.tensor_copy(onehot_sb[:], onehot_raw[:].unsqueeze(2).to_broadcast([40, EXPERTS, 128]))
                link(P.tensor_copy(band_hi[:], band_raw))
                P.tensor_tensor(band_lo[:], band_raw, band_hi[:].bitcast(fp32), ALU.subtract)
                link(P.tensor_copy(band0_hi[:, :, 32:], band_raw[:, :, 32:]))
                P.memset(band0_hi[:, :, 0:32].bitcast(fp32), CLOSED).then_inc(S["consts_done"], 1)
                for s in range(2, len(SPLITS) - 1):
                    split(s)

                def far_scores(q):
                    pool.wait_ge(hg_in[q], 48)
                    if q >= 2:
                        pool.wait_ge(S["inv_done"], q - 1)
                    pv = prod[:].rearrange("p (g t x) -> p g t x", g=4, t=QT)
                    qv = hg_q[:, q % 2, :, :].rearrange("p (g t) x -> p g t x", g=4)
                    for f, n in list(enumerate(FAR_SHIFT))[::-1]:
                        if f == 0:
                            pool.wait_ge(k48_in[q], total48(q))
                            last = P.tensor_tensor(pv, qv,
                                                   kv48[:, q % 2, 0, :, :].rearrange("p (g t) x -> p g t x", g=4),
                                                   ALU.mult)
                        else:
                            for g0, g1, s0, back, skip in shifted_pieces(n, QT * q):
                                t0 = QT * q - back
                                if skip >= QT:
                                    continue
                                last = P.tensor_tensor(pv[:, g0:g1, skip:QT, :],
                                                       qv[:, g0:g1, skip:QT, :],
                                                       hg_kv[:, 0, s0:s0 + g1 - g0, t0 + skip:t0 + QT, :], ALU.mult)
                        link(last)
                        p8 = prod[:].rearrange("p (n d) -> p n d", d=HD)
                        t4 = tree[:].rearrange("p (n d) -> p n d", d=4)
                        link(P.tensor_tensor(t4, p8[:, :, 0:4], p8[:, :, 4:8], ALU.add))
                        link(P.tensor_tensor(t4[:, :, 0:2], t4[:, :, 0:2], t4[:, :, 2:4], ALU.add))
                        link(P.tensor_tensor(sfar[:, q % 2, f, :], t4[:, :, 0], t4[:, :, 1], ALU.add))
                        s3 = sfar[:, q % 2, f, :].rearrange("p (s h) -> p s h", h=HG)
                        last = P.tensor_tensor(s3, s3, far_bias_sb[:, f, :].unsqueeze(1).to_broadcast(
                            [128, 4 * QT, HG]), ALU.add)
                        if q == 0:
                            link(last)
                            s4 = sfar[:, 0, f, :].rearrange("p (g t h) -> p g t h", g=4, t=QT)
                            if f == 0:
                                link(P.memset(s4[:, 0, 0, :], CLOSED))
                                for j in range(4):
                                    last = P.memset(s4[32 * j:32 * j + 16, 1, 0, :], CLOSED)
                                    if j < 3:
                                        link(last)
                            else:
                                full, part = n // 4, n % 4
                                if full:
                                    last = P.memset(s4[:, :, 0:full, :], CLOSED)
                                if part:
                                    last = P.memset(s4[:, 0:part, full, :], CLOSED)
                    last.then_inc(S["sfar_done"], 1)

                def far_output(q):
                    pool.wait_ge(S["mall_done"], 8 * q + 8)
                    P.tensor_tensor(sfar[:, q % 2, :, :], sfar[:, q % 2, :, :],
                                    mall[:, q % 2].rearrange("p g t h -> p (g t h)").unsqueeze(1).to_broadcast(
                                        [128, NFAR, 4 * QT * HG]), ALU.add).then_inc(S["far_sh"], 1)
                    pool.wait_ge(S["far_exp"], q + 1)
                    if q >= 2:
                        pool.wait_ge(far_out[q - 2], 64)
                    ov = ofar[:, q % 2, :, 0:32].rearrange("p (g t) x -> p g t x", g=4)
                    pv = prod[:].rearrange("p (g t x) -> p g t x", g=4, t=QT)
                    for f, n in enumerate(FAR_SHIFT):
                        pf = sfar[:, q % 2, f, :].rearrange("p (g n) -> p g n", g=4)
                        if f == 0:
                            pool.wait_ge(v48_in[q], total48(q))
                            a = pf.unsqueeze(3).to_broadcast([128, 4, QT * HG, HD])
                            b = kv48[:, q % 2, 1, :, :].rearrange("p (g t) (h d) -> p g (t h) d", g=4, d=HD)
                            o = ofar[:, q % 2, :, 0:32].rearrange("p s (h d) -> p s h d", d=HD)
                            link(P.tensor_tensor(
                                o, sfar[:, q % 2, 0, :].rearrange("p (s h) -> p s h", h=HG).unsqueeze(3).to_broadcast(
                                    [128, 4 * QT, HG, HD]),
                                kv48[:, q % 2, 1, :, :].rearrange("p s (h d) -> p s h d", d=HD), ALU.mult))
                            continue
                        pieces = [p for p in shifted_pieces(n, QT * q) if p[4] < QT]
                        for g0, g1, s0, back, skip in pieces:
                            t0 = QT * q - back
                            last = P.tensor_tensor(
                                pv[:, g0:g1, skip:QT, :].rearrange("p g t (h d) -> p g (t h) d", d=HD),
                                pf[:, g0:g1, skip * HG:].unsqueeze(3).to_broadcast(
                                    [128, g1 - g0, (QT - skip) * HG, HD]),
                                hg_kv[:, 1, s0:s0 + g1 - g0, t0 + skip:t0 + QT, :].rearrange(
                                    "p g t (h d) -> p g (t h) d", d=HD), ALU.mult)
                        link(last)
                        for g0, g1, s0, back, skip in pieces:
                            last = P.tensor_tensor(ov[:, g0:g1, skip:QT, :], ov[:, g0:g1, skip:QT, :],
                                                   pv[:, g0:g1, skip:QT, :], ALU.add)
                        if f < NFAR - 1:
                            link(last)
                        else:
                            last.then_inc(S["ofar_done"], 1)
                            pool.wait_ge(S["ofar_done"], q + 1)

                far_scores(0)
                pool.wait_ge(S["tok_ps"], TILES)
                pool.wait_ge(S["sfar_done"], 1)
                P.memset(w3.bitcast(fp32), 0.0).then_inc(S["w3_zeroed"], 1)
                pool.wait_ge(S["gate_tanh"], QUARTERS)
                P.tensor_scalar(gate[:], gate[:], 0.5, 0.5, ALU.mult, ALU.add).then_inc(S["gate_done"], 1)
                far_scores(1)
                split(len(SPLITS) - 1)
                far_output(0)
                far_scores(2)
                far_output(1)
                far_scores(3)
                far_output(2)

                def base(q):
                    pool.wait_ge(S["x1_done"], q + 1)
                    pool.wait_ge(S["acc_done"], q + 1)
                    t = slice(QT * q, QT * q + QT)
                    P.tensor_tensor(x_sb[:, t, :], x_sb[:, t, :], xn0[:, t, :], ALU.add).then_inc(S["base_done"], 1)

                base(0)
                base(1)
                far_output(3)
                base(2)
                base(3)

            @block.scalar
            def _(act):
                A = nc.scalar

                def col(c):
                    return cols_sb[:, c:c + 1]

                def first_sqrt(part):
                    t = slice(0, QT) if part == 0 else slice(QT, TILES)
                    act.wait_ge(S["aggr_done"], part + 1)
                    A.activation(sd[:, 0, t], mv[:, t, 1], ACT.Sqrt, bias=EPS).then_inc(S["sd_done"], 1)

                def second_sqrt(part):
                    t = slice(0, QT) if part == 0 else slice(QT, TILES)
                    act.wait_ge(S["var1_done"], part + 1)
                    A.activation(sd[:, 1, t], rs[:, 1, t], ACT.Sqrt, bias=EPS).then_inc(S["sd_done"], 1)

                def x_high(q):
                    act.wait_ge(S["x_tr"], q + 1)
                    A.copy(xt_hi[:, 512 * q:512 * q + 512], bank[0][:]).then_inc(S["x_hi"], 1)

                def h_high(q):
                    act.wait_ge(S["xf_done"], q + 1)
                    if q >= 2:
                        act.wait_ge(S["tok_ps"], QT * (q - 1))
                    A.copy(xn_hi[:, q % 2, :], xf[:, q % 2, :]).then_inc(S["h_hi"], 1)

                def q_and_k(q):
                    if q == 0:
                        act.wait_ge(S["bias_done"], 1)
                        act.wait_ge(S["zeroed"], 1)
                    act.wait_ge(S["qk_ps"], 2 * q + 1)
                    A.activation(qt[:, 512 * q:512 * q + 512], bank[2][:], ACT.Identity, bias=col(C_BQ)
                                 ).then_inc(S["qt_done"], 1)
                    act.wait_ge(S["qk_ps"], 2 * q + 2)
                    A.activation(kt[:, 32 + 512 * q:32 + 512 * q + 512], bank[3][:], ACT.Identity,
                                 bias=col(C_BK)).then_inc(S["kt_done"], 1)

                def tokens(t):
                    if t % QT == 0 and t > 0:
                        act.wait_ge(qkv_out[t // QT - 1], 64)
                    act.wait_ge(S["tok_ps"], t + 1)
                    A.copy(tok[:, :, :, t % QT, :].rearrange("p w j x -> p (w j) x"),
                           bank[4 + t % 2][:, 0:384].rearrange("p (a x) -> p a x", x=32)).then_inc(S["tok_done"], 1)
                    A.copy(gate[:, t, :], bank[4 + t % 2][:, 384:512]).then_inc(S["gate_pre"], 1)

                first_sqrt(0)
                second_sqrt(0)
                x_high(0)
                first_sqrt(1)
                h_high(0)
                second_sqrt(1)
                for q in range(QUARTERS):
                    q_and_k(q)
                    if q + 1 < QUARTERS:
                        x_high(q + 1)
                    tokens(QT * q)
                    tokens(QT * q + 1)
                    if q + 1 < QUARTERS:
                        h_high(q + 1)
                    tokens(QT * q + 2)
                    tokens(QT * q + 3)
                act.wait_ge(S["logit_sh"], 1)
                A.activation(logit[:], logit[:], ACT.Exp).then_inc(S["logit_exp"], 1)
                for q in range(QUARTERS):
                    act.wait_ge(S["gate_pre"], QT * q + QT)
                    t = slice(QT * q, QT * q + QT)
                    A.activation(gate[:, t, :], gate[:, t, :], ACT.Tanh, scale=0.5).then_inc(S["gate_tanh"], 1)
                act.wait_ge(small_in, N_SMALL)
                act.wait_ge(S["zeroed"], 1)
                A.copy(db3[0:8, :], db_raw[:])
                A.copy(db3[32:40, :], db_raw[:]).then_inc(S["db_hi"], 1)
                act.wait_ge(S["w3_zeroed"], 1)
                for q in range(QUARTERS):
                    ts = slice(512 * q, 512 * q + 512)
                    act.wait_ge(S["w_tr"], q + 1)
                    A.copy(w3[0:8, ts], bank[W_BANK[q]][0:8, :])
                    A.copy(w3[64:72, ts], bank[W_BANK[q]][0:8, :]).then_inc(S["w_hi"], 1)

                def masked_q(c, j):
                    if c >= 2 and j == 0:
                        act.wait_ge(S["score_ps"], 4 * (c - 1))
                    A.activation(qm[:, c % 2, :, j, :],
                                 qt[:, 256 * c:256 * c + 256].rearrange("p (s r) -> p s r", r=32),
                                 ACT.Copy, scale=headmask_sb[:, j:j + 1]).then_inc(S["qm_done"], 1)

                def v_block(q, j):
                    if j == 0:
                        act.wait_ge(hg_in[q], 48)
                        if q >= 2:
                            act.wait_ge(S["o_pv"], 8 * (q - 1) + 4)
                    A.copy(vbd[32 * j:32 * j + 32, q % 2, :, :, j].rearrange("p (g t) x -> p g (t x)", g=4),
                           hg_kv[32 * j:32 * j + 32, 1, :, QT * q:QT * q + QT, :].rearrange(
                               "p g t x -> p g (t x)")).then_inc(S["vbd_done"], 1)

                def near_out(c):
                    act.wait_ge(S["o_pv"], 4 * c + 4)
                    if c == 0:
                        act.wait_ge(qkv_out[QUARTERS - 1], 64)
                    if c >= 4 and c % 2 == 0:
                        act.wait_ge(S["o_tr"], c // 2 - 1)
                    A.copy(onear[:, (c // 2) % 2, 256 * (c % 2):256 * (c % 2) + 256], bank[2][:, 0:256]
                           ).then_inc(S["o_done"], 1)

                def far_weights(q):
                    act.wait_ge(S["far_sh"], q + 1)
                    A.activation(sfar[:, q % 2, :, :], sfar[:, q % 2, :, :], ACT.Exp).then_inc(S["far_exp"], 1)

                def near_weights(i):
                    c, h = i // 4, i % 4
                    act.wait_ge(S["mall_done"], i + 1)
                    if i == 0:
                        act.wait_ge(S["split_done"], 6)
                    if i >= 2:
                        act.wait_ge(S["probt_done"], i - 1)
                    for s in range(8):
                        least = mall[:, (c // 2) % 2, s % 4, 2 * (c % 2) + s // 4, h:h + 1]
                        last = A.activation(prob[:, i % 2, s, :], bank[i % 2][:, WINDOW * s:WINDOW * s + WINDOW],
                                            ACT.Exp, bias=least)
                    last.then_inc(S["near_exp"], 1)

                def mix_evac(q):
                    act.wait_ge(S["mix_tr"], q + 1)
                    A.copy(mix_t, bank[7][:]).then_inc(S["mixt_done"], 1)

                act.wait_ge(S["qt_done"], QUARTERS)
                act.wait_ge(small_in, N_SMALL)
                for j in range(4):
                    masked_q(0, j)
                masked_q(1, 0)
                for j in range(4):
                    v_block(0, j)
                for i in range(STEPS + 1):
                    if i >= 1:
                        act.wait_ge(S["g_half"], i)
                        A.activation(th_act[:, (i - 1) % 2, :], g_act[:, (i - 1) % 2, :], ACT.Tanh, scale=ALPHA
                                     ).then_inc(S["g_tanh"], 1)
                    if i < STEPS:
                        near_weights(i)
                        e = i % EXPERTS
                        act.wait_ge(S["gate_ps"], i + 1)
                        if i >= 2:
                            act.wait_ge(S["glu_done"], i - 1)
                        A.activation(g_act[:, i % 2, :], bank[3][:], ACT.Identity,
                                     bias=col(C_GU + 2 * e)).then_inc(S["g_raw"], 1)
                        act.wait_ge(S["up_ps"], i + 1)
                        if i >= 2:
                            act.wait_ge(S["down_ps"], i - 1)
                        A.activation(u_act[:, i % 2, :], bank[4][:], ACT.Identity,
                                     bias=up_bias1[:, e:e + 1]).then_inc(S["u_raw"], 1)
                    if i + 5 < STEPS:
                        masked_q((i + 5) // 4, (i + 5) % 4)
                    if i % 4 == 1 and i > 4:
                        near_out(i // 4 - 1)
                    if i % 8 == 2 and i > 8:
                        far_weights(i // 8 - 1)
                    if 5 <= i < 5 + 8 * (QUARTERS - 1) and (i - 5) % 8 < 4:
                        v_block((i - 5) // 8 + 1, (i - 5) % 8)
                    if i % 8 == 7 and i > 8:
                        mix_evac(i // 8 - 1)
                near_out(7)
                far_weights(3)

                def ffn_sqrt(part):
                    t = slice(0, 3 * QT) if part == 0 else slice(3 * QT, TILES)
                    act.wait_ge(S["stats2"], part + 1)
                    A.activation(sd[:, 0, t], mv[:, t, 1], ACT.Sqrt, bias=EPS).then_inc(S["sd_done"], 1)

                def ffn_high(q):
                    act.wait_ge(S["h2_aff"], q + 1)
                    A.copy(xt_hi[:, 512 * q:512 * q + 512], xf[:, q % 2, :]).then_inc(S["h2_hi"], 1)

                def ffn_gelu(q):
                    for f in range(FC):
                        act.wait_ge(S["fc1_ps"], FC * q + f + 1)
                        if q >= 2 and f == 0:
                            act.wait_ge(S["fc2_ps"], q - 1)
                        A.activation(hid[:, q % 2, f, :], bank[2 + f][:], ACT.Gelu,
                                     bias=col(C_F1 + f)).then_inc(S["hid_done"], 1)

                ffn_sqrt(0)
                ffn_high(0)
                ffn_high(1)
                ffn_gelu(0)
                ffn_high(2)
                ffn_gelu(1)
                ffn_gelu(2)
                act.wait_ge(S["h2_lo"], 3)
                mix_evac(3)
                ffn_sqrt(1)
                ffn_high(3)
                ffn_gelu(3)

            @block.vector
            def _(dve):
                V = nc.vector
                chain = [0]

                def link(ins):
                    chain[0] += 1
                    ins.then_inc(S["dve_chain"], 1)
                    dve.wait_ge(S["dve_chain"], chain[0])

                def col(c):
                    return cols_sb[:, c:c + 1]

                def statistics(t0, t1, part):
                    for t in range(t0, t1):
                        if t % QT == 0:
                            dve.wait_ge(x_in[t // QT], 16)
                        last = V.bn_stats(stats[:, t, :], x_sb[:, t, :])
                    last.then_inc(S["stats_done"], 1)
                    dve.wait_ge(S["stats_done"], part + 1)
                    for t in range(t0, t1):
                        last = V.bn_aggr(mv[:, t, :], stats[:, t, :])
                    last.then_inc(S["aggr_done"], 1)

                def scale0(t0, t1, part):
                    t = slice(t0, t1)
                    dve.wait_ge(S["sd_done"], 2 * part + 1)
                    link(V.reciprocal(rs[:, 0, t], sd[:, 0, t]))
                    link(V.tensor_tensor(rs[:, 1, t], mv[:, t, 1], rs[:, 0, t], ALU.mult))
                    V.tensor_tensor(rs[:, 1, t], rs[:, 1, t], rs[:, 0, t], ALU.mult).then_inc(S["var1_done"], 1)

                def scale1(t0, t1, part):
                    t = slice(t0, t1)
                    dve.wait_ge(S["sd_done"], 2 * part + 2)
                    link(V.reciprocal(rs[:, 2, t], sd[:, 1, t]))
                    link(V.tensor_tensor(rs[:, 3, t], rs[:, 2, t], rs[:, 0, t], ALU.mult))

                def normalize0(q):
                    for t in range(QT * q, QT * q + QT):
                        V.tensor_scalar(xn0[:, t, :], x_sb[:, t, :], mv[:, t, 0:1], rs[:, 0, t:t + 1],
                                        ALU.subtract, ALU.mult)

                def normalize1(q):
                    for t in range(QT * q, QT * q + QT):
                        last = V.tensor_scalar(gate[:, t, :], x_sb[:, t, :], mv[:, t, 0:1], rs[:, 3, t:t + 1],
                                               ALU.subtract, ALU.mult)
                    last.then_inc(S["normed"], 1)

                def operands(q):
                    ts = slice(512 * q, 512 * q + 512)
                    dve.wait_ge(S["h_tr"], q + 1)
                    if q >= 2:
                        dve.wait_ge(S["h_lo"], q - 1)
                    V.tensor_scalar(xf[:, q % 2, :], bank[1][:], col(C_G1), col(C_B1), ALU.mult, ALU.add
                                    ).then_inc(S["xf_done"], 1)
                    dve.wait_ge(S["x_hi"], q + 1)
                    V.tensor_tensor(xt_lo[:, ts], bank[0][:], xt_hi[:, ts].bitcast(fp32), ALU.subtract
                                    ).then_inc(S["x_lo"], 1)
                    dve.wait_ge(S["h_hi"], q + 1)
                    if q >= 2:
                        dve.wait_ge(S["tok_ps"], QT * (q - 1))
                    V.tensor_tensor(xn_lo[:, q % 2, :], xf[:, q % 2, :], xn_hi[:, q % 2, :].bitcast(fp32),
                                    ALU.subtract).then_inc(S["h_lo"], 1)

                statistics(0, QT, 0)
                scale0(0, QT, 0)
                normalize0(0)
                scale1(0, QT, 0)
                normalize1(0)
                statistics(QT, TILES, 1)
                dve.wait_ge(first_in, 48)
                operands(0)
                scale0(QT, TILES, 1)
                normalize0(1)
                scale1(QT, TILES, 1)
                normalize1(1)
                normalize0(2)
                normalize1(2)
                operands(1)
                normalize0(3)
                normalize1(3)
                operands(2)
                operands(3)

                dve.wait_ge(S["logits_ps"], 1)
                logits = bank[6][:, 0:TILES * EXPERTS].rearrange("p (t e) -> p t e", e=EXPERTS)
                link(V.tensor_reduce(logit_m[:, 0, :], logits, AX.X, ALU.max))
                V.tensor_tensor(logit[:], logits, logit_m[:, 0, :].unsqueeze(2).to_broadcast(
                    [128, TILES, EXPERTS]), ALU.subtract).then_inc(S["logit_sh"], 1)
                dve.wait_ge(S["logit_exp"], 1)
                dve.wait_ge(S["consts_done"], 1)
                dve.wait_ge(small_in, N_SMALL)
                e4 = logit[:].unsqueeze(3).to_broadcast([128, TILES, EXPERTS, EXPERTS])
                e4t = logit[:].unsqueeze(2).to_broadcast([128, TILES, EXPERTS, EXPERTS])
                equal = rank_a.rearrange("p (t a b) -> p t a b", t=TILES, a=EXPERTS)
                greater = rank_b.rearrange("p (t a b) -> p t a b", t=TILES, a=EXPERTS)
                link(V.tensor_tensor(equal, e4t, e4, ALU.is_equal))
                link(V.tensor_tensor(equal, equal, before_sb[:].rearrange("p (a b) -> p a b", a=EXPERTS).unsqueeze(1)
                                     .to_broadcast([128, TILES, EXPERTS, EXPERTS]), ALU.mult))
                link(V.tensor_tensor(greater, e4t, e4, ALU.is_gt))
                link(V.tensor_tensor(equal, equal, greater, ALU.add))
                link(V.tensor_reduce(logit_m[:, 1, :], logit[:], AX.X, ALU.add))
                link(V.reciprocal(logit_m[:, 2, :], logit_m[:, 1, :]))
                rank = rank_b[:, 0:TILES * EXPERTS]
                link(V.tensor_reduce(rank.rearrange("p (t e) -> p t e", e=EXPERTS),
                                     rank_a.rearrange("p (t a b) -> p t a b", t=TILES, a=EXPERTS), AX.X, ALU.add))
                link(V.tensor_scalar(rank, rank, 2.0, None, ALU.is_lt))
                link(V.tensor_tensor(rank, rank, logit[:].rearrange("p t e -> p (t e)"), ALU.mult))
                V.tensor_tensor(rank_a[:, 0:TILES * EXPERTS].rearrange("p (t e) -> p t e", e=EXPERTS),
                                rank.rearrange("p (t e) -> p t e", e=EXPERTS),
                                logit_m[:, 2, :].unsqueeze(2).to_broadcast([128, TILES, EXPERTS]), ALU.mult
                                ).then_inc(S["normed2"], 1)
                dve.wait_ge(S["db_hi"], 1)
                V.tensor_tensor(db3[64:72, :], db_raw[:], db3[0:8, :].bitcast(fp32), ALU.subtract
                                ).then_inc(S["db_done"], 1)
                for q in range(QUARTERS):
                    ts = slice(512 * q, 512 * q + 512)
                    dve.wait_ge(S["w_hi"], q + 1)
                    V.tensor_tensor(w3[32:40, ts], bank[W_BANK[q]][0:8, :], w3[0:8, ts].bitcast(fp32), ALU.subtract
                                    ).then_inc(S["w_lo"], 1)

                def far_max(q):
                    dve.wait_ge(S["sfar_done"], q + 1)
                    mf = mfar[:, q % 2].rearrange("p g t h -> p (g t h)")
                    link(V.tensor_reduce(mf, sfar[:, q % 2, :, :].rearrange("p f n -> p n f"), AX.X, ALU.max))
                    V.tensor_scalar(mf, mf, -1.0, None, ALU.mult).then_inc(S["mfar_done"], 1)

                def sums_and_transpose(i):
                    c, h = i // 4, i % 4
                    q, tl = c // 2, 2 * (c % 2)
                    dve.wait_ge(S["near_exp"], i + 1)
                    if i >= 2:
                        dve.wait_ge(S["o_pv"], i - 1)
                    V.tensor_reduce(lsum[:, q % 2, :, tl:tl + 2, h].rearrange("p g t -> p t g"),
                                    prob[:, i % 2].rearrange("p (t g) w -> p t g w", t=2), AX.X, ALU.add
                                    ).then_inc(S["sum_done"], 1)
                    V.transpose(prob_t[:, i % 2].rearrange("p s w -> p (s w)"),
                                prob[:, i % 2].rearrange("p s w -> p (s w)")).then_inc(S["probt_done"], 1)

                def expert_out(i):
                    dve.wait_ge(S["g_tanh"], i + 1)
                    V.scalar_tensor_tensor(out=th_act[:, i % 2, :], in0=th_act[:, i % 2, :], scalar=1.0,
                                           in1=g_act[:, i % 2, :], op0=ALU.add, op1=ALU.mult).then_inc(S["glu_done"], 1)
                    dve.wait_ge(S["glu_done"], i + 1)
                    V.tensor_tensor(u_act[:, i % 2, :], th_act[:, i % 2, :], u_act[:, i % 2, :], ALU.mult
                                    ).then_inc(S["gu_done"], 1)
                    dve.wait_ge(S["gu_done"], i + 1)
                    dve.wait_ge(S["wrep_ps"], i + 1)
                    V.tensor_tensor(u_act[:, i % 2, :], u_act[:, i % 2, :], bank[5][:], ALU.mult
                                    ).then_inc(S["act_done"], 1)

                def acc_out(q):
                    dve.wait_ge(S["down_ps"], EXPERTS * (q + 1))
                    t = slice(QT * q, QT * q + QT)
                    V.tensor_tensor(x_sb[:, t, :], x_sb[:, t, :], bank[6][:].rearrange("p (t c) -> p t c", c=D),
                                    ALU.add).then_inc(S["acc_done"], 1)

                def far_sum(q):
                    dve.wait_ge(S["far_exp"], q + 1)
                    if q >= 2:
                        dve.wait_ge(far_out[q - 2], 64)
                    dve.wait_ge(S["sum_done"], 8 * q + 8)
                    link(V.tensor_reduce(lfar[:, q % 2, :], sfar[:, q % 2, :, :].rearrange("p f n -> p n f"),
                                         AX.X, ALU.add))
                    link(V.tensor_tensor(lfar[:, q % 2, :], lfar[:, q % 2, :],
                                         lsum[:, q % 2].rearrange("p g t h -> p (g t h)"), ALU.add))
                    if q == 0:
                        dve.wait_ge(S["zeroed"], 1)
                    V.reciprocal(ofar[:, q % 2, :, 32:36], lfar[:, q % 2, :].rearrange("p (s h) -> p s h", h=HG)
                                 ).then_inc(S["inv_done"], 1)

                def mix_heads(q):
                    t = slice(QT * q, QT * q + QT)
                    dve.wait_ge(far_in[q], 16)
                    dve.wait_ge(S["o_tr"], q + 1)
                    if q >= 1:
                        dve.wait_ge(S["mix_tr"], q)
                    if q == 0:
                        dve.wait_ge(S["gate_done"], 1)
                    V.tensor_tensor(mix, bank[7][:].rearrange("p (t x j) -> p t x j", t=QT, j=4),
                                    ofar_tok[:, :, :, 0:32].rearrange("p j t x -> p t x j"), ALU.add
                                    ).then_inc(S["mix1"], 1)
                    dve.wait_ge(S["mix1"], q + 1)
                    for tt in range(QT):
                        last = V.tensor_tensor(
                            mix[:, tt].rearrange("p (h d) j -> p h d j", d=HD),
                            mix[:, tt].rearrange("p (h d) j -> p h d j", d=HD),
                            ofar_tok[:, :, tt, 32:36].rearrange("p j h -> p h j").unsqueeze(2).to_broadcast(
                                [128, HG, HD, 4]), ALU.mult)
                    last.then_inc(S["mix2"], 1)
                    dve.wait_ge(S["mix2"], q + 1)
                    V.tensor_tensor(mix.rearrange("p t x j -> p t (x j)"), mix.rearrange("p t x j -> p t (x j)"),
                                    gate[:, t, :], ALU.mult).then_inc(S["mix_done"], 1)

                def residual(q):
                    t = slice(QT * q, QT * q + QT)
                    dve.wait_ge(S["attn_ps"], q + 1)
                    V.tensor_tensor(xn0[:, t, :], xn0[:, t, :], bank[7][:].rearrange("p (t c) -> p t c", c=D),
                                    ALU.add).then_inc(S["x1_done"], 1)
                    dve.wait_ge(S["x1_done"], q + 1)
                    for tt in range(QT * q, QT * q + QT):
                        last = V.bn_stats(stats[:, tt, :], xn0[:, tt, :])
                    last.then_inc(S["stats_done"], 1)

                def clips(i):
                    dve.wait_ge(S["g_raw"], i + 1)
                    V.tensor_scalar(g_act[:, i % 2, :], g_act[:, i % 2, :], LIMIT, 0.5, ALU.min, ALU.mult
                                    ).then_inc(S["g_half"], 1)
                    dve.wait_ge(S["u_raw"], i + 1)
                    V.tensor_scalar(u_act[:, i % 2, :], u_act[:, i % 2, :], 1.0 - LIMIT, 1.0 + LIMIT, ALU.max, ALU.min
                                    ).then_inc(S["u_clip"], 1)

                far_max(0)
                dve.wait_ge(S["split_done"], 6)
                for i in range(STEPS):
                    c, h = i // 4, i % 4
                    q, tl = c // 2, 2 * (c % 2)
                    if i >= 1:
                        clips(i - 1)
                    dve.wait_ge(S["score_ps"], i + 1)
                    V.tensor_reduce(mnear[:, i % 2, :], bank[i % 2][:].rearrange("p (s w) -> p s w", w=WINDOW),
                                    AX.X, ALU.max).then_inc(S["near_max"], 1)
                    dve.wait_ge(S["near_max"], i + 1)
                    if i % 8 == 0:
                        dve.wait_ge(S["mfar_done"], q + 1)
                        if q >= 2:
                            dve.wait_ge(S["far_sh"], q - 1)
                    mv_ = mall[:, q % 2, :, tl:tl + 2, h].rearrange("p g t -> p t g")
                    V.scalar_tensor_tensor(out=mv_, in0=mnear[:, i % 2, :].rearrange("p (t g) -> p t g", t=2),
                                           scalar=-1.0, in1=mfar[:, q % 2, :, tl:tl + 2, h].rearrange("p g t -> p t g"),
                                           op0=ALU.mult, op1=ALU.min).then_inc(S["mall_done"], 1)
                    if i >= 1:
                        sums_and_transpose(i - 1)
                        expert_out(i - 1)
                    if i % 8 == 1 and i > 8:
                        acc_out(q - 1)
                    if i % 8 == 3 and i > 8:
                        far_sum(q - 1)
                    if i % 8 == 7 and q + 1 < QUARTERS:
                        far_max(q + 1)
                    if i % 8 == 6 and q >= 1:
                        mix_heads(q - 1)
                    if i % 8 == 1 and q >= 2:
                        residual(q - 2)
                clips(STEPS - 1)
                sums_and_transpose(STEPS - 1)
                expert_out(STEPS - 1)
                acc_out(3)
                far_sum(3)
                residual(2)

                def ffn_statistics(t0, t1, part):
                    dve.wait_ge(S["stats_done"], 2 + t1 // QT)
                    for t in range(t0, t1):
                        last = V.bn_aggr(mv[:, t, :], stats[:, t, :])
                    last.then_inc(S["stats2"], 1)
                    dve.wait_ge(S["sd_done"], 5 + part)
                    link(V.reciprocal(rs[:, 0, t0:t1], sd[:, 0, t0:t1]))

                def ffn_normalize(q):
                    for t in range(QT * q, QT * q + QT):
                        last = V.tensor_scalar(gate[:, t, :], xn0[:, t, :], mv[:, t, 0:1], rs[:, 0, t:t + 1],
                                               ALU.subtract, ALU.mult)
                    last.then_inc(S["normed"], 1)

                def ffn_operands(q):
                    ts = slice(512 * q, 512 * q + 512)
                    dve.wait_ge(S["h2_tr"], q + 1)
                    if q >= 2:
                        dve.wait_ge(S["h2_lo"], q - 1)
                    V.tensor_scalar(xf[:, q % 2, :], bank[q % 2][:], col(C_G2), col(C_B2), ALU.mult, ALU.add
                                    ).then_inc(S["h2_aff"], 1)
                    dve.wait_ge(S["h2_hi"], q + 1)
                    V.tensor_tensor(xt_lo[:, ts], xf[:, q % 2, :], xt_hi[:, ts].bitcast(fp32), ALU.subtract
                                    ).then_inc(S["h2_lo"], 1)

                def ffn_out(q):
                    t = slice(QT * q, QT * q + QT)
                    dve.wait_ge(S["fc2_ps"], q + 1)
                    dve.wait_ge(S["base_done"], q + 1)
                    V.tensor_tensor(x_sb[:, t, :], x_sb[:, t, :], bank[6][:].rearrange("p (t c) -> p t c", c=D),
                                    ALU.add).then_inc(S["y_done"], 1)

                ffn_statistics(0, 3 * QT, 0)
                for q in range(3):
                    ffn_normalize(q)
                ffn_operands(0)
                ffn_operands(1)
                ffn_out(0)
                ffn_operands(2)
                ffn_out(1)
                ffn_out(2)
                mix_heads(3)
                residual(3)
                ffn_statistics(3 * QT, TILES, 1)
                ffn_normalize(3)
                ffn_operands(3)
                ffn_out(3)

            @block.tensor
            def _(pe):
                E = nc.tensor

                def three(out_ap, w_hi, w_lo, m_hi, m_lo, start=True):
                    E.matmul(out_ap, w_hi, m_hi, start=start, stop=False)
                    E.matmul(out_ap, w_lo, m_hi, start=False, stop=False)
                    return E.matmul(out_ap, w_hi, m_lo, start=False, stop=True)

                def transposes(q):
                    pe.wait_ge(S["normed"], q + 1)
                    if q >= 1:
                        pe.wait_ge(S["x_lo"], q)
                        pe.wait_ge(S["xf_done"], q)
                    for tt in range(QT):
                        last = E.transpose(bank[0][:, 128 * tt:128 * tt + 128], xn0[:, QT * q + tt, :], ident_sb[:])
                    last.then_inc(S["x_tr"], 1)
                    for tt in range(QT):
                        last = E.transpose(bank[1][:, 128 * tt:128 * tt + 128], gate[:, QT * q + tt, :], ident_sb[:])
                    last.then_inc(S["h_tr"], 1)

                def add_rows(out_ap, r0, n, times=1):
                    rows = bias_row[0:40, r0:r0 + n]
                    if times > 1:
                        rows = rows.unsqueeze(1).to_broadcast([40, times, n])
                    return E.matmul(out_ap, ones[0:40, :], rows, start=True, stop=False, skip_group_check=True)

                def on(out_ap, w_hi, w_lo, m_hi, m_lo):
                    E.matmul(out_ap, w_hi, m_hi, start=False, stop=False, skip_group_check=True)
                    E.matmul(out_ap, w_lo, m_hi, start=False, stop=False, skip_group_check=True)
                    return E.matmul(out_ap, w_hi, m_lo, start=False, stop=True, skip_group_check=True)

                def project_channels(q):
                    b = q % 2
                    pe.wait_ge(S["x_lo"], q + 1)
                    if q == 0:
                        pe.wait_ge(S["split_done"], 2)
                        pe.wait_ge(S["bias_done"], 1)
                        add_rows(bank[6][:, 0:TILES * EXPERTS].rearrange("p (t e) -> p t e", e=EXPERTS),
                                 R_ROUTER, EXPERTS, TILES)
                    for tt in range(QT):
                        t = QT * q + tt
                        ts = slice(128 * t, 128 * t + 128)
                        last = on(bank[6][:, EXPERTS * t:EXPERTS * t + EXPERTS], xt_hi[:, ts], xt_lo[:, ts],
                                  wqk_hi[:, 256:264], wqk_lo[:, 256:264])
                    if q == QUARTERS - 1:
                        last.then_inc(S["logits_ps"], 1)
                    pe.wait_ge(S["h_lo"], q + 1)
                    for k in range(2):
                        if q >= 1:
                            pe.wait_ge(S["kt_done"] if k else S["qt_done"], q)
                        three(bank[2 + k][:], wqk_hi[:, 128 * k:128 * k + 128], wqk_lo[:, 128 * k:128 * k + 128],
                              xn_hi[:, b, :], xn_lo[:, b, :]).then_inc(S["qk_ps"], 1)

                def project_tokens(q):
                    b = q % 2
                    for tt in range(QT):
                        t = QT * q + tt
                        ts = slice(128 * tt, 128 * tt + 128)
                        if t >= 2:
                            pe.wait_ge(S["gate_pre"], t - 1)
                        add_rows(bank[4 + t % 2][:], R_TOK, 512)
                        on(bank[4 + t % 2][:], xn_hi[:, b, ts], xn_lo[:, b, ts], wtok_hi[:], wtok_lo[:]
                           ).then_inc(S["tok_ps"], 1)

                pe.wait_ge(first_in, 48)
                transposes(0)
                for q in range(QUARTERS):
                    project_channels(q)
                    if q + 1 < QUARTERS:
                        transposes(q + 1)
                    project_tokens(q)

                pe.wait_ge(S["normed2"], 1)
                pe.wait_ge(S["gate_pre"], TILES)
                pe.wait_ge(S["x_lo"], QUARTERS)
                pe.wait_ge(S["xf_done"], QUARTERS)
                for q in range(QUARTERS):
                    for tt in range(QT):
                        t = QT * q + tt
                        last = E.transpose(bank[W_BANK[q]][0:8, 128 * tt:128 * tt + 128],
                                           rank_a[:, EXPERTS * t:EXPERTS * t + EXPERTS], ident_sb[:])
                    last.then_inc(S["w_tr"], 1)

                def scores(i):
                    c, h = i // 4, i % 4
                    b = bank[i % 2]
                    if h == 0:
                        pe.wait_ge(S["qm_done"], 4 * c + 4)
                        pe.wait_ge(S["kt_done"], c // 2 + 1)
                    if i == 0:
                        pe.wait_ge(S["consts_done"], 1)
                        pe.wait_ge(S["w_lo"], QUARTERS)
                        pe.wait_ge(S["zeroed"], 1)
                    if i >= 2:
                        pe.wait_ge(S["near_exp"], i - 1)
                    n0 = 0
                    if c == 0:
                        E.matmul(b[:, 0:WINDOW], anti_sb[:], band0_hi[:, h, :], start=True, stop=False,
                                 skip_group_check=True)
                        E.matmul(b[:, 32:WINDOW], anti_sb[:], band_lo[:, h, 32:], start=False, stop=False,
                                 skip_group_check=True)
                        n0 = 1
                    n = 8 - n0
                    for k, part in enumerate((band_hi, band_lo)):
                        E.matmul(b[:, WINDOW * n0:512].rearrange("p (s w) -> p s w", w=WINDOW), anti_sb[:],
                                 part[:, h, :].unsqueeze(1).to_broadcast([128, n, WINDOW]),
                                 start=(k == 0 and n0 == 0), stop=False, skip_group_check=True)
                    for s in range(8):
                        for j in range(4):
                            last = E.matmul(b[32 * j:32 * j + 32, WINDOW * s:WINDOW * s + WINDOW],
                                            qm[32 * h:32 * h + 32, c % 2, s, j, :],
                                            kt[32 * h:32 * h + 32, 256 * c + 32 * s:256 * c + 32 * s + WINDOW],
                                            start=False, stop=True, skip_group_check=True,
                                            tile_position=(32 * h, 32 * j))
                    last.then_inc(S["score_ps"], 1)

                def weighted_v(i):
                    c, h = i // 4, i % 4
                    if h == 0:
                        pe.wait_ge(S["vbd_done"], 4 * (c // 2) + 4)
                        if c >= 1:
                            pe.wait_ge(S["o_done"], c)
                    pe.wait_ge(S["probt_done"], i + 1)
                    if i == 0:
                        pe.wait_ge(S["qt_done"], QUARTERS)
                    for s in range(8):
                        st = 8 * c + s
                        for half in range(2):
                            kst = st - 1 + half
                            if kst < 0:
                                continue
                            slot, tile, g = (kst // 16) % 2, (kst // 4) % QT, kst % 4
                            last = E.matmul(bank[2][32 * h:32 * h + 32, 32 * s:32 * s + 32],
                                            vbd[:, slot, QT * g + tile, 8 * h:8 * h + 8, :].rearrange("p x j -> p (x j)"),
                                            prob_t[:, i % 2, s, 32 * half:32 * half + 32],
                                            start=(half == 0 or st == 0), stop=(half == 1), skip_group_check=True,
                                            tile_position=(0, 32 * h))
                    last.then_inc(S["o_pv"], 1)

                def experts_in(i):
                    q, e = i // EXPERTS, i % EXPERTS
                    ts = slice(512 * q, 512 * q + 512)
                    if i == 0:
                        pe.wait_ge(S["kt_done"], QUARTERS)
                        pe.wait_ge(S["gate_pre"], TILES)
                    if q == 0 and e % 2 == 0:
                        pe.wait_ge(S["split_done"], N_GU + e // 2)
                    for half, done, b, free in ((0, "gate_ps", 3, "g_raw"), (1, "up_ps", 4, "u_raw")):
                        if i >= 1:
                            pe.wait_ge(S[free], i)
                        ws = slice(INNER * half, INNER * half + INNER)
                        three(bank[b][:], gu_hi[:, e, ws], gu_lo[:, e, ws], xt_hi[:, ts], xt_lo[:, ts]
                              ).then_inc(S[done], 1)

                def weight_rows(i):
                    q, e = i // EXPERTS, i % EXPERTS
                    if i >= 1:
                        pe.wait_ge(S["act_done"], i)
                    E.matmul(bank[5][:], onehot_sb[:, e, :], w3[0:40, 512 * q:512 * q + 512], start=True, stop=True
                             ).then_inc(S["wrep_ps"], 1)

                def experts_out(i):
                    q, e = i // EXPERTS, i % EXPERTS
                    if e == 0:
                        if q == 0:
                            pe.wait_ge(S["db_done"], 1)
                            pe.wait_ge(mat_in, N_MAT)
                            pe.wait_ge(S["logit_sh"], 1)
                        else:
                            pe.wait_ge(S["acc_done"], q)
                        for tt in range(QT):
                            t = QT * q + tt
                            E.matmul(bank[6][:, 128 * tt:128 * tt + 128], w3[:, 128 * t:128 * t + 128], db3[:],
                                     start=(tt == 0), stop=False, skip_group_check=True)
                    pe.wait_ge(S["act_done"], i + 1)
                    for tt in range(QT):
                        last = E.matmul(bank[6][:, 128 * tt:128 * tt + 128], u_act[:, i % 2, 128 * tt:128 * tt + 128],
                                        down_sb[:, e, :], start=False, stop=(e == EXPERTS - 1), skip_group_check=True)
                    last.then_inc(S["down_ps"], 1)

                def heads_to_tokens(q):
                    pe.wait_ge(S["o_done"], 2 * q + 2)
                    if q >= 1:
                        pe.wait_ge(S["x1_done"], q)
                    for tt in range(QT):
                        last = E.transpose(bank[7][:, 128 * tt:128 * tt + 128],
                                           onear[:, q % 2, 128 * tt:128 * tt + 128], ident_sb[:])
                    last.then_inc(S["o_tr"], 1)

                def mix_to_channels(q):
                    pe.wait_ge(S["mix_done"], q + 1)
                    for tt in range(QT):
                        last = E.transpose(bank[7][:, 128 * tt:128 * tt + 128],
                                           mix[:, tt].rearrange("p x j -> p (x j)"), ident_sb[:])
                    last.then_inc(S["mix_tr"], 1)

                def attention_out(q):
                    pe.wait_ge(S["mixt_done"], q + 1)
                    add_rows(bank[7][:].rearrange("p (t c) -> p t c", c=D), R_OUT, D, QT)
                    for tt in range(QT):
                        last = E.matmul(bank[7][:, 128 * tt:128 * tt + 128], mix_t[:, 128 * tt:128 * tt + 128],
                                        outw_sb[:], start=False, stop=True, skip_group_check=True)
                    last.then_inc(S["attn_ps"], 1)

                scores(0)
                for i in range(STEPS + 2):
                    if i < STEPS:
                        experts_in(i)
                    if i >= 2:
                        experts_out(i - 2)
                    if 1 <= i <= STEPS:
                        weight_rows(i - 1)
                    if i >= 2:
                        weighted_v(i - 2)
                    if i + 1 < STEPS:
                        scores(i + 1)
                    if i % 8 == 5 and i > 8:
                        heads_to_tokens(i // 8 - 1)
                    if i % 8 == 7 and i > 8:
                        mix_to_channels(i // 8 - 1)
                    if i % 8 == 0 and i > 8:
                        attention_out(i // 8 - 2)
                heads_to_tokens(3)

                def ffn_transposes(q):
                    pe.wait_ge(S["normed"], QUARTERS + q + 1)
                    if q == 0:
                        pe.wait_ge(S["near_exp"], STEPS)
                    if q >= 2:
                        pe.wait_ge(S["h2_aff"], q - 1)
                        pe.wait_ge(S["h2_lo"], q - 1)
                    for tt in range(QT):
                        last = E.transpose(bank[q % 2][:, 128 * tt:128 * tt + 128], gate[:, QT * q + tt, :], ident_sb[:])
                    last.then_inc(S["h2_tr"], 1)

                def ffn_up(q):
                    ts = slice(512 * q, 512 * q + 512)
                    pe.wait_ge(S["h2_lo"], q + 1)
                    if q == 0:
                        pe.wait_ge(S["o_done"], 8)
                        pe.wait_ge(S["act_done"], STEPS)
                    for f in range(FC):
                        if q >= 1:
                            pe.wait_ge(S["hid_done"], FC * (q - 1) + f + 1)
                        ws = slice(128 * f, 128 * f + 128)
                        three(bank[2 + f][:], fc1_hi[:, ws], fc1_lo[:, ws], xt_hi[:, ts], xt_lo[:, ts]
                              ).then_inc(S["fc1_ps"], 1)

                def ffn_down(q):
                    pe.wait_ge(S["hid_done"], FC * q + FC)
                    if q == 0:
                        pe.wait_ge(S["acc_done"], QUARTERS)
                    if q >= 1:
                        pe.wait_ge(S["y_done"], q)
                    add_rows(bank[6][:].rearrange("p (t c) -> p t c", c=D), R_FC2, D, QT)
                    for tt in range(QT):
                        for f in range(FC):
                            last = E.matmul(bank[6][:, 128 * tt:128 * tt + 128],
                                            hid[:, q % 2, f, 128 * tt:128 * tt + 128], fc2_sb[:, f, :],
                                            start=False, stop=(f == FC - 1), skip_group_check=True)
                    last.then_inc(S["fc2_ps"], 1)

                pe.wait_ge(S["split_done"], len(SPLITS))
                ffn_transposes(0)
                ffn_transposes(1)
                ffn_up(0)
                ffn_transposes(2)
                ffn_up(1)
                ffn_down(0)
                ffn_up(2)
                ffn_down(1)
                ffn_down(2)
                mix_to_channels(3)
                attention_out(3)
                ffn_transposes(3)
                ffn_up(3)
                ffn_down(3)


def kernel(**inputs):
    import numpy as np
    import concourse.bacc as bacc
    from concourse.bass_utils import run_bass_kernel_spmd

    a = {k: np.asarray(v) for k, v in inputs.items()}
    qkv_w, qkv_b = a["L0_attn_qkv_w"], a["L0_attn_qkv_b"]
    pos = a["L0_attn_pos_bias"]
    f32 = np.float32

    def by_group(w):
        return w.reshape(w.shape[:-1] + (4, 4, 8)).swapaxes(-1, -2).reshape(w.shape)

    w_tok = np.concatenate([qkv_w.reshape(128, 3, 4, 4, 8).transpose(0, 1, 3, 2, 4).reshape(128, 384),
                            by_group(a["L0_attn_gate_w"])], axis=1)
    row = np.concatenate([qkv_b.reshape(3, 4, 4, 8).transpose(0, 2, 1, 3).reshape(384), by_group(a["L0_attn_gate_b"]),
                          a["L0_ffn_router_bias"], a["L0_attn_out_b"], a["L0_attn_fc2_b"]])[None, :]
    gub = a["L0_ffn_gate_up_bias"].reshape(8, 2, 128).transpose(2, 0, 1).reshape(128, 16)
    cols = np.stack([a["L0_attn_ln1_g"], a["L0_attn_ln1_b"], a["L0_attn_ln2_g"], a["L0_attn_ln2_b"],
                     qkv_b[0:128], qkv_b[128:256]], axis=1)
    cols = np.concatenate([cols, gub, a["L0_attn_fc1_b"].reshape(4, 128).T], axis=1)
    band = np.full((HEADS, 96), CLOSED, f32)
    band[:, 31:64] = pos[32::-1, :].T
    far = np.broadcast_to(pos[33:38].reshape(NFAR, 4, 4).transpose(2, 0, 1).reshape(4, 1, NFAR * 4),
                          (4, 32, NFAR * 4)).reshape(128, NFAR * 4)
    p = np.arange(128)
    anti = (p[:, None] // 32 * 32 + 31 - p[:, None] % 32 == p[None, :]).astype(f32)
    headmask = (p[:, None] % 32 // 8 == np.arange(4)[None, :]).astype(f32)
    before = (np.arange(8)[None, :] < np.arange(8)[:, None]).astype(f32).reshape(1, 64)
    onehot = (np.arange(40)[:, None] % 32 == np.arange(8)[None, :]).astype(f32)
    arrays = {
        "x": a["L0_attn_x"].reshape(TOKENS, D), "ident": np.eye(128, dtype=f32), "anti": anti, "headmask": headmask,
        "before": before, "onehot": onehot, "cols": cols, "row": row, "far_bias": far, "band": band, "w_tok": w_tok,
        "w_qk_router": np.concatenate([qkv_w[:, 0:256], a["L0_ffn_router_weight"].T], axis=1),
        "gate_up": a["L0_ffn_gate_up_proj"].transpose(1, 0, 2).reshape(128, 2048), "down": a["L0_ffn_down_proj"],
        "down_bias": a["L0_ffn_down_bias"], "fc1": a["L0_attn_fc1_w"], "fc2": a["L0_attn_fc2_w"],
        "out_w": by_group(a["L0_attn_out_w"].T).T,
    }
    arrays = {"in_" + k: np.ascontiguousarray(v) for k, v in arrays.items()}

    nc = bacc.Bacc("TRN2", target_bir_lowering=False, num_devices=1)
    aps = [nc.dram_tensor(k, v.shape, mybir.dt.from_np(v.dtype), kind="ExternalInput").ap() for k, v in arrays.items()]
    y = nc.dram_tensor("y", (TOKENS, D), mybir.dt.float32, kind="ExternalOutput").ap()
    build(nc, *aps, y)
    r = run_bass_kernel_spmd(nc, [arrays], core_ids=[0])
    return r.results[0]["y"].reshape(1, TOKENS, D)
```

```python
import concourse.bass as bass
from concourse import mybir
from contextlib import ExitStack

TOKENS, D = 2048, 128
TILES = TOKENS // 128
QUARTERS, QT = 4, 4
HEADS, HD = 16, 8
HG = HEADS // 4
WINDOW = 64
FF, EXPERTS, INNER = 512, 8, 128
FC = FF // 128
EPS = 1e-5
CLOSED = -1e30
FAR = (48, 64, 96, 128, 192)
NFAR = len(FAR)
LIMIT, ALPHA = 7.0, 1.702
STEPS = 32
C_G1, C_B1, C_G2, C_B2, C_BQ, C_BK, C_GU, C_F1 = 0, 1, 2, 3, 4, 5, 6, 22
N_COLS = C_F1 + FC
R_TOK, R_ROUTER, R_OUT, R_FC2 = 0, 512, 520, 648
N_ROW = 776


def shifted_pieces(n, first_tile):
    a, back = n % 4, n // 4
    out = []
    if a < 4:
        out.append((a, 4, 0, back))
    if a:
        out.append((0, a, 4 - a, back + 1))
    return [(g0, g1, s0, b, max(0, b - first_tile)) for g0, g1, s0, b in out]


def build(nc, x, ident, anti, headmask, before, onehot, cols, row, far_bias, band, w_tok, w_qk_router,
          gate_up, down, down_bias, fc1, fc2, out_w, out):
    fp32, fp32r = mybir.dt.float32, mybir.dt.float32r
    ALU, ACT, AX = mybir.AluOpType, mybir.ActivationFunctionType, mybir.AxisListType

    qkv_dram = nc.dram_tensor("qkv_scratch", (3, 4, 32, 4, TILES, 32), fp32, kind="Internal").ap()
    far_dram = nc.dram_tensor("far_scratch", (QUARTERS, 4, 4, 32, QT * 36), fp32, kind="Internal").ap()

    with ExitStack() as ctx:
        def sb(name, shape, dt=fp32):
            return ctx.enter_context(nc.sbuf_tensor(name, shape, dt))

        def sem(name):
            return ctx.enter_context(nc.semaphore(name))

        x_sb = sb("x_sb", [128, TILES, D])
        xn0 = sb("xn0", [128, TILES, D])
        gate = sb("gate", [128, TILES, D])
        xt_hi = sb("xt_hi", [128, TOKENS], fp32r)
        xt_lo = sb("xt_lo", [128, TOKENS], fp32r)
        xf = sb("xf", [128, 2, 512])
        xn_parts = sb("xn_parts", [128, 4, 512], fp32r)
        xn_hi, xn_lo = xn_parts[:, 0:2, :], xn_parts[:, 2:4, :]
        stats = sb("stats", [128, TILES, 6])
        mv = sb("mv", [128, TILES, 2])
        sd = sb("sd", [128, 2, TILES])
        rs = sb("rs", [128, 4, TILES])
        ident_sb = sb("ident_sb", [128, 128])
        anti_sb = sb("anti_sb", [128, 128], fp32r)
        headmask_sb = sb("headmask_sb", [128, 4])
        before_sb = sb("before_sb", [128, EXPERTS * EXPERTS])
        onehot_raw = sb("onehot_raw", [40, EXPERTS])
        onehot_sb = sb("onehot_sb", [40, EXPERTS, 128], fp32r)
        cols_sb = sb("cols_sb", [128, N_COLS])
        up_bias1 = sb("up_bias1", [128, EXPERTS])
        bias_row = sb("bias_row", [40, N_ROW], fp32r)
        ones = sb("ones", [40, 128], fp32r)
        far_bias_sb = sb("far_bias_sb", [128, NFAR, HG])
        band_hi = sb("band_hi", [128, HG, WINDOW], fp32r)
        band_lo = sb("band_lo", [128, HG, WINDOW], fp32r)
        band0_hi = sb("band0_hi", [128, HG, WINDOW], fp32r)
        stage = sb("stage", [128, 2, 512])
        wtok_hi = sb("wtok_hi", [128, 512], fp32r)
        wtok_lo = sb("wtok_lo", [128, 512], fp32r)
        wqk_hi = sb("wqk_hi", [128, 264], fp32r)
        wqk_lo = sb("wqk_lo", [128, 264], fp32r)
        gu_hi = sb("gu_hi", [128, EXPERTS, 2 * INNER], fp32r)
        gu_lo = sb("gu_lo", [128, EXPERTS, 2 * INNER], fp32r)
        fc1_hi, fc1_lo = wtok_hi, wtok_lo
        fc2_sb = sb("fc2_sb", [128, FC, D])
        outw_sb = sb("outw_sb", [128, D])
        down_sb = sb("down_sb", [128, EXPERTS, D])
        db_raw = sb("db_raw", [EXPERTS, D])
        db3 = sb("db3", [72, D], fp32r)
        w3 = xn_parts[0:72, :, :].rearrange("p b n -> p (b n)")
        logit = sb("logit", [128, TILES, EXPERTS])
        logit_m = sb("logit_m", [128, 4, TILES])
        tok = sb("tok", [128, 3, 4, QT, 32])
        hg_q = sb("hg_q", [128, 2, 4 * QT, 32])
        hg_kv = sb("hg_kv", [128, 2, 4, TILES, 32])
        kv48 = sb("kv48", [128, 2, 2, 4 * QT, 32])
        qt = sb("qt", [128, TOKENS])
        kt = sb("kt", [128, 32 + TOKENS])
        qm = sb("qm", [128, 2, 8, 4, 32])
        vbd = sb("vbd", [128, 2, 4 * QT, 32, 4])
        prob = sb("prob", [128, 2, 8, WINDOW])
        prob_t = sb("prob_t", [128, 2, 8, WINDOW])
        mnear = sb("mnear", [128, 2, 8])
        mall = sb("mall", [128, 2, 4, QT, HG])
        lsum = sb("lsum", [128, 2, 4, QT, HG])
        sfar = sb("sfar", [128, 2, NFAR, 4 * QT * HG])
        mfar = sb("mfar", [128, 2, 4, QT, HG])
        lfar = sb("lfar", [128, 2, 4 * QT * HG])
        prod = sb("prod", [128, 4 * QT * 32])
        tree = sb("tree", [128, 4 * QT * 16])
        ofar = sb("ofar", [128, 2, 4 * QT, 36])
        ofar_tok = sb("ofar_tok", [128, 4, QT, 36])
        tok_flat = tok[:].rearrange("p w j t x -> p (w j t x)")
        onear = tok_flat[:, 0:1024].rearrange("p (b n) -> p b n", b=2)
        mix = tok_flat[:, 1024:1536].rearrange("p (t x j) -> p t x j", t=QT, j=4)
        mix_t = xf[:, 0, :]
        g_act = sb("g_act", [128, 2, 512])
        u_act = sb("u_act", [128, 2, 512])
        th_act = sb("th_act", [128, 2, 512])
        rank_a = th_act[:].rearrange("p b n -> p (b n)")
        rank_b = u_act[:].rearrange("p b n -> p (b n)")
        row_raw = g_act[:].rearrange("p b n -> p (b n)")[0:1, 0:N_ROW]
        raw_w = [stage[:, 0, :], stage[:, 1, :]] + [
            t[:, b].rearrange("p s w -> p (s w)") for t in (prob, prob_t) for b in range(2)] + [stage[:, 0, :]]
        anti_raw = u_act[:, 0, 0:128]
        band_raw = u_act[:, 1, 0:HG * WINDOW].rearrange("p (h w) -> p h w", h=HG)
        hid = vbd[:, :, :, :, :].rearrange("p b s x j -> p b (s x j)").rearrange("p b (f n) -> p b f n", f=FC)

        bank = [ctx.enter_context(nc.psum_tensor(f"bank{i}", [128, 512], fp32)) for i in range(8)]

        x_in = [sem(f"x_in{q}") for q in range(QUARTERS)]
        small_in, mat_in = sem("small_in"), sem("mat_in")
        first_in = sem("first_in")
        w_in = [sem(f"w_in{s}") for s in range(7)]
        qkv_out = [sem(f"qkv_out{q}") for q in range(QUARTERS)]
        hg_in = [sem(f"hg_in{q}") for q in range(QUARTERS)]
        k48_in = [sem(f"k48_in{q}") for q in range(QUARTERS)]
        v48_in = [sem(f"v48_in{q}") for q in range(QUARTERS)]
        far_out = [sem(f"far_out{q}") for q in range(QUARTERS)]
        far_in = [sem(f"far_in{q}") for q in range(QUARTERS)]
        stored = sem("stored")
        names = ("stats_done aggr_done sd_done dve_chain normed x_tr h_tr x_hi x_lo xf_done h_hi h_lo logits_ps "
                 "qk_ps qt_done kt_done tok_ps tok_done gate_pre gate_tanh gate_done split_done consts_done zeroed "
                 "pool_chain logit_sh logit_exp w_tr w_hi w_lo w_hi2 db_done db_hi vbd_done qm_done sfar_done "
                 "far_sh far_exp mfar_done score_ps near_max near_exp sum_done probt_done gate_ps up_ps wrep_ps "
                 "g_raw u_raw g_half u_clip g_tanh glu_done gu_done act_done acc_done o_done inv_done ofar_done "
                 "o_tr mix1 bias_done scaled high_done rows_zeroed var1_done mix2 mix_done mix_tr mixt_done "
                 "attn_ps x1_done base_done fc1_ps hid_done fc2_ps y_done h2_tr h2_aff h2_hi h2_lo stats2 "
                 "mall_done ranked down_ps o_pv").split()
        S = {n: sem(n) for n in names}

        SPLITS = ([(wtok_hi, wtok_lo, 0, 512), (wqk_hi, wqk_lo, 0, 264)]
                  + [(gu_hi, gu_lo, 512 * i, 512) for i in range(4)] + [(fc1_hi, fc1_lo, 0, 512)])
        SPLIT_SRC = [w_tok, w_qk_router] + [gate_up[:, 512 * i:512 * i + 512] for i in range(4)] + [fc1]
        N_GU = 3

        def flat2(t):
            ap = t[:]
            return ap.rearrange("p e n -> p (e n)") if len(t.shape) == 3 else ap

        FAR_SHIFT = (0, 2, 3, 4, 6)
        FFN_STEP = 26
        FFN_PARTS = ((0, 2 * QT), (2 * QT, 3 * QT), (3 * QT, TILES))
        T_BANK = (7, 1, 0, 1)
        W_BANK = (7, 5, 2, 6)
        N_SMALL = 16 * 10
        N_MAT = 16 * 3

        with nc.Block() as block:

            @block.sync
            def _(sp):
                xv = x.rearrange("(t p) c -> p t c", p=128)

                def load_x(q):
                    sp.dma_start(x_sb[:, QT * q:QT * q + QT, :], xv[:, QT * q:QT * q + QT, :]).then_inc(x_in[q], 16)

                def load_weights(s):
                    sp.dma_start(raw_w[s][:, 0:SPLITS[s][3]], SPLIT_SRC[s]).then_inc(w_in[s], 16)

                load_x(0)
                sp.dma_start(ident_sb[:], ident).then_inc(first_in, 16)
                sp.dma_start(cols_sb[:], cols).then_inc(first_in, 16)
                sp.dma_start(row_raw, row).then_inc(first_in, 16)
                load_weights(1)
                load_weights(0)
                for q in range(1, QUARTERS):
                    load_x(q)
                load_weights(2)
                load_weights(3)
                sp.dma_start(anti_raw, anti).then_inc(small_in, 16)
                for j in range(4):
                    src = bass.AP(tensor=band.tensor, offset=96 * j, ap=[[1, 32], [4 * 96, HG], [1, WINDOW]])
                    sp.dma_start(band_raw[32 * j:32 * j + 32, :, :], src).then_inc(small_in, 16)
                sp.dma_start(onehot_raw[:], onehot).then_inc(small_in, 16)
                sp.dma_start(far_bias_sb[:, :, :].rearrange("p f h -> p (f h)"), far_bias).then_inc(small_in, 16)
                sp.dma_start(headmask_sb[:], headmask).then_inc(small_in, 16)
                sp.dma_start(before_sb[:], before.to_broadcast([128, EXPERTS * EXPERTS])).then_inc(small_in, 16)
                sp.dma_start(db_raw[:], down_bias).then_inc(small_in, 16)
                load_weights(4)
                load_weights(5)

                def before48(q, w, heads=range(4)):
                    for j in heads:
                        for half in range(2):
                            n, r0, rs0 = (1, 16, 0) if half else (2, 0, 16)
                            for g0, g1, s0, back, skip in shifted_pieces(n, QT * q):
                                dst = kv48[32 * j + r0:32 * j + r0 + 16, q % 2, w - 1, :, :].rearrange(
                                    "p (g t) x -> p g t x", g=4)[:, g0:g1, skip:QT, :]
                                src = qkv_dram[w, j, rs0:rs0 + 16, s0:s0 + g1 - g0,
                                               QT * q - back + skip:QT * q - back + QT, :]
                                sp.dma_start(dst, src).then_inc(k48_in[q] if w == 1 else v48_in[q], 16)

                def qkv_to_dram(q):
                    sp.wait_ge(S["tok_done"], QT * q + QT)
                    for g in range(4):
                        sp.dma_start(qkv_dram[:, :, :, g, QT * q:QT * q + QT, :].rearrange("w j r t x -> r (w j) (t x)"),
                                     tok[32 * g:32 * g + 32].rearrange("p w j t x -> p (w j) (t x)")
                                     ).then_inc(qkv_out[q], 16)

                def head_groups(q):
                    sp.wait_ge(qkv_out[q], 64)
                    if q >= 2:
                        sp.wait_ge(S["sfar_done"], q - 1)
                    tiles = slice(QT * q, QT * q + QT)
                    for w in range(3):
                        dst = (hg_kv[:, w - 1, :, tiles, :] if w else
                               hg_q[:, q % 2, :, :].rearrange("p (g t) x -> p g t x", g=4))
                        sp.dma_start(dst.rearrange("p g t x -> p g (t x)"),
                                     qkv_dram[w, :, :, :, tiles, :].rearrange("j r g t x -> (j r) g (t x)")
                                     ).then_inc(hg_in[q], 16)

                qkv_to_dram(0)
                head_groups(0)
                qkv_to_dram(1)
                sp.wait_ge(S["zeroed"], 1)
                before48(0, 1, (0, 1))
                qkv_to_dram(2)
                before48(0, 1, (2, 3))
                qkv_to_dram(3)
                head_groups(1)
                sp.dma_start(down_sb[:], down.rearrange("e i h -> i e h")).then_inc(mat_in, 16)
                sp.dma_start(outw_sb[:], out_w).then_inc(mat_in, 16)
                sp.dma_start(fc2_sb[:], fc2.rearrange("(f p) n -> p f n", p=128)).then_inc(mat_in, 16)
                sp.wait_ge(S["split_done"], 2)
                load_weights(6)
                before48(1, 1)
                before48(0, 2)
                head_groups(2)
                before48(2, 1)
                before48(1, 2)
                head_groups(3)
                before48(3, 1)

                for q in range(QUARTERS):
                    sp.wait_ge(S["ofar_done"], q + 1)
                    sp.wait_ge(S["inv_done"], q + 1)
                    for j in range(4):
                        sp.dma_start(far_dram[q, j].rearrange("g r n -> r g n"),
                                     ofar[32 * j:32 * j + 32, q % 2, :, :].rearrange("p (g t) x -> p g (t x)", g=4)
                                     ).then_inc(far_out[q], 16)
                    sp.wait_ge(far_out[q], 64)
                    if q >= 1:
                        sp.wait_ge(S["mix2"], q)
                    sp.dma_start(ofar_tok[:].rearrange("p j t x -> p j (t x)"),
                                 far_dram[q].rearrange("j g r n -> (g r) j n")).then_inc(far_in[q], 16)
                    if q + 2 < QUARTERS:
                        before48(q + 2, 2)

                ov = out.rearrange("(t p) c -> p t c", p=128)
                for q in range(QUARTERS):
                    sp.wait_ge(S["y_done"], q + 1)
                    sp.dma_start(ov[:, QT * q:QT * q + QT, :], x_sb[:, QT * q:QT * q + QT, :]).then_inc(stored, 16)
                sp.wait_ge(stored, 16 * QUARTERS)

            def total48(q):
                return 16 * sum(4 * len(shifted_pieces(n, QT * q)) for n in (1, 2))

            @block.gpsimd
            def _(pool):
                P = nc.gpsimd
                chain = [0]

                def link(ins):
                    chain[0] += 1
                    ins.then_inc(S["pool_chain"], 1)
                    pool.wait_ge(S["pool_chain"], chain[0])

                P.memset(bias_row[:].bitcast(fp32), 0.0)
                P.memset(ones[:].bitcast(fp32), 1.0).then_inc(S["rows_zeroed"], 1)

                pool.wait_ge(first_in, 48)
                P.tensor_scalar(cols_sb[:, C_BQ:C_BQ + 1], cols_sb[:, C_BQ:C_BQ + 1], HD ** -0.5, None, ALU.mult)
                P.tensor_scalar(row_raw[:, 0:128], row_raw[:, 0:128], HD ** -0.5, None, ALU.mult
                                ).then_inc(S["scaled"], 1)
                for s in (1, 0):
                    pool.wait_ge(w_in[s], 16)
                    P.tensor_scalar(raw_w[s][:, 0:128], raw_w[s][:, 0:128], HD ** -0.5, None, ALU.mult
                                    ).then_inc(S["scaled"], 1)
                pool.wait_ge(S["scaled"], 3)
                pool.wait_ge(S["high_done"], 1)
                P.tensor_tensor(bias_row[32:33, :], row_raw, bias_row[0:1, :].bitcast(fp32), ALU.subtract
                                ).then_inc(S["bias_done"], 1)
                pool.wait_ge(S["bias_done"], 1)
                for k, s in enumerate((1, 0)):
                    hi, lo, at, n = SPLITS[s]
                    pool.wait_ge(S["high_done"], 2 + k)
                    P.tensor_tensor(lo[:, 0:n], raw_w[s][:, 0:n], hi[:, 0:n].bitcast(fp32), ALU.subtract
                                    ).then_inc(S["split_done"], 1)

                def split(s):
                    hi, lo, at, n = SPLITS[s]
                    raw = raw_w[s][:, 0:n]
                    pool.wait_ge(w_in[s], 16)
                    link(P.tensor_copy(flat2(hi)[:, at:at + n], raw))
                    P.tensor_tensor(flat2(lo)[:, at:at + n], raw, flat2(hi)[:, at:at + n].bitcast(fp32),
                                    ALU.subtract).then_inc(S["split_done"], 1)

                link(P.memset(kv48[:, 0, :, :, :], 0.0))
                link(P.memset(kt[:, 0:32], 0.0))
                P.memset(db3[:].bitcast(fp32), 0.0)
                P.memset(prod[:], 0.0)
                P.memset(ofar[:, 0, :, :], 0.0)
                P.memset(vbd[:], 0.0).then_inc(S["zeroed"], 1)
                pool.wait_ge(small_in, N_SMALL)
                P.tensor_scalar(up_bias1[:], cols_sb[:, C_GU:C_GU + 16].rearrange("p (e h) -> p e h", h=2)[:, :, 1],
                                1.0, None, ALU.add)
                P.tensor_copy(anti_sb[:], anti_raw)
                P.tensor_copy(onehot_sb[:], onehot_raw[:].unsqueeze(2).to_broadcast([40, EXPERTS, 128]))
                link(P.tensor_copy(band_hi[:], band_raw))
                P.tensor_tensor(band_lo[:], band_raw, band_hi[:].bitcast(fp32), ALU.subtract)
                link(P.tensor_copy(band0_hi[:, :, 32:], band_raw[:, :, 32:]))
                P.memset(band0_hi[:, :, 0:32].bitcast(fp32), CLOSED).then_inc(S["consts_done"], 1)
                for s in (2, 3, 4):
                    split(s)

                def far_scores(q):
                    pool.wait_ge(hg_in[q], 48)
                    if q >= 2:
                        pool.wait_ge(S["inv_done"], q - 1)
                    pv = prod[:].rearrange("p (g t x) -> p g t x", g=4, t=QT)
                    qv = hg_q[:, q % 2, :, :].rearrange("p (g t) x -> p g t x", g=4)
                    for f, n in list(enumerate(FAR_SHIFT))[::-1]:
                        if f == 0:
                            pool.wait_ge(k48_in[q], total48(q))
                            last = P.tensor_tensor(pv, qv,
                                                   kv48[:, q % 2, 0, :, :].rearrange("p (g t) x -> p g t x", g=4),
                                                   ALU.mult)
                        else:
                            for g0, g1, s0, back, skip in shifted_pieces(n, QT * q):
                                t0 = QT * q - back
                                if skip >= QT:
                                    continue
                                last = P.tensor_tensor(pv[:, g0:g1, skip:QT, :],
                                                       qv[:, g0:g1, skip:QT, :],
                                                       hg_kv[:, 0, s0:s0 + g1 - g0, t0 + skip:t0 + QT, :], ALU.mult)
                        link(last)
                        p8 = prod[:].rearrange("p (n d) -> p n d", d=HD)
                        t4 = tree[:].rearrange("p (n d) -> p n d", d=4)
                        link(P.tensor_tensor(t4, p8[:, :, 0:4], p8[:, :, 4:8], ALU.add))
                        link(P.tensor_tensor(t4[:, :, 0:2], t4[:, :, 0:2], t4[:, :, 2:4], ALU.add))
                        link(P.tensor_tensor(sfar[:, q % 2, f, :], t4[:, :, 0], t4[:, :, 1], ALU.add))
                        s3 = sfar[:, q % 2, f, :].rearrange("p (s h) -> p s h", h=HG)
                        last = P.tensor_tensor(s3, s3, far_bias_sb[:, f, :].unsqueeze(1).to_broadcast(
                            [128, 4 * QT, HG]), ALU.add)
                        if q == 0:
                            link(last)
                            s4 = sfar[:, 0, f, :].rearrange("p (g t h) -> p g t h", g=4, t=QT)
                            if f == 0:
                                link(P.memset(s4[:, 0, 0, :], CLOSED))
                                for j in range(4):
                                    last = P.memset(s4[32 * j:32 * j + 16, 1, 0, :], CLOSED)
                                    if j < 3:
                                        link(last)
                            else:
                                full, part = n // 4, n % 4
                                if full:
                                    last = P.memset(s4[:, :, 0:full, :], CLOSED)
                                if part:
                                    last = P.memset(s4[:, 0:part, full, :], CLOSED)
                    last.then_inc(S["sfar_done"], 1)

                def far_output(q):
                    pool.wait_ge(S["mall_done"], 8 * q + 8)
                    P.tensor_tensor(sfar[:, q % 2, :, :], sfar[:, q % 2, :, :],
                                    mall[:, q % 2].rearrange("p g t h -> p (g t h)").unsqueeze(1).to_broadcast(
                                        [128, NFAR, 4 * QT * HG]), ALU.add).then_inc(S["far_sh"], 1)
                    pool.wait_ge(S["far_exp"], q + 1)
                    if q >= 2:
                        pool.wait_ge(far_out[q - 2], 64)
                    ov = ofar[:, q % 2, :, 0:32].rearrange("p (g t) x -> p g t x", g=4)
                    pv = prod[:].rearrange("p (g t x) -> p g t x", g=4, t=QT)
                    for f, n in enumerate(FAR_SHIFT):
                        pf = sfar[:, q % 2, f, :].rearrange("p (g n) -> p g n", g=4)
                        if f == 0:
                            pool.wait_ge(v48_in[q], total48(q))
                            a = pf.unsqueeze(3).to_broadcast([128, 4, QT * HG, HD])
                            b = kv48[:, q % 2, 1, :, :].rearrange("p (g t) (h d) -> p g (t h) d", g=4, d=HD)
                            o = ofar[:, q % 2, :, 0:32].rearrange("p s (h d) -> p s h d", d=HD)
                            link(P.tensor_tensor(
                                o, sfar[:, q % 2, 0, :].rearrange("p (s h) -> p s h", h=HG).unsqueeze(3).to_broadcast(
                                    [128, 4 * QT, HG, HD]),
                                kv48[:, q % 2, 1, :, :].rearrange("p s (h d) -> p s h d", d=HD), ALU.mult))
                            continue
                        pieces = [p for p in shifted_pieces(n, QT * q) if p[4] < QT]
                        for g0, g1, s0, back, skip in pieces:
                            t0 = QT * q - back
                            last = P.tensor_tensor(
                                pv[:, g0:g1, skip:QT, :].rearrange("p g t (h d) -> p g (t h) d", d=HD),
                                pf[:, g0:g1, skip * HG:].unsqueeze(3).to_broadcast(
                                    [128, g1 - g0, (QT - skip) * HG, HD]),
                                hg_kv[:, 1, s0:s0 + g1 - g0, t0 + skip:t0 + QT, :].rearrange(
                                    "p g t (h d) -> p g (t h) d", d=HD), ALU.mult)
                        link(last)
                        for g0, g1, s0, back, skip in pieces:
                            last = P.tensor_tensor(ov[:, g0:g1, skip:QT, :], ov[:, g0:g1, skip:QT, :],
                                                   pv[:, g0:g1, skip:QT, :], ALU.add)
                        if f < NFAR - 1:
                            link(last)
                        else:
                            last.then_inc(S["ofar_done"], 1)
                            pool.wait_ge(S["ofar_done"], q + 1)

                far_scores(0)
                pool.wait_ge(S["sfar_done"], 1)
                split(5)
                pool.wait_ge(S["split_done"], 6)
                far_scores(1)
                pool.wait_ge(S["sfar_done"], 2)
                pool.wait_ge(S["gate_tanh"], QUARTERS)
                P.tensor_scalar(gate[:], gate[:], 0.5, 0.5, ALU.mult, ALU.add).then_inc(S["gate_done"], 1)
                split(len(SPLITS) - 1)
                far_output(0)
                far_scores(2)
                far_output(1)
                far_scores(3)
                far_output(2)

                def base(q):
                    pool.wait_ge(S["x1_done"], q + 1)
                    pool.wait_ge(S["acc_done"], q + 1)
                    t = slice(QT * q, QT * q + QT)
                    P.tensor_tensor(x_sb[:, t, :], x_sb[:, t, :], xn0[:, t, :], ALU.add).then_inc(S["base_done"], 1)

                base(0)
                base(1)
                far_output(3)
                base(2)
                base(3)

            @block.scalar
            def _(act):
                A = nc.scalar

                def col(c):
                    return cols_sb[:, c:c + 1]

                def first_sqrt(part):
                    t = slice(0, QT) if part == 0 else slice(QT, TILES)
                    act.wait_ge(S["aggr_done"], part + 1)
                    A.activation(sd[:, 0, t], mv[:, t, 1], ACT.Sqrt, bias=EPS).then_inc(S["sd_done"], 1)

                def second_sqrt(part):
                    t = slice(0, QT) if part == 0 else slice(QT, TILES)
                    act.wait_ge(S["var1_done"], part + 1)
                    A.activation(sd[:, 1, t], rs[:, 1, t], ACT.Sqrt, bias=EPS).then_inc(S["sd_done"], 1)

                def x_high(q):
                    act.wait_ge(S["x_tr"], q + 1)
                    A.copy(xt_hi[:, 512 * q:512 * q + 512], bank[0][:]).then_inc(S["x_hi"], 1)

                def h_high(q):
                    act.wait_ge(S["xf_done"], q + 1)
                    if q >= 2:
                        act.wait_ge(S["tok_ps"], QT * (q - 1))
                    A.copy(xn_hi[:, q % 2, :], xf[:, q % 2, :]).then_inc(S["h_hi"], 1)

                def q_and_k(q):
                    if q == 0:
                        act.wait_ge(S["bias_done"], 1)
                        act.wait_ge(S["zeroed"], 1)
                    act.wait_ge(S["qk_ps"], 2 * q + 1)
                    A.activation(qt[:, 512 * q:512 * q + 512], bank[2][:], ACT.Identity, bias=col(C_BQ)
                                 ).then_inc(S["qt_done"], 1)
                    act.wait_ge(S["qk_ps"], 2 * q + 2)
                    A.activation(kt[:, 32 + 512 * q:32 + 512 * q + 512], bank[3][:], ACT.Identity,
                                 bias=col(C_BK)).then_inc(S["kt_done"], 1)

                def tokens(t):
                    if t % QT == 0 and t > 0:
                        act.wait_ge(qkv_out[t // QT - 1], 64)
                    act.wait_ge(S["tok_ps"], t + 1)
                    A.copy(tok[:, :, :, t % QT, :].rearrange("p w j x -> p (w j) x"),
                           bank[4 + t % 2][:, 0:384].rearrange("p (a x) -> p a x", x=32)).then_inc(S["tok_done"], 1)
                    A.copy(gate[:, t, :], bank[4 + t % 2][:, 384:512]).then_inc(S["gate_pre"], 1)

                first_sqrt(0)
                second_sqrt(0)
                act.wait_ge(S["rows_zeroed"], 1)
                act.wait_ge(S["scaled"], 1)
                A.copy(bias_row[0:1, :], row_raw).then_inc(S["high_done"], 1)
                x_high(0)
                act.wait_ge(S["scaled"], 2)
                A.copy(wqk_hi[:], raw_w[1][:, 0:264]).then_inc(S["high_done"], 1)
                h_high(0)
                act.wait_ge(S["scaled"], 3)
                A.copy(wtok_hi[:], raw_w[0][:, 0:512]).then_inc(S["high_done"], 1)
                first_sqrt(1)
                second_sqrt(1)
                def logit_weights(part):
                    act.wait_ge(S["logit_sh"], part + 1)
                    t = slice(8 * part, 8 * part + 8)
                    A.activation(logit[:, t, :], logit[:, t, :], ACT.Exp).then_inc(S["logit_exp"], 1)

                for q in range(QUARTERS):
                    q_and_k(q)
                    if q + 1 < QUARTERS:
                        x_high(q + 1)
                        if q == 2:
                            logit_weights(0)
                    else:
                        logit_weights(1)
                    tokens(QT * q)
                    tokens(QT * q + 1)
                    if q + 1 < QUARTERS:
                        h_high(q + 1)
                    tokens(QT * q + 2)
                    tokens(QT * q + 3)
                act.wait_ge(small_in, N_SMALL)
                act.wait_ge(S["zeroed"], 1)
                A.copy(db3[0:8, :], db_raw[:])
                A.copy(db3[32:40, :], db_raw[:]).then_inc(S["db_hi"], 1)
                def masked_q(c, j):
                    if c >= 2 and j == 0:
                        act.wait_ge(S["score_ps"], 4 * (c - 1))
                    A.activation(qm[:, c % 2, :, j, :],
                                 qt[:, 256 * c:256 * c + 256].rearrange("p (s r) -> p s r", r=32),
                                 ACT.Copy, scale=headmask_sb[:, j:j + 1]).then_inc(S["qm_done"], 1)

                act.wait_ge(S["qt_done"], QUARTERS)
                for j in range(4):
                    masked_q(0, j)
                masked_q(1, 0)
                act.wait_ge(S["tok_ps"], TILES)
                for q in range(QUARTERS):
                    ts = slice(512 * q, 512 * q + 512)
                    act.wait_ge(S["w_tr"], q + 1)
                    A.copy(w3[0:8, ts], bank[W_BANK[q]][0:8, :]).then_inc(S["w_hi"], 1)

                def v_block(q, j):
                    if j == 0:
                        act.wait_ge(hg_in[q], 48)
                        if q >= 2:
                            act.wait_ge(S["o_pv"], 8 * (q - 1) + 4)
                    A.copy(vbd[32 * j:32 * j + 32, q % 2, :, :, j].rearrange("p (g t) x -> p g (t x)", g=4),
                           hg_kv[32 * j:32 * j + 32, 1, :, QT * q:QT * q + QT, :].rearrange(
                               "p g t x -> p g (t x)")).then_inc(S["vbd_done"], 1)

                def near_out(c):
                    act.wait_ge(S["o_pv"], 4 * c + 4)
                    if c == 0:
                        act.wait_ge(qkv_out[QUARTERS - 1], 64)
                    if c >= 4 and c % 2 == 0:
                        act.wait_ge(S["o_tr"], c // 2 - 1)
                    A.copy(onear[:, (c // 2) % 2, 256 * (c % 2):256 * (c % 2) + 256], bank[2][:, 0:256]
                           ).then_inc(S["o_done"], 1)

                def far_weights(q):
                    act.wait_ge(S["far_sh"], q + 1)
                    A.activation(sfar[:, q % 2, :, :], sfar[:, q % 2, :, :], ACT.Exp).then_inc(S["far_exp"], 1)

                def near_weights(i):
                    c, h = i // 4, i % 4
                    act.wait_ge(S["mall_done"], i + 1)
                    if i == 0:
                        act.wait_ge(S["split_done"], 4)
                    if i >= 2:
                        act.wait_ge(S["probt_done"], i - 1)
                    for s in range(8):
                        least = mall[:, (c // 2) % 2, s % 4, 2 * (c % 2) + s // 4, h:h + 1]
                        last = A.activation(prob[:, i % 2, s, :], bank[i % 2][:, WINDOW * s:WINDOW * s + WINDOW],
                                            ACT.Exp, bias=least)
                    last.then_inc(S["near_exp"], 1)

                def gate_tanh(q):
                    act.wait_ge(S["gate_pre"], QT * q + QT)
                    t = slice(QT * q, QT * q + QT)
                    A.activation(gate[:, t, :], gate[:, t, :], ACT.Tanh, scale=0.5).then_inc(S["gate_tanh"], 1)

                def mix_evac(q):
                    act.wait_ge(S["mix_tr"], q + 1)
                    A.copy(mix_t, bank[7][:]).then_inc(S["mixt_done"], 1)

                def ffn_sqrt(part):
                    t = slice(*FFN_PARTS[part])
                    act.wait_ge(S["stats2"], part + 1)
                    A.activation(sd[:, 0, t], mv[:, t, 1], ACT.Sqrt, bias=EPS).then_inc(S["sd_done"], 1)

                def ffn_high(q):
                    act.wait_ge(S["h2_aff"], q + 1)
                    A.copy(xt_hi[:, 512 * q:512 * q + 512], xf[:, q % 2, :]).then_inc(S["h2_hi"], 1)

                def gate_up_bias(i):
                    e = i % EXPERTS
                    act.wait_ge(S["gate_ps"], i + 1)
                    if i >= 2:
                        act.wait_ge(S["glu_done"], i - 1)
                    A.activation(g_act[:, i % 2, :], bank[3][:], ACT.Identity,
                                 bias=col(C_GU + 2 * e)).then_inc(S["g_raw"], 1)
                    act.wait_ge(S["up_ps"], i + 1)
                    if i >= 2:
                        act.wait_ge(S["down_ps"], i - 1)
                    A.activation(u_act[:, i % 2, :], bank[4][:], ACT.Identity,
                                 bias=up_bias1[:, e:e + 1]).then_inc(S["u_raw"], 1)

                gate_up_bias(0)
                act.wait_ge(S["w_hi"], QUARTERS)
                for q in range(QUARTERS):
                    A.copy(w3[64:72, 512 * q:512 * q + 512], w3[0:8, 512 * q:512 * q + 512].bitcast(fp32)
                           ).then_inc(S["w_hi2"], 1)
                for i in range(STEPS + 1):
                    if i >= 1:
                        act.wait_ge(S["g_half"], i)
                        A.activation(th_act[:, (i - 1) % 2, :], g_act[:, (i - 1) % 2, :], ACT.Tanh, scale=ALPHA
                                     ).then_inc(S["g_tanh"], 1)
                    if i < STEPS:
                        near_weights(i)
                        if i > 0:
                            gate_up_bias(i)
                    if i + 5 < STEPS:
                        masked_q((i + 5) // 4, (i + 5) % 4)
                    if i % 4 == 1 and i > 4:
                        near_out(i // 4 - 1)
                    if i % 8 == 0 and 0 < i < STEPS:
                        far_weights(i // 8 - 1)
                    if 5 <= i < 5 + 8 * (QUARTERS - 1) and (i - 5) % 8 < 4:
                        v_block((i - 5) // 8 + 1, (i - 5) % 8)
                    if i < 2:
                        v_block(0, 2 * i)
                        v_block(0, 2 * i + 1)
                    if 2 <= i < 2 + QUARTERS:
                        gate_tanh(i - 2)
                    if i == FFN_STEP:
                        ffn_sqrt(0)
                    if i == FFN_STEP + 3:
                        ffn_high(0)
                    if i % 8 == 7 and i > 8:
                        if i == STEPS - 1:
                            act.wait_ge(S["h2_lo"], 1)
                        mix_evac(i // 8 - 1)
                far_weights(3)
                near_out(7)

                def ffn_gelu(q):
                    for f in range(FC):
                        act.wait_ge(S["fc1_ps"], FC * q + f + 1)
                        if q >= 2 and f == 0:
                            act.wait_ge(S["fc2_ps"], q - 1)
                        A.activation(hid[:, q % 2, f, :], bank[2 + f][:], ACT.Gelu,
                                     bias=col(C_F1 + f)).then_inc(S["hid_done"], 1)

                ffn_sqrt(1)
                ffn_high(1)
                ffn_gelu(0)
                ffn_high(2)
                ffn_gelu(1)
                ffn_gelu(2)
                act.wait_ge(S["h2_lo"], 3)
                mix_evac(3)
                ffn_sqrt(2)
                ffn_high(3)
                ffn_gelu(3)

            @block.vector
            def _(dve):
                V = nc.vector
                chain = [0]

                def link(ins):
                    chain[0] += 1
                    ins.then_inc(S["dve_chain"], 1)
                    dve.wait_ge(S["dve_chain"], chain[0])

                def col(c):
                    return cols_sb[:, c:c + 1]

                def statistics(t0, t1, part):
                    for t in range(t0, t1):
                        if t % QT == 0:
                            dve.wait_ge(x_in[t // QT], 16)
                        last = V.bn_stats(stats[:, t, :], x_sb[:, t, :])
                    last.then_inc(S["stats_done"], 1)
                    dve.wait_ge(S["stats_done"], part + 1)
                    for t in range(t0, t1):
                        last = V.bn_aggr(mv[:, t, :], stats[:, t, :])
                    last.then_inc(S["aggr_done"], 1)

                def scale0(t0, t1, part):
                    t = slice(t0, t1)
                    dve.wait_ge(S["sd_done"], 2 * part + 1)
                    link(V.reciprocal(rs[:, 0, t], sd[:, 0, t]))
                    link(V.tensor_tensor(rs[:, 1, t], mv[:, t, 1], rs[:, 0, t], ALU.mult))
                    V.tensor_tensor(rs[:, 1, t], rs[:, 1, t], rs[:, 0, t], ALU.mult).then_inc(S["var1_done"], 1)

                def scale1(t0, t1, part):
                    t = slice(t0, t1)
                    dve.wait_ge(S["sd_done"], 2 * part + 2)
                    link(V.reciprocal(rs[:, 2, t], sd[:, 1, t]))
                    link(V.tensor_tensor(rs[:, 3, t], rs[:, 2, t], rs[:, 0, t], ALU.mult))

                def normalize0(q):
                    for t in range(QT * q, QT * q + QT):
                        V.tensor_scalar(xn0[:, t, :], x_sb[:, t, :], mv[:, t, 0:1], rs[:, 0, t:t + 1],
                                        ALU.subtract, ALU.mult)

                def normalize1(q):
                    for t in range(QT * q, QT * q + QT):
                        last = V.tensor_scalar(gate[:, t, :], x_sb[:, t, :], mv[:, t, 0:1], rs[:, 3, t:t + 1],
                                               ALU.subtract, ALU.mult)
                    last.then_inc(S["normed"], 1)

                def operands(q):
                    ts = slice(512 * q, 512 * q + 512)
                    dve.wait_ge(S["h_tr"], q + 1)
                    if q >= 2:
                        dve.wait_ge(S["h_lo"], q - 1)
                    V.tensor_scalar(xf[:, q % 2, :], bank[1][:], col(C_G1), col(C_B1), ALU.mult, ALU.add
                                    ).then_inc(S["xf_done"], 1)
                    dve.wait_ge(S["x_hi"], q + 1)
                    V.tensor_tensor(xt_lo[:, ts], bank[0][:], xt_hi[:, ts].bitcast(fp32), ALU.subtract
                                    ).then_inc(S["x_lo"], 1)
                    dve.wait_ge(S["h_hi"], q + 1)
                    if q >= 2:
                        dve.wait_ge(S["tok_ps"], QT * (q - 1))
                    V.tensor_tensor(xn_lo[:, q % 2, :], xf[:, q % 2, :], xn_hi[:, q % 2, :].bitcast(fp32),
                                    ALU.subtract).then_inc(S["h_lo"], 1)

                statistics(0, QT, 0)
                scale0(0, QT, 0)
                normalize0(0)
                scale1(0, QT, 0)
                normalize1(0)
                dve.wait_ge(first_in, 48)
                operands(0)
                statistics(QT, TILES, 1)
                scale0(QT, TILES, 1)
                normalize0(1)
                scale1(QT, TILES, 1)
                normalize1(1)
                normalize0(2)
                normalize1(2)
                operands(1)
                normalize0(3)
                normalize1(3)
                def router_shift(part):
                    t = slice(8 * part, 8 * part + 8)
                    dve.wait_ge(S["logits_ps"], part + 1)
                    logits = bank[6 + part][:, 0:64].rearrange("p (t e) -> p t e", e=EXPERTS)
                    link(V.tensor_reduce(logit_m[:, 0, t], logits, AX.X, ALU.max))
                    V.tensor_tensor(logit[:, t, :], logits, logit_m[:, 0, t].unsqueeze(2).to_broadcast(
                        [128, 8, EXPERTS]), ALU.subtract).then_inc(S["logit_sh"], 1)

                def router_rank(part):
                    t = slice(8 * part, 8 * part + 8)
                    dve.wait_ge(S["logit_exp"], part + 1)
                    if part == 0:
                        dve.wait_ge(S["consts_done"], 1)
                        dve.wait_ge(small_in, N_SMALL)
                    half = slice(512 * part, 512 * part + 512)
                    e4 = logit[:, t, :].unsqueeze(3).to_broadcast([128, 8, EXPERTS, EXPERTS])
                    e4t = logit[:, t, :].unsqueeze(2).to_broadcast([128, 8, EXPERTS, EXPERTS])
                    equal = rank_a[:, half].rearrange("p (t a b) -> p t a b", t=8, a=EXPERTS)
                    greater = rank_b[:, half].rearrange("p (t a b) -> p t a b", t=8, a=EXPERTS)
                    V.tensor_tensor(equal, e4t, e4, ALU.is_equal)
                    link(V.tensor_tensor(greater, e4t, e4, ALU.is_gt))
                    link(V.tensor_tensor(equal, equal, before_sb[:].rearrange("p (a b) -> p a b", a=EXPERTS).unsqueeze(1)
                                         .to_broadcast([128, 8, EXPERTS, EXPERTS]), ALU.mult))
                    V.tensor_reduce(logit_m[:, 1, t], logit[:, t, :], AX.X, ALU.add)
                    link(V.tensor_tensor(equal, equal, greater, ALU.add))
                    V.reciprocal(logit_m[:, 2, t], logit_m[:, 1, t])
                    rank = rank_b[:, 64 * part:64 * part + 64]
                    link(V.tensor_reduce(rank.rearrange("p (t e) -> p t e", e=EXPERTS), equal, AX.X, ALU.add))
                    link(V.tensor_scalar(rank, rank, 2.0, None, ALU.is_lt))
                    link(V.tensor_tensor(rank, rank, logit[:, t, :].rearrange("p t e -> p (t e)"), ALU.mult))
                    V.tensor_tensor(rank_a[:, 64 * part:64 * part + 64].rearrange("p (t e) -> p t e", e=EXPERTS),
                                    rank.rearrange("p (t e) -> p t e", e=EXPERTS),
                                    logit_m[:, 2, t].unsqueeze(2).to_broadcast([128, 8, EXPERTS]), ALU.mult
                                    ).then_inc(S["ranked"], 1)

                operands(2)
                router_shift(0)
                operands(3)
                router_rank(0)
                router_shift(1)
                router_rank(1)
                dve.wait_ge(S["db_hi"], 1)
                V.tensor_tensor(db3[64:72, :], db_raw[:], db3[0:8, :].bitcast(fp32), ALU.subtract
                                ).then_inc(S["db_done"], 1)
                for q in range(QUARTERS):
                    ts = slice(512 * q, 512 * q + 512)
                    dve.wait_ge(S["w_hi"], q + 1)
                    V.tensor_tensor(w3[32:40, ts], bank[W_BANK[q]][0:8, :], w3[0:8, ts].bitcast(fp32), ALU.subtract
                                    ).then_inc(S["w_lo"], 1)

                def far_max(q):
                    dve.wait_ge(S["sfar_done"], q + 1)
                    mf = mfar[:, q % 2].rearrange("p g t h -> p (g t h)")
                    link(V.tensor_reduce(mf, sfar[:, q % 2, :, :].rearrange("p f n -> p n f"), AX.X, ALU.max))
                    V.tensor_scalar(mf, mf, -1.0, None, ALU.mult).then_inc(S["mfar_done"], 1)

                def near_sums(i):
                    c, h = i // 4, i % 4
                    q, tl = c // 2, 2 * (c % 2)
                    dve.wait_ge(S["near_exp"], i + 1)
                    V.tensor_reduce(lsum[:, q % 2, :, tl:tl + 2, h].rearrange("p g t -> p t g"),
                                    prob[:, i % 2].rearrange("p (t g) w -> p t g w", t=2), AX.X, ALU.add
                                    ).then_inc(S["sum_done"], 1)

                def transpose_weights(i):
                    if i == 0:
                        dve.wait_ge(S["split_done"], 6)
                    if i >= 2:
                        dve.wait_ge(S["o_pv"], i - 1)
                    V.transpose(prob_t[:, i % 2].rearrange("p s w -> p (s w)"),
                                prob[:, i % 2].rearrange("p s w -> p (s w)")).then_inc(S["probt_done"], 1)

                def glu(i):
                    dve.wait_ge(S["g_tanh"], i + 1)
                    V.scalar_tensor_tensor(out=th_act[:, i % 2, :], in0=th_act[:, i % 2, :], scalar=1.0,
                                           in1=g_act[:, i % 2, :], op0=ALU.add, op1=ALU.mult).then_inc(S["glu_done"], 1)

                def glu_times_up(i):
                    dve.wait_ge(S["glu_done"], i + 1)
                    V.tensor_tensor(u_act[:, i % 2, :], th_act[:, i % 2, :], u_act[:, i % 2, :], ALU.mult
                                    ).then_inc(S["gu_done"], 1)

                def times_weight(i):
                    dve.wait_ge(S["gu_done"], i + 1)
                    dve.wait_ge(S["wrep_ps"], i + 1)
                    V.tensor_tensor(u_act[:, i % 2, :], u_act[:, i % 2, :], bank[5][:], ALU.mult
                                    ).then_inc(S["act_done"], 1)

                def acc_out(q):
                    dve.wait_ge(S["down_ps"], EXPERTS * (q + 1))
                    t = slice(QT * q, QT * q + QT)
                    V.tensor_tensor(x_sb[:, t, :], x_sb[:, t, :], bank[6][:].rearrange("p (t c) -> p t c", c=D),
                                    ALU.add).then_inc(S["acc_done"], 1)

                def far_sum(q):
                    dve.wait_ge(S["far_exp"], q + 1)
                    if q >= 2:
                        dve.wait_ge(far_out[q - 2], 64)
                    dve.wait_ge(S["sum_done"], 8 * q + 8)
                    link(V.tensor_reduce(lfar[:, q % 2, :], sfar[:, q % 2, :, :].rearrange("p f n -> p n f"),
                                         AX.X, ALU.add))
                    link(V.tensor_tensor(lfar[:, q % 2, :], lfar[:, q % 2, :],
                                         lsum[:, q % 2].rearrange("p g t h -> p (g t h)"), ALU.add))
                    if q == 0:
                        dve.wait_ge(S["zeroed"], 1)
                    V.reciprocal(ofar[:, q % 2, :, 32:36], lfar[:, q % 2, :].rearrange("p (s h) -> p s h", h=HG)
                                 ).then_inc(S["inv_done"], 1)

                def mix_heads(q):
                    t = slice(QT * q, QT * q + QT)
                    dve.wait_ge(far_in[q], 16)
                    dve.wait_ge(S["o_tr"], q + 1)
                    if q >= 1:
                        dve.wait_ge(S["mix_tr"], q)
                    if q == 0:
                        dve.wait_ge(S["gate_done"], 1)
                    V.tensor_tensor(mix, bank[7][:].rearrange("p (t x j) -> p t x j", t=QT, j=4),
                                    ofar_tok[:, :, :, 0:32].rearrange("p j t x -> p t x j"), ALU.add
                                    ).then_inc(S["mix1"], 1)
                    dve.wait_ge(S["mix1"], q + 1)
                    for tt in range(QT):
                        last = V.tensor_tensor(
                            mix[:, tt].rearrange("p (h d) j -> p h d j", d=HD),
                            mix[:, tt].rearrange("p (h d) j -> p h d j", d=HD),
                            ofar_tok[:, :, tt, 32:36].rearrange("p j h -> p h j").unsqueeze(2).to_broadcast(
                                [128, HG, HD, 4]), ALU.mult)
                    last.then_inc(S["mix2"], 1)
                    dve.wait_ge(S["mix2"], q + 1)
                    V.tensor_tensor(mix.rearrange("p t x j -> p t (x j)"), mix.rearrange("p t x j -> p t (x j)"),
                                    gate[:, t, :], ALU.mult).then_inc(S["mix_done"], 1)

                def residual(q):
                    t = slice(QT * q, QT * q + QT)
                    dve.wait_ge(S["attn_ps"], q + 1)
                    V.tensor_tensor(xn0[:, t, :], xn0[:, t, :], bank[7][:].rearrange("p (t c) -> p t c", c=D),
                                    ALU.add).then_inc(S["x1_done"], 1)
                    dve.wait_ge(S["x1_done"], q + 1)
                    for tt in range(QT * q, QT * q + QT):
                        last = V.bn_stats(stats[:, tt, :], xn0[:, tt, :])
                    last.then_inc(S["stats_done"], 1)

                def clip_gate(i):
                    dve.wait_ge(S["g_raw"], i + 1)
                    V.tensor_scalar(g_act[:, i % 2, :], g_act[:, i % 2, :], LIMIT, 0.5, ALU.min, ALU.mult
                                    ).then_inc(S["g_half"], 1)

                def clip_up(i):
                    dve.wait_ge(S["u_raw"], i + 1)
                    V.tensor_scalar(u_act[:, i % 2, :], u_act[:, i % 2, :], 1.0 - LIMIT, 1.0 + LIMIT, ALU.max, ALU.min
                                    ).then_inc(S["u_clip"], 1)

                def ffn_statistics(part):
                    t0, t1 = FFN_PARTS[part]
                    dve.wait_ge(S["stats_done"], 2 + t1 // QT)
                    for t in range(t0, t1):
                        last = V.bn_aggr(mv[:, t, :], stats[:, t, :])
                    last.then_inc(S["stats2"], 1)

                def ffn_scale(part):
                    t = slice(*FFN_PARTS[part])
                    dve.wait_ge(S["sd_done"], 5 + part)
                    link(V.reciprocal(rs[:, 0, t], sd[:, 0, t]))

                def ffn_normalize(q):
                    for t in range(QT * q, QT * q + QT):
                        last = V.tensor_scalar(gate[:, t, :], xn0[:, t, :], mv[:, t, 0:1], rs[:, 0, t:t + 1],
                                               ALU.subtract, ALU.mult)
                    last.then_inc(S["normed"], 1)

                def ffn_affine(q):
                    dve.wait_ge(S["h2_tr"], q + 1)
                    if q >= 2:
                        dve.wait_ge(S["h2_lo"], q - 1)
                    V.tensor_scalar(xf[:, q % 2, :], bank[T_BANK[q]][:], col(C_G2), col(C_B2), ALU.mult, ALU.add
                                    ).then_inc(S["h2_aff"], 1)

                def ffn_low(q):
                    ts = slice(512 * q, 512 * q + 512)
                    dve.wait_ge(S["h2_hi"], q + 1)
                    V.tensor_tensor(xt_lo[:, ts], xf[:, q % 2, :], xt_hi[:, ts].bitcast(fp32), ALU.subtract
                                    ).then_inc(S["h2_lo"], 1)

                far_max(0)
                for i in range(STEPS):
                    c, h = i // 4, i % 4
                    q, tl = c // 2, 2 * (c % 2)
                    if i >= 1:
                        clip_gate(i - 1)
                    dve.wait_ge(S["score_ps"], i + 1)
                    V.tensor_reduce(mnear[:, i % 2, :], bank[i % 2][:].rearrange("p (s w) -> p s w", w=WINDOW),
                                    AX.X, ALU.max).then_inc(S["near_max"], 1)
                    if i >= 1:
                        clip_up(i - 1)
                    dve.wait_ge(S["near_max"], i + 1)
                    if i % 8 == 0:
                        dve.wait_ge(S["mfar_done"], q + 1)
                        if q >= 2:
                            dve.wait_ge(S["far_sh"], q - 1)
                    mv_ = mall[:, q % 2, :, tl:tl + 2, h].rearrange("p g t -> p t g")
                    V.scalar_tensor_tensor(out=mv_, in0=mnear[:, i % 2, :].rearrange("p (t g) -> p t g", t=2),
                                           scalar=-1.0, in1=mfar[:, q % 2, :, tl:tl + 2, h].rearrange("p g t -> p t g"),
                                           op0=ALU.mult, op1=ALU.min).then_inc(S["mall_done"], 1)
                    if i >= 1:
                        near_sums(i - 1)
                        glu(i - 1)
                        transpose_weights(i - 1)
                        glu_times_up(i - 1)
                        times_weight(i - 1)
                    if i % 8 == 1 and i > 8:
                        acc_out(q - 1)
                    if i % 8 == 2 and i > 8:
                        far_sum(q - 1)
                    if i % 8 == 7 and q + 1 < QUARTERS:
                        far_max(q + 1)
                    if i % 8 == 6 and q >= 1:
                        mix_heads(q - 1)
                    if i % 8 == 1 and q >= 2:
                        residual(q - 2)
                    if i == FFN_STEP - 1:
                        ffn_statistics(0)
                    if i == FFN_STEP + 1:
                        ffn_scale(0)
                        ffn_normalize(0)
                        ffn_normalize(1)
                    if i == FFN_STEP + 2:
                        ffn_affine(0)
                    if i == FFN_STEP + 4:
                        ffn_low(0)
                clip_gate(STEPS - 1)
                clip_up(STEPS - 1)
                near_sums(STEPS - 1)
                glu(STEPS - 1)
                transpose_weights(STEPS - 1)
                glu_times_up(STEPS - 1)
                times_weight(STEPS - 1)
                residual(2)

                def ffn_out(q):
                    t = slice(QT * q, QT * q + QT)
                    dve.wait_ge(S["fc2_ps"], q + 1)
                    dve.wait_ge(S["base_done"], q + 1)
                    V.tensor_tensor(x_sb[:, t, :], x_sb[:, t, :], bank[6][:].rearrange("p (t c) -> p t c", c=D),
                                    ALU.add).then_inc(S["y_done"], 1)

                ffn_statistics(1)
                far_sum(3)
                ffn_affine(1)
                ffn_scale(1)
                ffn_normalize(2)
                ffn_low(1)
                acc_out(3)
                ffn_affine(2)
                ffn_low(2)
                ffn_out(0)
                mix_heads(3)
                residual(3)
                ffn_statistics(2)
                ffn_out(1)
                ffn_scale(2)
                ffn_normalize(3)
                ffn_out(2)
                ffn_affine(3)
                ffn_low(3)
                ffn_out(3)

            @block.tensor
            def _(pe):
                E = nc.tensor

                def three(out_ap, w_hi, w_lo, m_hi, m_lo, start=True):
                    E.matmul(out_ap, w_hi, m_hi, start=start, stop=False)
                    E.matmul(out_ap, w_lo, m_hi, start=False, stop=False)
                    return E.matmul(out_ap, w_hi, m_lo, start=False, stop=True)

                def transposes(q):
                    pe.wait_ge(S["normed"], q + 1)
                    if q >= 1:
                        pe.wait_ge(S["x_lo"], q)
                        pe.wait_ge(S["xf_done"], q)
                    for tt in range(QT):
                        last = E.transpose(bank[0][:, 128 * tt:128 * tt + 128], xn0[:, QT * q + tt, :], ident_sb[:])
                    last.then_inc(S["x_tr"], 1)
                    for tt in range(QT):
                        last = E.transpose(bank[1][:, 128 * tt:128 * tt + 128], gate[:, QT * q + tt, :], ident_sb[:])
                    last.then_inc(S["h_tr"], 1)

                def add_rows(out_ap, r0, n, times=1):
                    rows = bias_row[0:40, r0:r0 + n]
                    if times > 1:
                        rows = rows.unsqueeze(1).to_broadcast([40, times, n])
                    return E.matmul(out_ap, ones[0:40, :], rows, start=True, stop=False, skip_group_check=True)

                def on(out_ap, w_hi, w_lo, m_hi, m_lo):
                    E.matmul(out_ap, w_hi, m_hi, start=False, stop=False, skip_group_check=True)
                    E.matmul(out_ap, w_lo, m_hi, start=False, stop=False, skip_group_check=True)
                    return E.matmul(out_ap, w_hi, m_lo, start=False, stop=True, skip_group_check=True)

                def project_channels(q):
                    b = q % 2
                    pe.wait_ge(S["x_lo"], q + 1)
                    if q == 0:
                        pe.wait_ge(S["split_done"], 1)
                        pe.wait_ge(S["bias_done"], 1)
                    logits = bank[6 + q // 2]
                    if q % 2 == 0:
                        add_rows(logits[:, 0:64].rearrange("p (t e) -> p t e", e=EXPERTS), R_ROUTER, EXPERTS, 8)
                    for tt in range(QT):
                        t = QT * q + tt
                        ts = slice(128 * t, 128 * t + 128)
                        e0 = EXPERTS * (t % 8)
                        last = on(logits[:, e0:e0 + EXPERTS], xt_hi[:, ts], xt_lo[:, ts],
                                  wqk_hi[:, 256:264], wqk_lo[:, 256:264])
                    if q % 2 == 1:
                        last.then_inc(S["logits_ps"], 1)
                    pe.wait_ge(S["h_lo"], q + 1)
                    for k in range(2):
                        if q >= 1:
                            pe.wait_ge(S["kt_done"] if k else S["qt_done"], q)
                        three(bank[2 + k][:], wqk_hi[:, 128 * k:128 * k + 128], wqk_lo[:, 128 * k:128 * k + 128],
                              xn_hi[:, b, :], xn_lo[:, b, :]).then_inc(S["qk_ps"], 1)

                def project_tokens(q):
                    b = q % 2
                    for tt in range(QT):
                        t = QT * q + tt
                        ts = slice(128 * tt, 128 * tt + 128)
                        if t == 0:
                            pe.wait_ge(S["split_done"], 2)
                        if t >= 2:
                            pe.wait_ge(S["gate_pre"], t - 1)
                        add_rows(bank[4 + t % 2][:], R_TOK, 512)
                        on(bank[4 + t % 2][:], xn_hi[:, b, ts], xn_lo[:, b, ts], wtok_hi[:], wtok_lo[:]
                           ).then_inc(S["tok_ps"], 1)

                pe.wait_ge(first_in, 48)
                transposes(0)
                for q in range(QUARTERS):
                    project_channels(q)
                    if q + 1 < QUARTERS:
                        transposes(q + 1)
                    project_tokens(q)

                def scores(i):
                    c, h = i // 4, i % 4
                    b = bank[i % 2]
                    if h == 0:
                        pe.wait_ge(S["qm_done"], 4 * c + 4)
                        pe.wait_ge(S["kt_done"], c // 2 + 1)
                    if i == 0:
                        pe.wait_ge(S["consts_done"], 1)
                        pe.wait_ge(S["x_lo"], QUARTERS)
                        pe.wait_ge(S["xf_done"], QUARTERS)
                        pe.wait_ge(S["zeroed"], 1)
                    if i >= 2:
                        pe.wait_ge(S["near_exp"], i - 1)
                    n0 = 0
                    if c == 0:
                        E.matmul(b[:, 0:WINDOW], anti_sb[:], band0_hi[:, h, :], start=True, stop=False,
                                 skip_group_check=True)
                        E.matmul(b[:, 32:WINDOW], anti_sb[:], band_lo[:, h, 32:], start=False, stop=False,
                                 skip_group_check=True)
                        n0 = 1
                    n = 8 - n0
                    for k, part in enumerate((band_hi, band_lo)):
                        E.matmul(b[:, WINDOW * n0:512].rearrange("p (s w) -> p s w", w=WINDOW), anti_sb[:],
                                 part[:, h, :].unsqueeze(1).to_broadcast([128, n, WINDOW]),
                                 start=(k == 0 and n0 == 0), stop=False, skip_group_check=True)
                    for s in range(8):
                        for j in range(4):
                            last = E.matmul(b[32 * j:32 * j + 32, WINDOW * s:WINDOW * s + WINDOW],
                                            qm[32 * h:32 * h + 32, c % 2, s, j, :],
                                            kt[32 * h:32 * h + 32, 256 * c + 32 * s:256 * c + 32 * s + WINDOW],
                                            start=False, stop=True, skip_group_check=True,
                                            tile_position=(32 * h, 32 * j))
                    last.then_inc(S["score_ps"], 1)

                def weighted_v(i):
                    c, h = i // 4, i % 4
                    if h == 0:
                        pe.wait_ge(S["vbd_done"], 4 * (c // 2) + 4)
                        if c >= 1:
                            pe.wait_ge(S["o_done"], c)
                    pe.wait_ge(S["probt_done"], i + 1)
                    if i == 0:
                        pe.wait_ge(S["qt_done"], QUARTERS)
                    for s in range(8):
                        st = 8 * c + s
                        for half in range(2):
                            kst = st - 1 + half
                            if kst < 0:
                                continue
                            slot, tile, g = (kst // 16) % 2, (kst // 4) % QT, kst % 4
                            last = E.matmul(bank[2][32 * h:32 * h + 32, 32 * s:32 * s + 32],
                                            vbd[:, slot, QT * g + tile, 8 * h:8 * h + 8, :].rearrange("p x j -> p (x j)"),
                                            prob_t[:, i % 2, s, 32 * half:32 * half + 32],
                                            start=(half == 0 or st == 0), stop=(half == 1), skip_group_check=True,
                                            tile_position=(0, 32 * h))
                    last.then_inc(S["o_pv"], 1)

                def experts_in(i):
                    q, e = i // EXPERTS, i % EXPERTS
                    ts = slice(512 * q, 512 * q + 512)
                    if i == 0:
                        pe.wait_ge(S["kt_done"], QUARTERS)
                        pe.wait_ge(S["gate_pre"], TILES)
                    if q == 0 and e % 2 == 0:
                        pe.wait_ge(S["split_done"], N_GU + e // 2)
                    for half, done, b, free in ((0, "gate_ps", 3, "g_raw"), (1, "up_ps", 4, "u_raw")):
                        if i >= 1:
                            pe.wait_ge(S[free], i)
                        ws = slice(INNER * half, INNER * half + INNER)
                        three(bank[b][:], gu_hi[:, e, ws], gu_lo[:, e, ws], xt_hi[:, ts], xt_lo[:, ts]
                              ).then_inc(S[done], 1)

                def weight_rows(i):
                    q, e = i // EXPERTS, i % EXPERTS
                    if i == 0:
                        pe.wait_ge(S["w_lo"], QUARTERS)
                    else:
                        pe.wait_ge(S["act_done"], i)
                    E.matmul(bank[5][:], onehot_sb[:, e, :], w3[0:40, 512 * q:512 * q + 512], start=True, stop=True
                             ).then_inc(S["wrep_ps"], 1)

                def experts_out(i):
                    q, e = i // EXPERTS, i % EXPERTS
                    if e == 0:
                        if q == 0:
                            pe.wait_ge(S["db_done"], 1)
                            pe.wait_ge(mat_in, N_MAT)
                            pe.wait_ge(S["logit_sh"], 2)
                            pe.wait_ge(S["w_hi2"], QUARTERS)
                        else:
                            pe.wait_ge(S["acc_done"], q)
                        for tt in range(QT):
                            t = QT * q + tt
                            E.matmul(bank[6][:, 128 * tt:128 * tt + 128], w3[:, 128 * t:128 * t + 128], db3[:],
                                     start=(tt == 0), stop=False, skip_group_check=True)
                    pe.wait_ge(S["act_done"], i + 1)
                    for tt in range(QT):
                        last = E.matmul(bank[6][:, 128 * tt:128 * tt + 128], u_act[:, i % 2, 128 * tt:128 * tt + 128],
                                        down_sb[:, e, :], start=False, stop=(e == EXPERTS - 1), skip_group_check=True)
                    last.then_inc(S["down_ps"], 1)

                def weights_to_rows():
                    pe.wait_ge(S["ranked"], 2)
                    pe.wait_ge(S["qt_done"], QUARTERS)
                    for q in range(QUARTERS):
                        for tt in range(QT):
                            t = QT * q + tt
                            last = E.transpose(bank[W_BANK[q]][0:8, 128 * tt:128 * tt + 128],
                                               rank_a[:, EXPERTS * t:EXPERTS * t + EXPERTS], ident_sb[:])
                        last.then_inc(S["w_tr"], 1)

                def heads_to_tokens(q):
                    pe.wait_ge(S["o_done"], 2 * q + 2)
                    if q >= 1:
                        pe.wait_ge(S["x1_done"], q)
                    if q == 2:
                        pe.wait_ge(S["h2_aff"], 1)
                    for tt in range(QT):
                        last = E.transpose(bank[7][:, 128 * tt:128 * tt + 128],
                                           onear[:, q % 2, 128 * tt:128 * tt + 128], ident_sb[:])
                    last.then_inc(S["o_tr"], 1)

                def mix_to_channels(q):
                    pe.wait_ge(S["mix_done"], q + 1)
                    for tt in range(QT):
                        last = E.transpose(bank[7][:, 128 * tt:128 * tt + 128],
                                           mix[:, tt].rearrange("p x j -> p (x j)"), ident_sb[:])
                    last.then_inc(S["mix_tr"], 1)

                def attention_out(q):
                    pe.wait_ge(S["mixt_done"], q + 1)
                    add_rows(bank[7][:].rearrange("p (t c) -> p t c", c=D), R_OUT, D, QT)
                    for tt in range(QT):
                        last = E.matmul(bank[7][:, 128 * tt:128 * tt + 128], mix_t[:, 128 * tt:128 * tt + 128],
                                        outw_sb[:], start=False, stop=True, skip_group_check=True)
                    last.then_inc(S["attn_ps"], 1)

                def ffn_transposes(q):
                    pe.wait_ge(S["normed"], QUARTERS + q + 1)
                    if q == 0:
                        pe.wait_ge(S["x1_done"], 2)
                    if q == 1:
                        pe.wait_ge(S["near_exp"], STEPS)
                    if q == 3:
                        pe.wait_ge(S["h2_aff"], 2)
                    for tt in range(QT):
                        last = E.transpose(bank[T_BANK[q]][:, 128 * tt:128 * tt + 128], gate[:, QT * q + tt, :],
                                           ident_sb[:])
                    last.then_inc(S["h2_tr"], 1)

                experts_in(0)
                weights_to_rows()
                scores(0)
                for i in range(STEPS + 2):
                    if 1 <= i < STEPS:
                        experts_in(i)
                    if i >= 2:
                        experts_out(i - 2)
                    if 1 <= i <= STEPS:
                        weight_rows(i - 1)
                    if i + 1 < STEPS:
                        scores(i + 1)
                    if i >= 2:
                        weighted_v(i - 2)
                    if i == FFN_STEP + 1:
                        ffn_transposes(0)
                    if i % 8 == 5 and i > 8:
                        heads_to_tokens(i // 8 - 1)
                    if i % 8 == 7 and i > 8:
                        mix_to_channels(i // 8 - 1)
                    if i % 8 == 0 and i > 8:
                        attention_out(i // 8 - 2)

                def ffn_up(q):
                    ts = slice(512 * q, 512 * q + 512)
                    pe.wait_ge(S["h2_lo"], q + 1)
                    if q == 0:
                        pe.wait_ge(S["o_done"], 8)
                        pe.wait_ge(S["act_done"], STEPS)
                    for f in range(FC):
                        if q >= 1:
                            pe.wait_ge(S["hid_done"], FC * (q - 1) + f + 1)
                        ws = slice(128 * f, 128 * f + 128)
                        three(bank[2 + f][:], fc1_hi[:, ws], fc1_lo[:, ws], xt_hi[:, ts], xt_lo[:, ts]
                              ).then_inc(S["fc1_ps"], 1)

                def ffn_down(q):
                    pe.wait_ge(S["hid_done"], FC * q + FC)
                    if q == 0:
                        pe.wait_ge(S["acc_done"], QUARTERS)
                    if q >= 1:
                        pe.wait_ge(S["y_done"], q)
                    add_rows(bank[6][:].rearrange("p (t c) -> p t c", c=D), R_FC2, D, QT)
                    for tt in range(QT):
                        for f in range(FC):
                            last = E.matmul(bank[6][:, 128 * tt:128 * tt + 128],
                                            hid[:, q % 2, f, 128 * tt:128 * tt + 128], fc2_sb[:, f, :],
                                            start=False, stop=(f == FC - 1), skip_group_check=True)
                    last.then_inc(S["fc2_ps"], 1)

                pe.wait_ge(S["split_done"], len(SPLITS))
                ffn_transposes(1)
                heads_to_tokens(3)
                ffn_up(0)
                ffn_transposes(2)
                ffn_up(1)
                ffn_down(0)
                ffn_up(2)
                mix_to_channels(3)
                attention_out(3)
                ffn_down(1)
                ffn_down(2)
                ffn_transposes(3)
                ffn_up(3)
                ffn_down(3)


def kernel(**inputs):
    import numpy as np
    import concourse.bacc as bacc
    from concourse.bass_utils import run_bass_kernel_spmd

    a = {k: np.asarray(v) for k, v in inputs.items()}
    qkv_w, qkv_b = a["L0_attn_qkv_w"], a["L0_attn_qkv_b"]
    pos = a["L0_attn_pos_bias"]
    f32 = np.float32

    def by_group(w):
        return w.reshape(w.shape[:-1] + (4, 4, 8)).swapaxes(-1, -2).reshape(w.shape)

    w_tok = np.concatenate([qkv_w.reshape(128, 3, 4, 4, 8).transpose(0, 1, 3, 2, 4).reshape(128, 384),
                            by_group(a["L0_attn_gate_w"])], axis=1)
    row = np.concatenate([qkv_b.reshape(3, 4, 4, 8).transpose(0, 2, 1, 3).reshape(384), by_group(a["L0_attn_gate_b"]),
                          a["L0_ffn_router_bias"], a["L0_attn_out_b"], a["L0_attn_fc2_b"]])[None, :]
    gub = a["L0_ffn_gate_up_bias"].reshape(8, 2, 128).transpose(2, 0, 1).reshape(128, 16)
    cols = np.stack([a["L0_attn_ln1_g"], a["L0_attn_ln1_b"], a["L0_attn_ln2_g"], a["L0_attn_ln2_b"],
                     qkv_b[0:128], qkv_b[128:256]], axis=1)
    cols = np.concatenate([cols, gub, a["L0_attn_fc1_b"].reshape(4, 128).T], axis=1)
    band = np.full((HEADS, 96), CLOSED, f32)
    band[:, 31:64] = pos[32::-1, :].T
    far = np.broadcast_to(pos[33:38].reshape(NFAR, 4, 4).transpose(2, 0, 1).reshape(4, 1, NFAR * 4),
                          (4, 32, NFAR * 4)).reshape(128, NFAR * 4)
    p = np.arange(128)
    anti = (p[:, None] // 32 * 32 + 31 - p[:, None] % 32 == p[None, :]).astype(f32)
    headmask = (p[:, None] % 32 // 8 == np.arange(4)[None, :]).astype(f32)
    before = (np.arange(8)[None, :] < np.arange(8)[:, None]).astype(f32).reshape(1, 64)
    onehot = (np.arange(40)[:, None] % 32 == np.arange(8)[None, :]).astype(f32)
    arrays = {
        "x": a["L0_attn_x"].reshape(TOKENS, D), "ident": np.eye(128, dtype=f32), "anti": anti, "headmask": headmask,
        "before": before, "onehot": onehot, "cols": cols, "row": row, "far_bias": far, "band": band, "w_tok": w_tok,
        "w_qk_router": np.concatenate([qkv_w[:, 0:256], a["L0_ffn_router_weight"].T], axis=1),
        "gate_up": a["L0_ffn_gate_up_proj"].transpose(1, 0, 2).reshape(128, 2048), "down": a["L0_ffn_down_proj"],
        "down_bias": a["L0_ffn_down_bias"], "fc1": a["L0_attn_fc1_w"], "fc2": a["L0_attn_fc2_w"],
        "out_w": by_group(a["L0_attn_out_w"].T).T,
    }
    arrays = {"in_" + k: np.ascontiguousarray(v) for k, v in arrays.items()}

    nc = bacc.Bacc("TRN2", target_bir_lowering=False, num_devices=1)
    aps = [nc.dram_tensor(k, v.shape, mybir.dt.from_np(v.dtype), kind="ExternalInput").ap() for k, v in arrays.items()]
    y = nc.dram_tensor("y", (TOKENS, D), mybir.dt.float32, kind="ExternalOutput").ap()
    build(nc, *aps, y)
    r = run_bass_kernel_spmd(nc, [arrays], core_ids=[0])
    return r.results[0]["y"].reshape(1, TOKENS, D)
```
